# Optimizing a Trainium2 kernel written in Bass

```python
import numpy as np
import jax
import jax.numpy as jnp

def _softmax(x, axis=-1):
    return jax.nn.softmax(x, axis=axis)

def _gelu(x):
    return jax.nn.gelu(x, approximate=True)

def _silu(x):
    return jax.nn.silu(x)

def _sigmoid(x):
    return jax.nn.sigmoid(x)

def _layernorm(x, axis=-1, eps=1e-05):
    m = jnp.mean(x, axis=axis, keepdims=True)
    v = jnp.var(x, axis=axis, keepdims=True)
    return (x - m) / jnp.sqrt(v + eps)

def _scatter_add(tgt, idx, src, axis=0):
    return tgt.at[idx].add(src)

def _segment_sum(src, seg, n):
    return jax.ops.segment_sum(src, seg, n)
kernel_name = 'mk_gnn_resnorm_d4_gnn_r64_3a9c32'

def setup_inputs(seed: int=0):
    np.random.seed(seed)
    _w = jnp.asarray

    def _rec_inputs():
        import jax
        import jax.numpy as jnp
        _gk = jax.random.key(seed)
        x = -0.0005121 + 1.001 * jax.random.normal(jax.random.fold_in(_gk, 1), (100000, 32), jnp.float32)
        src = jax.random.randint(jax.random.fold_in(_gk, 2), (25000,), 0, 100000, jnp.int32)
        dst = jnp.minimum((100000 * jax.random.uniform(jax.random.fold_in(_gk, 3), (25000,)) ** 2.0).astype(jnp.int32), 99999)
        _o = jnp.argsort(dst, stable=True)
        src = src[_o]
        dst = dst[_o]
        edge_type_86 = jax.random.randint(jax.random.fold_in(_gk, 13), (25000,), 0, 86, jnp.int32)
        edge_weight = -0.000414295 + 0.999828 * jax.random.normal(jax.random.fold_in(_gk, 14), (25000,), jnp.float32)
        return (x, src, dst, edge_type_86, edge_weight)
    x, src, dst, edge_type_86, edge_weight = _rec_inputs()

    def _L0_gnn_setup():
        import jax, jax.numpy as jnp
        import numpy as np
        N_NODES = 100000
        N_EDGES = 25000
        D_FEAT = 32
        K = 10
        ALPHA = 0.1
        key = jax.random.key(seed)
        k1, k2, k3 = jax.random.split(key, 3)
        feat = jax.random.normal(k1, (N_NODES, D_FEAT), dtype=jnp.float32)
        src = jax.random.randint(k2, (N_EDGES,), 0, N_NODES, dtype=jnp.int64)
        dst = jax.random.randint(k3, (N_EDGES,), 0, N_NODES, dtype=jnp.int64)
        return {'feat': feat, 'src': src, 'dst': dst}
    _L0_gnn_all = _L0_gnn_setup()
    _L0_gnn_in = {k: v for k, v in _L0_gnn_all.items() if k in ()}
    del _L0_gnn_all

    def _L1_gnn_setup():
        import jax, jax.numpy as jnp
        import numpy as np
        N_NODES = 50000
        DEG = 16
        N_HEAD = 4
        F_IN = 32
        F_OUT = 32
        key = jax.random.key(seed)
        k_h, k_w, k_fw, k_fb = jax.random.split(key, 4)
        h = jax.random.normal(k_h, (N_NODES, F_IN), dtype=jnp.float32)
        src = jnp.repeat(jnp.arange(N_NODES, dtype=jnp.int64), DEG)
        offs = (jnp.arange(DEG, dtype=jnp.int64) + 1) * 97
        dst = (src.reshape(N_NODES, DEG) + offs[None, :]).reshape(-1) % N_NODES
        edge_index = jnp.stack([src, dst], axis=0)
        gain = 1.414
        bound_w = gain * np.sqrt(6.0 / (F_IN + F_OUT))
        w = jax.random.uniform(k_w, (N_HEAD, F_IN, F_OUT), jnp.float32, -bound_w, bound_w)
        bound_fc = np.sqrt(1.0 / (2 * F_OUT))
        fc_w = jax.random.uniform(k_fw, (1, 2 * F_OUT), jnp.float32, -bound_fc, bound_fc)
        fc_b = jax.random.uniform(k_fb, (1,), jnp.float32, -bound_fc, bound_fc)
        bias = jnp.zeros((F_OUT,), jnp.float32)
        return {'h': h, 'edge_index': edge_index, 'w': w, 'fc_w': fc_w, 'fc_b': fc_b, 'bias': bias}
    _L1_gnn_all = _L1_gnn_setup()
    _L1_gnn_in = {k: v for k, v in _L1_gnn_all.items() if k in ('w', 'fc_w', 'fc_b', 'bias')}
    del _L1_gnn_all

    def _L2_gnn_setup():
        import jax, jax.numpy as jnp
        import numpy as np
        N_NODES = 50000
        N_EDGES = 12500
        INP_DIM = 32
        OUT_DIM = 32
        ATTN_DIM = 32
        NUM_RELS = 86
        NUM_BASES = 16
        GAMMA = 0.0
        key = jax.random.key(seed)
        ks = jax.random.split(key, 12)
        return {'h': jax.random.normal(ks[0], (N_NODES, INP_DIM), jnp.float32), 'weight': jax.random.normal(ks[1], (NUM_BASES, INP_DIM, OUT_DIM), jnp.float32), 'w_comp': jax.random.normal(ks[2], (NUM_RELS, NUM_BASES), jnp.float32), 'self_loop_weight': jax.random.normal(ks[3], (INP_DIM, OUT_DIM), jnp.float32), 'A1_w': jax.random.normal(ks[4], (ATTN_DIM, INP_DIM), jnp.float32), 'A1_b': jax.random.normal(ks[5], (ATTN_DIM,), jnp.float32), 'A2_w': jax.random.normal(ks[6], (ATTN_DIM, INP_DIM), jnp.float32), 'A2_b': jax.random.normal(ks[7], (ATTN_DIM,), jnp.float32), 'rel_emb': jax.random.normal(ks[8], (NUM_RELS, ATTN_DIM), jnp.float32), 'src': jax.random.randint(ks[9], (N_EDGES,), 0, N_NODES, jnp.int32), 'dst': jax.random.randint(ks[10], (N_EDGES,), 0, N_NODES, jnp.int32), 'etype': jax.random.randint(ks[11], (N_EDGES,), 0, NUM_RELS, jnp.int32)}
    _L2_gnn_all = _L2_gnn_setup()
    _L2_gnn_in = {k: v for k, v in _L2_gnn_all.items() if k in ('weight', 'w_comp', 'self_loop_weight', 'A1_w', 'A1_b', 'A2_w', 'A2_b', 'rel_emb')}
    del _L2_gnn_all

    def _L3_gnn_setup():
        import jax, jax.numpy as jnp
        import numpy as np
        key = jax.random.key(seed)
        k1, k2, k3 = jax.random.split(key, 3)
        N, E, D = (100000, 25000, 32)
        node_feat = jax.random.normal(k1, (N, D), dtype=jnp.float32)
        edge_attr = jax.random.normal(k2, (E,), dtype=jnp.float32)
        edge_index = jax.random.randint(k3, (2, E), 0, N, dtype=jnp.int64)
        return {'node_feat': node_feat, 'edge_attr': edge_attr, 'edge_index': edge_index, 'num_nodes': N}
    _L3_gnn_all = _L3_gnn_setup()
    _L3_gnn_in = {k: v for k, v in _L3_gnn_all.items() if k in ()}
    del _L3_gnn_all
    return {'x': x, 'src': src, 'dst': dst, 'edge_type_86': edge_type_86, 'edge_weight': edge_weight, 'L1_gnn_w': _L1_gnn_in['w'], 'L1_gnn_fc_w': _L1_gnn_in['fc_w'], 'L1_gnn_fc_b': _L1_gnn_in['fc_b'], 'L1_gnn_bias': _L1_gnn_in['bias'], 'L2_gnn_weight': _L2_gnn_in['weight'], 'L2_gnn_w_comp': _L2_gnn_in['w_comp'], 'L2_gnn_self_loop_weight': _L2_gnn_in['self_loop_weight'], 'L2_gnn_A1_w': _L2_gnn_in['A1_w'], 'L2_gnn_A1_b': _L2_gnn_in['A1_b'], 'L2_gnn_A2_w': _L2_gnn_in['A2_w'], 'L2_gnn_A2_b': _L2_gnn_in['A2_b'], 'L2_gnn_rel_emb': _L2_gnn_in['rel_emb']}

def reference(x, src, dst, edge_type_86, edge_weight, L1_gnn_w, L1_gnn_fc_w, L1_gnn_fc_b, L1_gnn_bias, L2_gnn_weight, L2_gnn_w_comp, L2_gnn_self_loop_weight, L2_gnn_A1_w, L2_gnn_A1_b, L2_gnn_A2_w, L2_gnn_A2_b, L2_gnn_rel_emb):
    import jax
    import jax.numpy as jnp

    def _L0_gnn_ref(feat, src, dst):
        import jax, jax.numpy as jnp
        import numpy as np
        N_NODES = 100000
        N_EDGES = 25000
        D_FEAT = 32
        K = 10
        ALPHA = 0.1
        n = feat.shape[0]
        ones = jnp.ones(src.shape[0], dtype=feat.dtype)
        out_deg = jax.ops.segment_sum(ones, src, num_segments=n)
        in_deg = jax.ops.segment_sum(ones, dst, num_segments=n)
        src_norm = jnp.clip(out_deg, 1.0, None) ** (-0.5)
        dst_norm = jnp.clip(in_deg, 1.0, None) ** (-0.5)
        feat0 = feat

        def step(f, _):
            f = f * src_norm[:, None]
            agg = jax.ops.segment_sum(f[src], dst, num_segments=n)
            f = agg * dst_norm[:, None]
            f = (1.0 - ALPHA) * f + ALPHA * feat0
            return (f, None)
        feat, _ = jax.lax.scan(step, feat, None, length=K)
        return feat

    def _L1_gnn_ref(h, edge_index, w, fc_w, fc_b, bias):
        import jax, jax.numpy as jnp
        import numpy as np
        N_NODES = 50000
        DEG = 16
        N_HEAD = 4
        F_IN = 32
        F_OUT = 32
        n_head, f_in, f_out = w.shape
        n = h.shape[0]
        src, dst = (edge_index[0], edge_index[1])
        hp = jnp.einsum('nf,hfo->hno', h, w)
        w_src = fc_w[0, :f_out]
        w_dst = fc_w[0, f_out:]
        a_src = jnp.einsum('hnf,f->hn', hp, w_src)
        a_dst = jnp.einsum('hnf,f->hn', hp, w_dst)
        e = a_src[:, src] + a_dst[:, dst] + fc_b[0]
        e = jax.nn.leaky_relu(e, negative_slope=0.2)
        seg_max = jax.ops.segment_max(e.T, src, num_segments=n)
        e = jnp.exp(e - seg_max.T[:, src])
        seg_sum = jax.ops.segment_sum(e.T, src, num_segments=n)
        att = e / seg_sum.T[:, src]
        msg = att[:, :, None] * hp[:, dst, :]
        agg = jax.vmap(lambda m: jax.ops.segment_sum(m, src, num_segments=n))(msg)
        out = agg.mean(axis=0) + bias
        return out

    def _L2_gnn_ref(h, weight, w_comp, self_loop_weight, A1_w, A1_b, A2_w, A2_b, rel_emb, src, dst, etype):
        import jax, jax.numpy as jnp
        import numpy as np
        N_NODES = 50000
        N_EDGES = 12500
        INP_DIM = 32
        OUT_DIM = 32
        ATTN_DIM = 32
        NUM_RELS = 86
        NUM_BASES = 16
        GAMMA = 0.0
        E = src.shape[0]
        N = h.shape[0]
        x = h[src]
        y = h[dst]
        c = w_comp[etype]
        xb = jnp.einsum('ei,bio->ebo', x, weight)
        msg = jnp.einsum('eb,ebo->eo', c, xb)
        x_hat = x @ A1_w.T + A1_b
        y_hat = y @ A2_w.T + A2_b + rel_emb[etype]
        scale = jnp.sqrt(jnp.asarray(INP_DIM, h.dtype))
        a = jnp.tanh(jax.nn.relu(jnp.sum(x_hat * y_hat, axis=-1) / scale))
        a = jnp.where(a > GAMMA, a, jnp.zeros_like(a))
        nei = jax.ops.segment_sum(a[:, None] * msg, dst, num_segments=N)
        last_e = jax.ops.segment_max(jnp.arange(E, dtype=jnp.int32), dst, num_segments=N)
        last_e = jnp.clip(last_e, 0, E - 1)
        curr = h[src[last_e]] @ self_loop_weight
        in_deg = jax.ops.segment_sum(jnp.ones((E,), h.dtype), dst, num_segments=N)
        h_new = jnp.where((in_deg > 0)[:, None], nei + curr, jnp.zeros_like(nei))
        return jax.nn.relu(h_new)

    def _L3_gnn_ref(node_feat, edge_attr, edge_index, num_nodes):
        import jax, jax.numpy as jnp
        import numpy as np
        src, dst = (edge_index[0], edge_index[1])
        messages = node_feat[src] * edge_attr[:, None]
        aggr = jax.ops.segment_sum(messages, dst, num_segments=num_nodes)
        return aggr + node_feat
    edge_index = jnp.stack([src, dst])
    x = _layernorm(x + _L0_gnn_ref(x, src, dst), axis=-1)
    x = _layernorm(x + _L1_gnn_ref(x, edge_index, L1_gnn_w, L1_gnn_fc_w, L1_gnn_fc_b, L1_gnn_bias), axis=-1)
    x = _layernorm(x + _L2_gnn_ref(x, L2_gnn_weight, L2_gnn_w_comp, L2_gnn_self_loop_weight, L2_gnn_A1_w, L2_gnn_A1_b, L2_gnn_A2_w, L2_gnn_A2_b, L2_gnn_rel_emb, src, dst, edge_type_86), axis=-1)
    x = _layernorm(x + _L3_gnn_ref(x, edge_weight, edge_index, 100000), axis=-1)
    return x

_drawn_inputs = setup_inputs


def setup_inputs(seed=0):
    import zlib

    import numpy as np

    out = dict(_drawn_inputs(seed))
    spreads = {'L1_gnn_bias': (0.0, 0.1)}
    factors = {}
    for name, (base, spread) in spreads.items():
        noise = np.random.default_rng([zlib.crc32(name.encode()), seed]).standard_normal(out[name].shape)
        drawn = base * np.exp(spread * noise) if base else spread * noise
        out[name] = jnp.asarray(drawn.astype(out[name].dtype))
    for name, factor in factors.items():
        out[name] = (out[name] * factor).astype(out[name].dtype)
    return out
```

```python
from contextlib import ExitStack, contextmanager

import concourse.bass as bass
from concourse import mybir

ALU = mybir.AluOpType
ACT = mybir.ActivationFunctionType
AX = mybir.AxisListType
F32 = mybir.dt.float32
F16 = mybir.dt.float16
I32 = mybir.dt.int32

P = 128
BIG = 1.0e30
EPS = 1e-5


class Steps:

    def __init__(self, eng, sem):
        self.eng, self.sem, self.n, self.off = eng, sem, 0, None

    def do(self, ins):
        ins.then_inc(self.sem, 1)
        self.n += 1

    def wait(self):
        self.eng.wait_ge(self.sem, self.n if self.off is None else self.off + self.n)

    def seq(self, ins):
        self.do(ins)
        self.wait()

    @contextmanager
    def loop(self, count, per):
        start, outer = self.n, self.off
        with self.eng.Fori(0, count) as i:
            self.off = i * per if outer is None else outer + i * per
            yield i
            assert self.n - start == per, f"a round has {self.n - start} steps"
            self.off = outer
        self.n = start + per * count


def gnn_resnorm(nc, x, src, dst, etype, eweight, w1, fc_w, fc_b, bias1, w2, w_comp, w_self, A1w, A1b, A2w, A2b,
                rel_emb, out):
    N, D = x.shape
    E = src.shape[0]
    T = -(-E // P)
    EP = P * T
    LASTV = E - (P - 1) * T
    NH = w1.shape[0]
    NB = w2.shape[0]
    NR = w_comp.shape[0]
    NB_COL = 256
    NA_CH = -(-(N + 1) // (NB_COL * P))
    NT_ROWS = NA_CH * P * NB_COL
    ZROW = EP
    U = 14
    ROUNDS = T // (2 * U)
    LAND = 16 * U
    RW = 48
    ROW1 = 40
    K_STEPS = 10
    ALPHA = 0.1
    OOB = 2 * N
    NODE_P = 125
    NROWS = N // NODE_P
    CH = 16
    CR = NROWS // CH
    GT = 4
    NG = T // GT
    assert T % (2 * U) == 0 and T % GT == 0 and D == 32 and NROWS % CH == 0 and NG % 2 == 1

    ctx = ExitStack()
    with ctx:
        sb = lambda name, shape, dt=F32: ctx.enter_context(nc.sbuf_tensor(name, shape, dt))
        sem = lambda name: ctx.enter_context(nc.semaphore(name))

        nt_d = nc.dram_tensor("node_table", (NT_ROWS, 4), F32).ap()
        agg_d = nc.dram_tensor("appnp_table", (EP + P, D), F32).ap()
        att_d = nc.dram_tensor("attention_table", (EP + P, D), F32).ap()
        rgcn_d = nc.dram_tensor("rgcn_table", (EP + P, D), F32).ap()
        rel_d = nc.dram_tensor("relation_table", (NR, RW), F32).ap()
        row_d = nc.dram_tensor("rows_by_src", (EP, ROW1), F32).ap()

        bank = [ctx.enter_context(nc.psum_tensor(f"bank{i}", [P, 512], F32)) for i in range(8)]

        XS = sb("XS", [P, T * D])
        XD = sb("XD", [P, T * D])
        Y = sb("Y", [P, T * D])
        S = sb("S", [P, T * D])
        RB = sb("RB", [P, T * RW])
        v3 = lambda t, w=D: t.rearrange("p (t d) -> p t d", d=w)
        XS3, XD3, Y3, S3 = v3(XS[:, :]), v3(XD[:, :]), v3(Y[:, :]), v3(S[:, :])
        REL3 = v3(RB[:, :], RW)
        ROWS = RB[:, 0:T * ROW1]
        ROWS3 = v3(ROWS, ROW1)
        ring = sb("ring", [P, 2, U * RW])
        ridx = sb("ridx", [P, 2, U], I32)

        e_i = lambda name: sb(name, [P, T], I32)
        e_f = lambda name: sb(name, [P, T], F32)
        srci, dsti, etyi = e_i("srci"), e_i("dsti"), e_i("etyi")
        ew = e_f("ew")
        srcf, dstf = e_f("srcf"), e_f("dstf")
        tmpi = e_i("tmpi")
        a_s, b_s, a_d, b_d = e_f("a_s"), e_f("b_s"), e_f("a_d"), e_f("b_d")
        xsi, xdi = e_i("xsi"), e_i("xdi")
        gin, gout_s, gout_d, posi = e_i("gin"), e_i("gout_s"), e_i("gout_d"), e_i("posi")
        osi, odi = xsi, xdi
        c1, c2, c3 = e_f("c1"), e_f("c2"), e_f("c3")
        posf = e_f("posf")
        q_f = e_f("q_f")
        dmask, dfirst, dend = e_f("dmask"), e_f("dfirst"), e_f("dend")
        smask, sfirst, send, ks = a_s, b_s, a_d, b_d
        t1, t2, t3 = e_f("t1"), e_f("t2"), e_f("t3")
        z4t, e4t = sb("z4", [P, T * NH]), sb("e4", [P, T * NH])
        z43, e43 = v3(z4t[:, :], NH), v3(e4t[:, :], NH)

        iota_h = sb("iota_h", [P, NA_CH * P], F16)
        ident = sb("ident", [P, P])
        ident_h = sb("ident_h", [P, P], F16)
        up = sb("up", [P, P])
        low = sb("low", [P, P])
        ones = sb("ones", [P, P])
        emask = sb("emask", [P, 4 * P])
        dcar, dbak = sb("dcar", [P, P]), sb("dbak", [P, P])
        scar, sbak = sb("scar", [P, P]), sb("sbak", [P, P])
        sneg = sb("sneg", [P, P])
        zrow = sb("zrow", [P, D])
        eps_c = sb("eps_c", [P, 1])

        AW = NA_CH * P
        halves = XD[:, :].bitcast(F16)
        at = 0

        def half(n):
            nonlocal at
            at += 4 * n
            return halves[:, at - 4 * n:at].rearrange("p (j n) -> p j n", j=4)

        oha, ohb, oha2, ohb2, ohaT = half(AW), half(NB_COL), half(AW), half(NB_COL), half(AW)
        rhi, rlo = half(NB_COL), half(NB_COL)
        zh = sb("zh", [P, 512], F16)
        eqs = XD[:, at // 2:at // 2 + 512]
        assert at // 2 + 512 <= T * D
        cnt4 = sb("cnt4", [P, 4])
        rk4 = sb("rk4", [P, 4])
        kcol = sb("kcol", [P, 4])
        tot = sb("tot", [P, 2, NA_CH])
        base = sb("base", [P, 2, NA_CH])
        TB = NA_CH * NB_COL
        HC, IC = Y[:, 0:2 * TB], Y[:, 2 * TB:4 * TB]
        NTB = RB[:, 0:4 * TB]
        NS3, ND3 = v3(S[:, 0:4 * T], 4), v3(S[:, 4 * T:8 * T], 4)

        wcat = sb("wcat", [P, NH * D])
        wsd = sb("wsd", [P, 2 * D])
        ua = sb("ua", [P, 2, NH])
        bdu = sb("bdu", [P, 2, GT * NH])
        bd1 = sb("bd1", [P, GT * NH * D])
        bdx = sb("bdx", [P, GT * 2 * D])
        bdy = sb("bdy", [P, GT * D])
        bw = sb("bw", [P, GT, NB * D])
        aw = sb("aw", [P, 3 * D])
        b_bias, b_b1, b_b2 = sb("b_bias", [P, D]), sb("b_b1", [P, D]), sb("b_b2", [P, D])
        b_fcb = sb("b_fcb", [P, 1])
        bc = sb("bc", [P, D])
        bm = sb("bm", [P, 1])
        xt = sb("xt", [P, 2, 2 * P])
        xg = sb("xg", [P, 2, P])
        xt_y = sb("xt_y", [P, 2, P])
        prod = sb("prod", [P, 512])
        pr2, pq2, sc4 = sb("pr2", [P, GT * D]), sb("pq2", [P, GT * D]), sb("sc4", [P, GT])
        car = sb("car", [P, D])
        tl = sb("tl", [P, D])

        nx, nsq = RB[:, 0:CR * D], RB[:, CR * D:2 * CR * D]
        nr1, nr2, nr3 = sb("nr1", [P, CR]), sb("nr2", [P, CR]), sb("nr3", [P, CR])
        nx3, nsq3 = v3(nx), v3(nsq)

        s_pad = sem("padding_set")
        s_in = sem("edges_loaded")
        s_w = sem("weights_loaded")
        s_bd0 = sem("blocks_zeroed")
        s_bd = sem("blocks_loaded")
        s_relt = sem("relation_table_written")
        s_zr = sem("zero_row_set")
        s_ztab = sem("zero_rows_written")
        s_const = sem("pool_constants_ready")
        s_cst2 = sem("masks_ready")
        s_ids = sem("node_indices_ready")
        s_slot = sem("ring_slot_ready")
        s_land = [[sem(f"landed{f}{h}") for h in range(2)] for f in range(2)]
        s_tick = [sem(f"tick_{e}") for e in ("pool", "act", "dve", "pe", "sp")]
        s_oh = sem("onehots_ready")
        s_ohu = sem("onehots_used")
        s_hist = sem("histogram_done")
        s_tot = sem("totals_ready")
        s_base = sem("bases_ready")
        s_nt = sem("node_table_ready")
        s_ntw = sem("node_table_written")
        s_actp = sem("act_passes_done")
        s_dve = sem("dve_steps")
        s_rinit = sem("running_counts_zeroed")
        s_ohT = sem("onehots_transposed")
        s_ohTc = sem("transposed_copied")
        s_kt = sem("keys_transposed")
        s_g = sem("counts_gathered")
        s_gu = sem("counts_read")
        s_ru = sem("running_counts_updated")
        s_rhi = sem("high_parts_ready")
        s_rc = sem("low_parts_ready")
        s_tr = sem("row_of_keys_ready")
        s_trw = sem("row_of_keys_wanted")
        s_tail = sem("tails_ready")
        s_carry = sem("carries_ready")
        s_tab = sem("table_tile_ready")
        s_tabw = sem("table_written")
        s_sqi = sem("squares_wanted")
        s_sqo = sem("squares_ready")
        s_sri = sem("roots_wanted")
        s_sro = sem("roots_ready")
        s_nin = sem("node_chunk_loaded")
        s_nok = sem("node_chunk_done")
        s_nout = sem("node_chunk_written")
        s_grp = sem("group_source_ready")
        s_xtp = sem("group_transposed")
        s_xtc = sem("group_copied")
        s_mm = sem("group_multiplied")
        s_mmu = sem("group_product_used")
        s_row = sem("src_rows_loaded")
        s_sct = sem("rows_scattered")
        s_wb = sem("blocks_built")
        s_nri = sem("node_roots_wanted")
        s_nro = sem("node_roots_ready")
        s_ei = sem("exponentials_wanted")
        s_eo = sem("exponentials_ready")
        s_stg = sem("group_staged")

        APPNP_STEPS, NODE_STEPS = 108, 26
        block = ctx.enter_context(nc.Block())
        edges = lambda a: a[0:(P - 1) * T].rearrange("(p t) -> p t", t=T)
        edges_last = lambda a: a[(P - 1) * T:E].rearrange("(p t) -> p t", p=1)
        dense = lambda a, w: a[0:EP, :].rearrange("(p t) d -> p (t d)", t=T)

        PASS_X_SRC, PASS_NT_SRC, PASS_NT_DST, PASS_L0 = range(4)
        PASS_X_DST = PASS_L0 + K_STEPS
        PASS_ROW, PASS_ATT_SRC, PASS_ATT_DST, PASS_REL, PASS_RGCN, PASS_OUT_DST, PASS_OUT_SRC = \
            range(PASS_X_DST + 1, PASS_X_DST + 8)

        def family(n):
            return (0, n) if n < PASS_ROW else (1, n - PASS_ROW)

        def slot_count(n, i, h):
            return 2 * ROUNDS * n + 2 * i + h + 1

        def land_count(n, i):
            return LAND * (ROUNDS * family(n)[1] + i + 1)

        def ring_row(h, j, w):
            return ring[:, h, j * w:(j + 1) * w]

        def dma_pass(pool, n, w, table, scatter=False, limit=None, k=0, f=None):
            f = family(n)[0] if f is None else f
            with pool.Fori(0, ROUNDS) as i:
                for h in range(2):
                    pool.wait_ge(s_slot, i * 2 + k * (2 * ROUNDS) + slot_count(n, 0, h))
                    pool.sem_inc(s_tick[0], 1)
                    for j in range(U):
                        off = bass.IndirectOffsetOnAxis(ap=ridx[:, h, j:j + 1], axis=0)
                        if scatter:
                            pool.indirect_dma_start(out=table, out_offset=off, in_=ring_row(h, j, w), in_offset=None,
                                                    bounds_check=limit, oob_is_err=False).then_inc(s_land[f][h], 16)
                        else:
                            pool.indirect_dma_start(out=ring_row(h, j, w), out_offset=None, in_=table,
                                                    in_offset=off).then_inc(s_land[f][h], 16)

        def ring_pass(eng, tick, n, fill, take, k=0, f=None):
            f = family(n)[0] if f is None else f
            for h in range(2):
                fill(0, h).then_inc(s_slot, 1)
            with eng.Fori(0, ROUNDS - 1) as i:
                for h in range(2):
                    eng.wait_ge(s_land[f][h], i * LAND + k * (LAND * ROUNDS) + land_count(n, 0))
                    eng.sem_inc(tick, 1)
                    take(i, h)
                    fill(i + 1, h).then_inc(s_slot, 1)
            for h in range(2):
                eng.wait_ge(s_land[f][h], k * (LAND * ROUNDS) + land_count(n, ROUNDS - 1))
                eng.sem_inc(tick, 1)
                take(ROUNDS - 1, h).then_inc(s_actp, 1)

        def cols(tile, i, h, w=1):
            return tile[:, bass.ds(i * (2 * U * w) + h * U * w, U * w)]

        @block.sync
        def _(sp):
            sp.wait_ge(s_pad, 1)
            for a, t in ((src, srci), (dst, dsti), (etype, etyi), (eweight, ew)):
                sp.dma_start(t[0:P - 1, :], edges(a)).then_inc(s_in, 16)
                sp.dma_start(t[P - 1:P, 0:LASTV], edges_last(a)).then_inc(s_in, 16)
            sp.dma_start(rel_d[:, 0:NB], w_comp).then_inc(s_relt, 16)
            sp.dma_start(rel_d[:, NB:NB + D], rel_emb).then_inc(s_relt, 16)
            for j in range(4):
                sp.dma_start(wcat[32 * j:32 * j + 32, :].rearrange("i (h o) -> i h o", h=NH),
                             w1.rearrange("h i o -> i h o")).then_inc(s_w, 16)
                with nc.allow_non_contiguous_dma(reason="transposed 32 x 32 weights"):
                    sp.dma_start(aw[32 * j:32 * j + 32, 0:D], A1w.rearrange("o i -> i o")).then_inc(s_w, 16)
                    sp.dma_start(aw[32 * j:32 * j + 32, D:2 * D], A2w.rearrange("o i -> i o")).then_inc(s_w, 16)
                sp.dma_start(aw[32 * j:32 * j + 32, 2 * D:3 * D], w_self).then_inc(s_w, 16)
            sp.dma_start(wsd[:, :], fc_w[0, :].partition_broadcast(P)).then_inc(s_w, 16)
            sp.dma_start(b_bias[:, :], bias1.partition_broadcast(P)).then_inc(s_w, 16)
            sp.dma_start(b_b1[:, :], A1b.partition_broadcast(P)).then_inc(s_w, 16)
            sp.dma_start(b_b2[:, :], A2b.partition_broadcast(P)).then_inc(s_w, 16)
            sp.dma_start(b_fcb[:, :], fc_b.partition_broadcast(P)).then_inc(s_w, 16)
            sp.wait_ge(s_bd0, 1)
            for j in range(4):
                sp.dma_start(bw[32 * j:32 * j + 32, j, :].rearrange("i (b o) -> i b o", b=NB),
                             w2.rearrange("b i o -> i b o")).then_inc(s_bd, 16)
            sp.wait_ge(s_zr, 1)
            for tab in (agg_d, att_d, rgcn_d):
                sp.dma_start(tab[EP:EP + P, :], zrow[:, :]).then_inc(s_ztab, 16)
            sp.wait_ge(s_nt, 1)
            for c in range(NA_CH):
                sp.dma_start(nt_d[c * P * NB_COL:(c + 1) * P * NB_COL, :].rearrange("(p b) f -> p (b f)", p=P),
                             NTB[:, c * NB_COL * 4:(c + 1) * NB_COL * 4]).then_inc(s_ntw, 16)

            def node_chunk(c):
                rows = lambda a: a.rearrange("(p r) d -> p (r d)", p=NODE_P)[:, bass.ds(c * (CR * D), CR * D)]
                sp.dma_start(nx[0:NODE_P, :], rows(x)).then_inc(s_nin, 16)
                sp.wait_ge(s_nok, c + 1)
                sp.sem_inc(s_tick[4], 1)
                sp.dma_start(rows(out), nx[0:NODE_P, :]).then_inc(s_nout, 16)
                sp.wait_ge(s_nout, c * 16 + 16)
                sp.sem_inc(s_tick[4], 1)

            def write_table(tab, n, k=0):
                sp.wait_ge(s_tab, k + n)
                sp.sem_inc(s_tick[4], 1)
                sp.dma_start(dense(tab, D), S[:, :]).then_inc(s_tabw, 16)

            sp.wait_ge(s_ntw, 16 * NA_CH)
            write_table(agg_d, 1)
            with sp.Fori(0, CH // 2) as k:
                for c in range(2):
                    node_chunk(k * 2 + c)
                write_table(agg_d, 2, k)
            write_table(agg_d, K_STEPS)
            sp.wait_ge(s_sct, 1)
            sp.dma_start(ROWS, dense(row_d, ROW1)).then_inc(s_row, 16)
            write_table(att_d, K_STEPS + 1)
            write_table(rgcn_d, K_STEPS + 2)

        @block.gpsimd
        def _(pool):
            pool.memset(ident[:, :], 0.0).then_inc(s_const, 1)
            pool.memset(ones[:, :], 1.0).then_inc(s_const, 1)
            pool.memset(up[:, :], 1.0).then_inc(s_const, 1)
            pool.memset(low[:, :], 1.0).then_inc(s_const, 1)
            pool.iota(q_f[:, :], pattern=[[1, T]], base=0, channel_multiplier=T,
                      allow_small_or_imprecise_dtypes=True).then_inc(s_const, 1)
            pool.iota(iota_h[:, :], pattern=[[1, NA_CH * P]], base=0, channel_multiplier=0,
                      allow_small_or_imprecise_dtypes=True).then_inc(s_const, 1)
            pool.wait_ge(s_const, 6)
            pool.affine_select(out=ident[:, :], in_=ident[:, :], compare_op=ALU.not_equal, fill=1.0, base=0,
                               pattern=[[-1, P]], channel_multiplier=1).then_inc(s_const, 1)
            pool.affine_select(out=up[:, :], in_=up[:, :], compare_op=ALU.is_gt, fill=0.0, base=0,
                               pattern=[[1, P]], channel_multiplier=-1).then_inc(s_const, 1)
            pool.affine_select(out=low[:, :], in_=low[:, :], compare_op=ALU.is_gt, fill=0.0, base=0,
                               pattern=[[-1, P]], channel_multiplier=1).then_inc(s_const, 1)
            dma_pass(pool, PASS_X_SRC, D, x[:, :])
            pool.wait_ge(s_ntw, 16 * NA_CH)
            dma_pass(pool, PASS_NT_SRC, 4, nt_d[:, :])
            dma_pass(pool, PASS_NT_DST, 4, nt_d[:, :])
            pool.wait_ge(s_ztab, 48)
            with pool.Fori(0, K_STEPS) as k:
                pool.wait_ge(s_tabw, k * 16 + 16)
                pool.sem_inc(s_tick[0], 1)
                dma_pass(pool, PASS_L0, D, agg_d[:, :], k=k)
            dma_pass(pool, PASS_X_DST, D, x[:, :])
            dma_pass(pool, PASS_ROW, ROW1, row_d[:, :], scatter=True)
            pool.wait_ge(s_tabw, 16 * (K_STEPS + 1))
            dma_pass(pool, PASS_ATT_SRC, D, att_d[:, :])
            dma_pass(pool, PASS_ATT_DST, D, att_d[:, :])
            pool.wait_ge(s_relt, 32)
            dma_pass(pool, PASS_REL, RW, rel_d[:, :])
            pool.wait_ge(s_tabw, 16 * (K_STEPS + 2))
            dma_pass(pool, PASS_RGCN, D, rgcn_d[:, :])
            pool.wait_ge(s_nout, 16 * CH)
            dma_pass(pool, PASS_OUT_DST, D, out[:, :], scatter=True, limit=N - 1)
            dma_pass(pool, PASS_OUT_SRC, D, out[:, :], scatter=True, limit=N - 1)
            for h in range(2):
                pool.wait_ge(s_land[1][h], land_count(PASS_OUT_SRC, ROUNDS - 1))

        def bc3(ap, n):
            return ap.unsqueeze(2).to_broadcast([ap.shape[0], ap.shape[1], n])

        def mid(ap, n):
            return ap.unsqueeze(1).to_broadcast([ap.shape[0], n, ap.shape[1]])

        @block.vector
        def _(dve):
            st = Steps(dve, s_dve)
            tick = s_tick[2]
            V = nc.vector

            st.do(V.memset(srci[:, :], N))
            st.do(V.memset(dsti[:, :], N))
            st.do(V.memset(etyi[:, :], 0))
            st.do(V.memset(ew[:, :], 0.0))
            st.wait()
            dve.sem_inc(s_pad, 1)
            V.memset(zrow[:, :], 0.0).then_inc(s_zr, 1)
            st.do(V.memset(bw[:, :, :], 0.0))
            st.do(V.memset(bdu[:, :, :], 0.0))
            st.do(V.memset(bd1[:, :], 0.0))
            st.do(V.memset(bdx[:, :], 0.0))
            st.do(V.memset(bdy[:, :], 0.0))
            st.do(V.memset(eps_c[:, :], EPS))
            st.do(V.memset(zh[:, :], 0.0))
            st.wait()
            dve.sem_inc(s_bd0, 1)

            dve.wait_ge(s_in, 16 * 8)
            st.do(V.tensor_scalar(srcf[:, :], srci[:, :], 0.0, None, ALU.add))
            st.do(V.tensor_scalar(dstf[:, :], dsti[:, :], 0.0, None, ALU.add))
            st.do(V.tensor_scalar(xsi[:, :], srci[:, :], float(N - 1), None, ALU.min))
            st.do(V.tensor_scalar(xdi[:, :], dsti[:, :], float(N - 1), None, ALU.min))
            st.wait()
            dve.sem_inc(s_ids, 1)
            for key, a, b in ((srci, a_s, b_s), (dsti, a_d, b_d)):
                st.seq(V.tensor_scalar(tmpi[:, :], key[:, :], NB_COL.bit_length() - 1, None, ALU.logical_shift_right))
                st.seq(V.tensor_scalar(a[:, :], tmpi[:, :], 0.0, None, ALU.add))
                st.seq(V.tensor_scalar(tmpi[:, :], key[:, :], NB_COL - 1, None, ALU.bitwise_and))
                st.seq(V.tensor_scalar(b[:, :], tmpi[:, :], 0.0, None, ALU.add))

            dve.wait_ge(s_const, 9)
            st.do(V.tensor_copy(ident_h[:, :], ident[:, :]))
            st.do(V.memset(emask[:, 0:3 * P], 1.0))
            st.do(V.tensor_copy(emask[:, 3 * P:4 * P], low[:, :]))
            st.wait()
            dve.sem_inc(s_cst2, 1)

            with dve.Fori(0, NG) as i:
                for j in range(4):
                    col = lambda t: t[:, bass.ds(i * 4 + j, 1)]
                    dve.wait_ge(s_ohu, i * 4 + j + 1)
                    dve.sem_inc(tick, 1)
                    V.tensor_scalar(oha[:, j, :], iota_h[:, :], col(a_d), None, ALU.is_equal)
                    V.tensor_scalar(ohb[:, j, :], iota_h[:, 0:NB_COL], col(b_d), None, ALU.is_equal)
                    V.tensor_scalar(oha2[:, j, :], iota_h[:, :], col(a_s), None, ALU.is_equal)
                    V.tensor_scalar(ohb2[:, j, :], iota_h[:, 0:NB_COL], col(b_s), None,
                                    ALU.is_equal).then_inc(s_oh, 1)
            dve.wait_ge(s_hist, 1)
            hc = lambda tile, k, c: tile[:, k * TB + c * NB_COL:k * TB + (c + 1) * NB_COL]
            for k in range(2):
                for c in range(NA_CH):
                    st.do(V.tensor_scalar(hc(HC, k, c), bank[c][:, k * NB_COL:(k + 1) * NB_COL], 0.0, None, ALU.add))
            st.wait()
            for k in range(2):
                for c in range(NA_CH):
                    st.do(V.tensor_tensor_scan(hc(IC, k, c), ones[:, 0:1].to_broadcast([P, NB_COL]), hc(HC, k, c),
                                               0.0, ALU.mult, ALU.add))
            st.wait()
            for k in range(2):
                st.do(V.tensor_copy(tot[:, k, :], IC[:, k * TB:(k + 1) * TB].rearrange(
                    "p (c b) -> p c b", b=NB_COL)[:, :, NB_COL - 1]))
            st.wait()
            dve.sem_inc(s_tot, 1)
            dve.wait_ge(s_base, 1)
            st.do(V.tensor_copy(base[:, :, :], bank[4][:, 0:2 * NA_CH].rearrange("p (k c) -> p k c", k=2)))
            st.do(V.tensor_copy(tot[:, :, :], bank[5][:, 0:2 * NA_CH].rearrange("p (k c) -> p k c", k=2)))
            st.wait()
            for c in range(1, NA_CH):
                for e in range(c):
                    st.seq(V.tensor_tensor(base[:, :, c:c + 1], base[:, :, c:c + 1], tot[:, :, e:e + 1], ALU.add))
            for k in range(2):
                for c in range(NA_CH):
                    st.do(V.tensor_scalar(hc(IC, k, c), hc(IC, k, c), base[:, k, c:c + 1], float(-1 - ZROW), ALU.add,
                                          ALU.add))
            st.wait()
            nt = NTB.rearrange("p (n f) -> p n f", f=4)
            for k in range(2):
                h, e = HC[:, k * TB:(k + 1) * TB], IC[:, k * TB:(k + 1) * TB]
                st.do(V.tensor_copy(nt[:, :, 2 * k + 1], h))
                st.seq(V.scalar_tensor_tensor(out=e, in0=h, scalar=0.0, in1=e, op0=ALU.is_gt, op1=ALU.mult))
                st.do(V.tensor_scalar(nt[:, :, 2 * k], e, float(ZROW), None, ALU.add))
            st.wait()
            dve.sem_inc(s_nt, 1)

            st.do(V.memset(rhi[:, :, :], 0.0))
            st.do(V.memset(rlo[:, :, :], 0.0))
            with st.loop(NG, 8 + 1 + 8 + 2 + 1) as i:
                dve.wait_ge(s_gu, i + 1)
                dve.sem_inc(tick, 1)
                for j in range(4):
                    col = lambda t: t[:, bass.ds(i * 4 + j, 1)]
                    st.do(V.tensor_scalar(oha[:, j, :], iota_h[:, :], col(a_s), None, ALU.is_equal))
                    st.do(V.tensor_scalar(ohb[:, j, :], iota_h[:, 0:NB_COL], col(b_s), None, ALU.is_equal))
                st.do(V.tensor_scalar(kcol[:, :], srcf[:, bass.ds(i * 4, 4)], 0.0, None, ALU.add))
                st.wait()
                dve.sem_inc(s_oh, 1)
                dve.wait_ge(s_kt, i + 1)
                dve.sem_inc(tick, 1)
                for j in range(4):
                    n = (j + 1) * P
                    st.seq(V.scalar_tensor_tensor(out=eqs[:, 0:n], in0=bank[4][:, 0:n],
                                                 scalar=srcf[:, bass.ds(i * 4 + j, 1)],
                                                 in1=emask[:, 4 * P - n:4 * P], op0=ALU.is_equal, op1=ALU.mult,
                                                 accum_out=rk4[:, j:j + 1]))
                dve.wait_ge(s_g, i + 1)
                dve.sem_inc(tick, 1)
                for j in range(4):
                    g = bank[5 + j // 2][:, (j % 2) * NB_COL:(j % 2 + 1) * NB_COL]
                    st.seq(V.scalar_tensor_tensor(out=eqs[:, 0:NB_COL], in0=g, scalar=1.0, in1=ohb[:, j, :],
                                                 op0=ALU.mult, op1=ALU.mult, accum_out=cnt4[:, j:j + 1]))
                dve.wait_ge(s_rhi, i + 1)
                dve.sem_inc(tick, 1)
                for b in range(2):
                    r = bank[b][:, :]
                    st.do(V.tensor_tensor(rlo[:, 2 * b:2 * b + 2, :].rearrange("p c n -> p (c n)"), r,
                                          rhi[:, 2 * b:2 * b + 2, :].rearrange("p c n -> p (c n)"), ALU.subtract))
                st.wait()
                dve.sem_inc(s_rc, 1)
                st.do(V.tensor_tensor(posf[:, bass.ds(i * 4, 4)], cnt4[:, :], rk4[:, :], ALU.add))
            st.wait()

            dve.wait_ge(s_actp, 6)
            st.do(V.tensor_copy(gin[:, :], NS3[:, :, 0]))
            st.do(V.tensor_copy(gout_s[:, :], NS3[:, :, 2]))
            st.do(V.tensor_copy(gout_d[:, :], ND3[:, :, 2]))
            st.do(V.tensor_tensor(t1[:, :], NS3[:, :, 2], NS3[:, :, 3], ALU.subtract))
            st.wait()
            st.seq(V.scalar_tensor_tensor(out=posf[:, :], in0=t1[:, :], scalar=1.0, in1=posf[:, :], op0=ALU.add,
                                          op1=ALU.add))
            st.do(V.tensor_copy(posi[:, :], posf[:, :]))
            st.do(V.tensor_tensor(dend[:, :], ND3[:, :, 0], q_f[:, :], ALU.is_equal))
            st.do(V.tensor_tensor(t1[:, :], NS3[:, :, 2], posf[:, :], ALU.is_equal))
            st.do(V.tensor_scalar(t2[:, :], NS3[:, :, 1], 0.0, None, ALU.is_equal))
            st.wait()
            st.seq(V.tensor_tensor(t1[:, :], t1[:, :], t2[:, :], ALU.mult))
            for flag, key, dest in ((t1, srcf, osi), (dend, dstf, odi)):
                st.seq(V.scalar_tensor_tensor(out=t2[:, :], in0=key[:, :], scalar=float(-OOB), in1=flag[:, :],
                                              op0=ALU.add, op1=ALU.mult))
                if dest is osi:
                    st.seq(V.tensor_scalar(t3[:, :], t2[:, :], float(OOB), None, ALU.add))
                else:
                    st.seq(V.tensor_scalar(posf[:, :], t2[:, :], float(OOB), None, ALU.add))
            st.do(V.tensor_scalar(t1[:, :], NS3[:, :, 1], 1.0, None, ALU.max))
            st.do(V.tensor_scalar(t2[:, :], NS3[:, :, 3], 1.0, None, ALU.max))
            st.do(V.tensor_scalar(c3[:, :], ND3[:, :, 1], 1.0, None, ALU.max))
            st.wait()
            dve.sem_inc(s_sri, 1)
            dve.wait_ge(s_sro, 1)
            st.do(V.reciprocal(t1[:, :], t1[:, :]))
            st.do(V.reciprocal(t2[:, :], t2[:, :]))
            st.seq(V.reciprocal(c3[:, :], c3[:, :]))
            st.do(V.tensor_scalar(c3[:, :], c3[:, :], 1.0 - ALPHA, None, ALU.mult))
            st.do(V.scalar_tensor_tensor(out=c1[:, :], in0=t1[:, :], scalar=1.0 - ALPHA, in1=t2[:, :], op0=ALU.mult,
                                         op1=ALU.mult))
            st.do(V.tensor_scalar(c2[:, :], t2[:, :], ALPHA, None, ALU.mult))

            def segments(key, mask, first, fcar, fbak, neg=None, n=0):
                st.do(V.tensor_tensor(mask[:, 1:T], key[:, 1:T], key[:, 0:T - 1], ALU.is_equal))
                st.do(V.memset(mask[:, 0:1], 0.0))
                st.do(V.tensor_scalar(first[:, :], key[:, :], key[:, 0:1], None, ALU.is_equal))
                st.do(V.tensor_copy(tl[:, 0:1], key[:, 0:1]))
                st.do(V.tensor_copy(tl[:, 1:2], key[:, T - 1:T]))
                st.wait()
                dve.sem_inc(s_trw, 1)
                dve.wait_ge(s_tr, n + 1)
                st.do(V.scalar_tensor_tensor(out=fcar[:, :], in0=bank[4][:, 0:P], scalar=tl[:, 1:2], in1=up[:, :],
                                             op0=ALU.is_equal, op1=ALU.mult))
                st.do(V.scalar_tensor_tensor(out=fbak[:, :], in0=bank[5][:, 0:P], scalar=tl[:, 0:1], in1=low[:, :],
                                             op0=ALU.is_equal, op1=ALU.mult))
                if neg is not None:
                    st.wait()
                    st.seq(V.tensor_scalar(neg[:, :], fbak[:, :], 1.0, BIG, ALU.subtract, ALU.mult))
                st.wait()

            ncarry = [0]

            def carries():
                dve.sem_inc(s_tail, 1)
                ncarry[0] += 1
                dve.wait_ge(s_carry, ncarry[0])

            def segment_sums(src3, dst3, width, mask, first):
                for d in range(width):
                    st.do(V.tensor_tensor_scan(dst3[:, :, d], mask[:, :], src3[:, :, d], 0.0, ALU.mult, ALU.add))
                st.wait()
                st.seq(V.tensor_scalar(tl[:, 0:width], dst3[:, T - 1, :], 0.0, None, ALU.add))
                carries()
                st.seq(V.tensor_copy(car[:, 0:width], bank[7][:, 0:width]))
                for d in range(width):
                    st.do(V.scalar_tensor_tensor(out=dst3[:, :, d], in0=first[:, :], scalar=car[:, d:d + 1],
                                                 in1=dst3[:, :, d], op0=ALU.mult, op1=ALU.add))
                st.wait()

            def spread_back(t3_, width, mask_end, key):
                st.seq(V.tensor_scalar(t1[:, :], mask_end[:, :], -1.0, 1.0, ALU.mult, ALU.add))
                st.seq(V.tensor_tensor(t3_, t3_, bc3(mask_end[:, :], width), ALU.mult))
                for d in range(width):
                    st.do(V.tensor_tensor_scan(t3_[:, ::-1, d], t1[:, ::-1], t3_[:, ::-1, d], 0.0, ALU.mult, ALU.add))
                st.do(V.tensor_scalar(t2[:, :], key[:, :], key[:, T - 1:T], None, ALU.is_equal))
                st.wait()
                st.do(V.tensor_scalar(tl[:, 0:width], t3_[:, 0, :], 0.0, None, ALU.add))
                st.do(V.tensor_scalar(t2[:, :], t2[:, :], t1[:, T - 1:T], None, ALU.mult))
                st.wait()
                carries()
                st.seq(V.tensor_copy(car[:, 0:width], bank[7][:, 0:width]))
                for d in range(width):
                    st.do(V.scalar_tensor_tensor(out=t3_[:, :, d], in0=t2[:, :], scalar=car[:, d:d + 1],
                                                 in1=t3_[:, :, d], op0=ALU.mult, op1=ALU.add))
                st.wait()

            nln = [0]

            def layernorm(t3_, sq3):
                nln[0] += 1
                st.seq(V.tensor_reduce(t1[:, :], t3_, AX.X, ALU.add))
                st.seq(V.tensor_scalar(t1[:, :], t1[:, :], 1.0 / D, None, ALU.mult))
                st.seq(V.tensor_tensor(t3_, t3_, bc3(t1[:, :], D), ALU.subtract))
                dve.sem_inc(s_sqi, 1)
                dve.wait_ge(s_sqo, nln[0])
                st.seq(V.tensor_reduce(t1[:, :], sq3, AX.X, ALU.add))
                dve.sem_inc(s_sri, 1)
                dve.wait_ge(s_sro, nln[0] + 1)
                st.seq(V.reciprocal(t1[:, :], t1[:, :]))
                st.seq(V.tensor_tensor(t3_, t3_, bc3(t1[:, :], D), ALU.mult))

            def fill_idx(idx):
                return lambda i, h: V.tensor_scalar(ridx[:, h, :], cols(idx, i, h), 0.0, None, ALU.add)

            def slot(h, w=D):
                return ring[:, h, 0:U * w]

            st.do(V.tensor_copy(osi[:, :], t3[:, :]))
            st.wait()
            st.do(V.tensor_copy(t3[:, :], t2[:, :]))
            segments(dstf, dmask, dfirst, dcar, dbak, n=0)

            st.seq(V.tensor_tensor(Y3, XS3, bc3(t3[:, :], D), ALU.mult))
            segment_sums(Y3, S3, D, dmask, dfirst)
            dve.sem_inc(s_tab, 1)

            def appnp_take(i, h):
                y = cols(Y, i, h, D).rearrange("p (t d) -> p t d", d=D)
                xs = cols(XS, i, h, D).rearrange("p (t d) -> p t d", d=D)
                r = slot(h).rearrange("p (t d) -> p t d", d=D)
                c1c = cols(c1, i, h).unsqueeze(2).to_broadcast([P, U, D])
                c2c = cols(c2, i, h).unsqueeze(2).to_broadcast([P, U, D])
                st.do(V.tensor_tensor(r, r, c1c, ALU.mult))
                st.do(V.tensor_tensor(y, xs, c2c, ALU.mult))
                st.wait()
                dve.sem_inc(tick, 1)
                st.do(V.tensor_tensor(y, y, r, ALU.add))
                st.wait()
                dve.sem_inc(tick, 1)

            def stepped_ring_pass(n, fill, take, per, k=0):
                f = family(n)[0]
                for h in range(2):
                    fill(0, h).then_inc(s_slot, 1)
                with st.loop(ROUNDS - 1, 2 * per) as i:
                    for h in range(2):
                        dve.wait_ge(s_land[f][h], i * LAND + k * (LAND * ROUNDS) + land_count(n, 0))
                        dve.sem_inc(tick, 1)
                        take(i, h)
                        fill(i + 1, h).then_inc(s_slot, 1)
                for h in range(2):
                    dve.wait_ge(s_land[f][h], k * (LAND * ROUNDS) + land_count(n, ROUNDS - 1))
                    dve.sem_inc(tick, 1)
                    take(ROUNDS - 1, h)

            def appnp_step(k):
                stepped_ring_pass(PASS_L0, fill_idx(gin), appnp_take, 3, k)
                for d in range(D):
                    st.do(V.tensor_tensor_scan(S3[:, :, d], dmask[:, :], Y3[:, :, d], 0.0, ALU.mult, ALU.add))
                st.wait()
                st.seq(V.tensor_scalar(tl[:, :], S3[:, T - 1, :], 0.0, None, ALU.add))
                dve.sem_inc(s_tail, 1)
                dve.wait_ge(s_carry, k + 2)
                st.seq(V.tensor_copy(car[:, :], bank[7][:, 0:D]))
                for d in range(D):
                    st.do(V.scalar_tensor_tensor(out=S3[:, :, d], in0=dfirst[:, :], scalar=car[:, d:d + 1],
                                                 in1=S3[:, :, d], op0=ALU.mult, op1=ALU.add))
                st.wait()
                dve.sem_inc(s_tab, 1)

            def node_chunk(c):
                x3, q3, m = nx3[0:NODE_P], nsq3[0:NODE_P], [t[0:NODE_P, :] for t in (nr1, nr2, nr3)]
                wide = lambda t: t.unsqueeze(2).to_broadcast([NODE_P, CR, D])
                dve.wait_ge(s_nin, c * 16 + 16)
                dve.sem_inc(tick, 1)
                st.seq(V.tensor_reduce(m[0], x3, AX.X, ALU.add))
                st.seq(V.tensor_scalar(m[0], m[0], 1.0 / D, None, ALU.mult))
                st.seq(V.tensor_tensor(x3, x3, wide(m[0]), ALU.subtract))
                st.seq(V.tensor_tensor(q3, x3, x3, ALU.mult))
                st.seq(V.tensor_reduce(m[0], q3, AX.X, ALU.add))
                st.seq(V.tensor_scalar(m[0], m[0], (1 + ALPHA) ** 2 / D, None, ALU.mult))
                root(m[0], m[1], 0)
                st.seq(V.tensor_scalar(m[1], m[1], 1 + ALPHA, None, ALU.mult))
                st.seq(V.tensor_tensor(x3, x3, wide(m[1]), ALU.mult))
                st.seq(V.tensor_tensor(x3, x3, mid(bc[0:NODE_P, :], CR), ALU.add))
                st.seq(V.tensor_tensor(q3, x3, x3, ALU.mult))
                st.seq(V.tensor_reduce(m[0], q3, AX.X, ALU.add))
                st.seq(V.tensor_scalar(m[0], m[0], 1.0 / D, None, ALU.mult))
                root(m[0], m[1], 1)
                st.seq(V.tensor_copy(m[2], m[1]))
                for f in (1.0, 4.0):
                    st.seq(V.tensor_tensor(m[0], m[0], m[1], ALU.mult))
                    st.seq(V.tensor_tensor(m[0], m[0], m[1], ALU.mult))
                    if f != 1.0:
                        st.seq(V.tensor_scalar(m[0], m[0], f, None, ALU.mult))
                    root(m[0], m[1], 2 if f == 1.0 else 3)
                    st.seq(V.tensor_tensor(m[2], m[2], m[1], ALU.mult))
                st.seq(V.tensor_scalar(m[2], m[2], 2.0, None, ALU.mult))
                st.do(V.tensor_tensor(x3, x3, wide(m[2]), ALU.mult))
                st.wait()
                dve.sem_inc(s_nok, 1)

            node_root = {}

            def root(v, r, which):
                dve.sem_inc(s_nri, 1)
                dve.wait_ge(s_nro, node_root["c"] * 4 + which + 1)
                dve.sem_inc(tick, 1)
                st.seq(V.reciprocal(r, r))

            dve.wait_ge(s_w, 16 * (4 * 4 + 5))
            dve.wait_ge(s_bd, 16 * 4)
            st.seq(V.tensor_reduce(bm[:, :], b_bias[:, :], AX.X, ALU.add))
            st.seq(V.tensor_scalar(bm[:, :], bm[:, :], -1.0 / D, None, ALU.mult))
            st.seq(V.tensor_scalar(bc[:, :], b_bias[:, :], bm[:, 0:1], None, ALU.add))
            for k in range(2):
                st.seq(V.tensor_tensor(prod[:, 0:NH * D].rearrange("p (h o) -> p h o", h=NH),
                                       wcat[:, :].rearrange("p (h o) -> p h o", h=NH),
                                       mid(wsd[:, k * D:(k + 1) * D], NH), ALU.mult))
                st.seq(V.tensor_reduce(ua[:, k, :], prod[:, 0:NH * D].rearrange("p (h o) -> p h o", h=NH), AX.X,
                                       ALU.add))
            for j in range(GT):
                r = slice(32 * j, 32 * j + 32)
                for k in range(2):
                    st.do(V.tensor_copy(bdu[r, k, j * NH:(j + 1) * NH], ua[r, k, :]))
                st.do(V.tensor_scalar(bd1[r, j * NH * D:(j + 1) * NH * D], wcat[r, :], 1.0 / NH, None, ALU.mult))
                st.do(V.tensor_copy(bdx[r, j * 2 * D:j * 2 * D + D], aw[r, 0:D]))
                st.do(V.tensor_copy(bdx[r, j * 2 * D + D:(j + 1) * 2 * D], aw[r, 2 * D:3 * D]))
                st.do(V.tensor_copy(bdy[r, j * D:(j + 1) * D], aw[r, D:2 * D]))
            st.wait()
            dve.sem_inc(s_wb, 1)

            with st.loop(CH // 2, APPNP_STEPS + 2 * NODE_STEPS) as k:
                for c in range(2):
                    node_root["c"] = k * 2 + c
                    node_chunk(k * 2 + c)
                appnp_step(k)
            appnp_step(K_STEPS - 2)
            ncarry[0] = K_STEPS

            dve.wait_ge(s_tabw, 16 * K_STEPS)

            def last_take(i, h):
                y = cols(Y, i, h, D).rearrange("p (t d) -> p t d", d=D)
                r = slot(h).rearrange("p (t d) -> p t d", d=D)
                dve.sem_inc(tick, 1)
                st.do(V.tensor_tensor(y, r, cols(c1, i, h).unsqueeze(2).to_broadcast([P, U, D]), ALU.mult))
                st.wait()
                dve.sem_inc(tick, 1)

            st.seq(V.reciprocal(t2[:, :], t3[:, :]))
            st.seq(V.tensor_tensor(c1[:, :], c1[:, :], t2[:, :], ALU.mult))
            stepped_ring_pass(PASS_L0, fill_idx(gin), last_take, 1, K_STEPS - 1)
            st.seq(V.scalar_tensor_tensor(out=XS[:, :], in0=XS[:, :], scalar=1 + ALPHA, in1=Y[:, :], op0=ALU.mult,
                                          op1=ALU.add))
            layernorm(XS3, Y3)

            def copy_take(dest, w=D):
                def take(i, h):
                    st.do(V.tensor_scalar(cols(dest, i, h, w), slot(h, w), 0.0, None, ALU.add))
                    st.wait()
                    dve.sem_inc(tick, 1)
                return take

            stepped_ring_pass(PASS_X_DST, fill_idx(xdi), copy_take(XD), 1)
            st.do(V.tensor_copy(odi[:, :], posf[:, :]))
            spread_back(S3, D, dend, dstf)
            st.seq(V.tensor_tensor(S3, S3, bc3(c3[:, :], D), ALU.mult))
            st.seq(V.scalar_tensor_tensor(out=XD[:, :], in0=XD[:, :], scalar=1 + ALPHA, in1=S[:, :], op0=ALU.mult,
                                          op1=ALU.add))
            layernorm(XD3, Y3)
            dve.sem_inc(s_grp, 1)
            dve.sem_inc(s_mmu, 1)
            with dve.Fori(0, NG) as g:
                dve.wait_ge(s_mm, g + 1)
                dve.sem_inc(tick, 1)
                V.tensor_scalar(z4t[:, bass.ds(g * (GT * NH), GT * NH)], bank[6][:, 0:GT * NH], b_fcb[:, 0:1], None,
                                ALU.add).then_inc(s_mmu, 1)
            dve.wait_ge(s_mmu, NG + 1)
            st.seq(V.scalar_tensor_tensor(out=z4t[:, :], in0=z4t[:, :], scalar=0.2, in1=z4t[:, :], op0=ALU.mult,
                                          op1=ALU.max))

            def row_fill(i, h):
                r = ring[:, h, 0:U * ROW1].rearrange("p (t d) -> p t d", d=ROW1)
                V.tensor_scalar(r[:, :, 0:D], cols(XD, i, h, D).rearrange("p (t d) -> p t d", d=D), 0.0, None, ALU.add)
                V.tensor_scalar(r[:, :, D:D + NH], cols(z4t, i, h, NH).rearrange("p (t d) -> p t d", d=NH), 0.0, None,
                                ALU.add)
                V.tensor_scalar(r[:, :, D + NH:D + NH + 1], cols(srcf, i, h).unsqueeze(2), 0.0, None, ALU.add)
                V.tensor_scalar(r[:, :, D + NH + 1:ROW1], cols(srcf, i, h).unsqueeze(2).to_broadcast([P, U, 3]), 0.0,
                                None, ALU.mult)
                return V.tensor_scalar(ridx[:, h, :], cols(posi, i, h), 0.0, None, ALU.add)

            stepped_ring_pass(PASS_ROW, row_fill, lambda i, h: None, 0)
            dve.sem_inc(s_sct, 1)
            dve.wait_ge(s_row, 16)

            ksrc = ROWS3[:, :, D + NH]
            st.seq(V.tensor_scalar(ks[:, :], ksrc, 0.0, None, ALU.add))
            segments(ks, smask, sfirst, scar, sbak, neg=sneg, n=1)
            st.do(V.tensor_scalar(send[:, 0:T - 1], smask[:, 1:T], -1.0, 1.0, ALU.mult, ALU.add))
            st.do(V.tensor_reduce(bm[:, :], scar[:, :], AX.X, ALU.max))
            st.wait()
            st.seq(V.tensor_scalar(send[:, T - 1:T], bm[:, :], -1.0, 1.0, ALU.mult, ALU.add))
            st.seq(V.tensor_scalar(t1[:, :], smask[:, :], 1.0, BIG, ALU.subtract, ALU.mult))
            zr = ROWS3[:, :, D:D + NH]
            for h in range(NH):
                st.do(V.tensor_tensor_scan(e43[:, :, h], t1[:, :], zr[:, :, h], -BIG, ALU.add, ALU.max))
            st.wait()
            st.seq(V.tensor_scalar(tl[:, 0:NH], e43[:, T - 1, :], 0.0, None, ALU.add))
            dve.sem_inc(s_trw, 1)
            dve.wait_ge(s_tr, 3)
            st.seq(V.tensor_tensor(prod[:, :].rearrange("p (h m) -> p h m", h=NH),
                                   bank[4][:, :].rearrange("p (h m) -> p h m", h=NH), mid(sneg[:, :], NH), ALU.add))
            st.seq(V.tensor_reduce(car[:, 0:NH], prod[:, :].rearrange("p (h m) -> p h m", h=NH), AX.X, ALU.max))
            st.seq(V.tensor_scalar(t1[:, :], sfirst[:, :], 1.0, BIG, ALU.subtract, ALU.mult))
            for h in range(NH):
                st.do(V.scalar_tensor_tensor(out=e43[:, :, h], in0=t1[:, :], scalar=car[:, h:h + 1], in1=e43[:, :, h],
                                             op0=ALU.add, op1=ALU.max))
            st.wait()
            spread_back(e43, NH, send, ks)
            st.seq(V.tensor_tensor(z43, zr, e43, ALU.subtract))
            dve.sem_inc(s_ei, 1)
            dve.wait_ge(s_eo, 1)
            segment_sums(z43, e43, NH, smask, sfirst)
            spread_back(e43, NH, send, ks)
            st.seq(V.reciprocal(e4t[:, :], e4t[:, :]))
            st.seq(V.tensor_tensor(z43, z43, e43, ALU.mult))
            dve.sem_inc(s_grp, 1)
            with st.loop(NG, 3) as g:
                dve.wait_ge(s_mm, g + NG + 1)
                dve.sem_inc(tick, 1)
                att = z4t[:, bass.ds(g * (GT * NH), GT * NH)]
                st.do(V.tensor_tensor(prod[:, :].rearrange("p (th o) -> p th o", o=D),
                                      bank[6][:, :].rearrange("p (th o) -> p th o", o=D),
                                      att.unsqueeze(2).to_broadcast([P, GT * NH, D]), ALU.mult))
                st.wait()
                dve.sem_inc(s_mmu, 1)
                st.do(V.tensor_reduce(pr2[:, :].rearrange("p (t o) -> p t o", o=D),
                                      prod[:, :].rearrange("p (t h o) -> p t o h", h=NH, o=D), AX.X, ALU.add))
                st.wait()
                dve.sem_inc(tick, 1)
                st.seq(V.tensor_scalar(Y[:, bass.ds(g * (GT * D), GT * D)], pr2[:, :], 0.0, None, ALU.add))
            segment_sums(Y3, S3, D, smask, sfirst)
            dve.sem_inc(s_tab, 1)

            def add_take(dest):
                def take(i, h):
                    st.do(V.tensor_tensor(cols(dest, i, h, D), cols(dest, i, h, D), slot(h), ALU.add))
                    st.wait()
                    dve.sem_inc(tick, 1)
                return take

            stepped_ring_pass(PASS_ATT_SRC, fill_idx(gout_s), add_take(XS), 1)
            stepped_ring_pass(PASS_ATT_DST, fill_idx(gout_d), add_take(XD), 1)
            for t in (XS3, XD3):
                st.seq(V.tensor_tensor(t, t, mid(b_bias[:, :], T), ALU.add))
                layernorm(t, Y3)
            stepped_ring_pass(PASS_REL, fill_idx(etyi), copy_take(RB, RW), 1)
            st.seq(V.tensor_tensor(REL3[:, :, NB:RW], REL3[:, :, NB:RW], mid(b_b2[:, :], T), ALU.add))
            dve.sem_inc(s_grp, 1)
            n_mm = 2 * NG
            with st.loop(NG, 7 + 2 * GT) as g:
                dve.wait_ge(s_mm, g * (1 + GT) + n_mm + 1)
                dve.sem_inc(tick, 1)
                xh = bank[6][:, 0:GT * 2 * D].rearrange("p (t o) -> p t o", t=GT)
                yh = bank[5][:, 0:GT * D].rearrange("p (t o) -> p t o", t=GT)
                relg = RB[:, bass.ds(g * (GT * RW), GT * RW)].rearrange("p (t o) -> p t o", t=GT)
                pr3 = pr2[:, :].rearrange("p (t o) -> p t o", t=GT)
                pq3 = pq2[:, :].rearrange("p (t o) -> p t o", t=GT)
                st.do(V.tensor_tensor(pr3, xh[:, :, 0:D], mid(b_b1[:, :], GT), ALU.add))
                st.do(V.tensor_tensor(pq3, yh, relg[:, :, NB:RW], ALU.add))
                st.wait()
                dve.sem_inc(tick, 1)
                st.do(V.tensor_tensor(pr3, pr3, pq3, ALU.mult))
                st.wait()
                dve.sem_inc(tick, 1)
                st.do(V.tensor_reduce(sc4[:, :], pr3, AX.X, ALU.add))
                st.wait()
                dve.sem_inc(tick, 1)
                st.do(V.tensor_scalar(t1[:, bass.ds(g * GT, GT)], sc4[:, :], 1.0 / D ** 0.5, 0.0, ALU.mult, ALU.max))
                st.do(V.tensor_scalar(S[:, bass.ds(g * (GT * D), GT * D)].rearrange("p (t o) -> p t o", t=GT),
                                      xh[:, :, D:2 * D], 0.0, None, ALU.add))
                st.wait()
                dve.sem_inc(s_mmu, 1)
                for j in range(GT):
                    dve.wait_ge(s_mm, g * (1 + GT) + n_mm + 2 + j)
                    dve.sem_inc(tick, 1)
                    st.do(V.tensor_tensor(prod[:, :].rearrange("p (b o) -> p b o", b=NB),
                                          bank[3 + j % 2][:, :].rearrange("p (b o) -> p b o", b=NB),
                                          relg[:, j, 0:NB].unsqueeze(2).to_broadcast([P, NB, D]), ALU.mult))
                    st.wait()
                    dve.sem_inc(s_mmu, 1)
                    st.do(V.tensor_reduce(pr2[:, j * D:(j + 1) * D],
                                          prod[:, :].rearrange("p (b o) -> p o b", b=NB), AX.X, ALU.add))
                    st.wait()
                dve.sem_inc(tick, 1)
                st.seq(V.tensor_scalar(Y[:, bass.ds(g * (GT * D), GT * D)], pr2[:, :], 0.0, None, ALU.add))
            st.do(V.memset(tl[:, 0:1], 0.0))
            st.wait()
            dve.sem_inc(s_ei, 1)
            dve.wait_ge(s_eo, 2)
            st.seq(V.tensor_tensor(Y3, Y3, bc3(t1[:, :], D), ALU.mult))
            st.seq(V.tensor_scalar(RB[:, 0:T * D], S[:, :], 0.0, None, ALU.add))
            segment_sums(Y3, S3, D, dmask, dfirst)
            st.seq(V.tensor_tensor(S[:, :], S[:, :], RB[:, 0:T * D], ALU.add))
            st.seq(V.tensor_scalar(S[:, :], S[:, :], 0.0, None, ALU.max))
            dve.sem_inc(s_tab, 1)
            stepped_ring_pass(PASS_RGCN, fill_idx(gin), add_take(XS), 1)
            layernorm(XS3, Y3)
            st.seq(V.tensor_tensor(XD[:, :], XD[:, :], S[:, :], ALU.add))
            layernorm(XD3, Y3)
            st.seq(V.tensor_tensor(Y3, XS3, bc3(ew[:, :], D), ALU.mult))
            dve.wait_ge(s_tabw, 16 * (K_STEPS + 2))
            segment_sums(Y3, S3, D, dmask, dfirst)
            st.seq(V.scalar_tensor_tensor(out=XD[:, :], in0=XD[:, :], scalar=2.0, in1=S[:, :], op0=ALU.mult,
                                          op1=ALU.add))
            layernorm(XD3, Y3)
            st.seq(V.tensor_scalar(XS[:, :], XS[:, :], 2.0, None, ALU.mult))
            layernorm(XS3, Y3)

            def out_fill(rows, idx):
                def fill(i, h):
                    V.tensor_scalar(slot(h), cols(rows, i, h, D), 0.0, None, ALU.add)
                    return V.tensor_scalar(ridx[:, h, :], cols(idx, i, h), 0.0, None, ALU.add)
                return fill

            stepped_ring_pass(PASS_OUT_DST, out_fill(XD, odi), lambda i, h: None, 0)
            stepped_ring_pass(PASS_OUT_SRC, out_fill(XS, osi), lambda i, h: None, 0)

        @block.scalar
        def _(act):
            A = nc.scalar
            tick = s_tick[1]

            def act_pass(n, idx, dest, w):
                ring_pass(act, tick, n,
                          lambda i, h: A.activation(ridx[:, h, :], cols(idx, i, h), ACT.Copy),
                          lambda i, h: A.activation(cols(dest, i, h, w), ring[:, h, 0:U * w], ACT.Copy))

            act.wait_ge(s_ids, 1)
            act_pass(PASS_X_SRC, xsi, XS, D)
            with act.Fori(0, NG) as i:
                for j in range(4):
                    act.wait_ge(s_ohT, i * 4 + j + 1)
                    act.sem_inc(tick, 1)
                    A.activation(ohaT[:, j, :], bank[2 + j % 2][:, :].bitcast(F16)[:, 0:AW], ACT.Copy).then_inc(s_ohTc, 1)
                act.wait_ge(s_ru, i + 1)
                act.sem_inc(tick, 1)
                for b in range(2):
                    last = A.activation(rhi[:, 2 * b:2 * b + 2, :].rearrange("p c n -> p (c n)"), bank[b][:, :], ACT.Copy)
                last.then_inc(s_rhi, 1)
            act_pass(PASS_NT_SRC, srci, S[:, 0:4 * T], 4)
            act_pass(PASS_NT_DST, dsti, S[:, 4 * T:8 * T], 4)
            act.wait_ge(s_sri, 1)
            A.activation(t1[:, :], t1[:, :], ACT.Sqrt)
            A.activation(t2[:, :], t2[:, :], ACT.Sqrt)
            A.activation(c3[:, :], c3[:, :], ACT.Sqrt).then_inc(s_sro, 1)
            with act.Fori(0, CH) as c:
                for r in range(4):
                    act.wait_ge(s_nri, c * 4 + r + 1)
                    act.sem_inc(tick, 1)
                    A.activation(nr2[0:NODE_P, :], nr1[0:NODE_P, :], ACT.Sqrt, bias=eps_c[0:NODE_P, 0:1]).then_inc(s_nro, 1)
            n = 0

            def norm(t, sq):
                nonlocal n
                n += 1
                act.wait_ge(s_sqi, n)
                A.activation(sq, t, ACT.Square).then_inc(s_sqo, 1)
                act.wait_ge(s_sri, n + 1)
                A.activation(t1[:, :], t1[:, :], ACT.Sqrt, scale=1.0 / D, bias=eps_c[:, 0:1]).then_inc(s_sro, 1)

            norm(XS[:, :], Y[:, :])
            norm(XD[:, :], Y[:, :])

            def transposed(sources, done):
                for k, source in enumerate(sources):
                    last = A.activation(xg[:, k, :].rearrange("p (t d) -> p t d", d=D), source, ACT.Copy)
                last.then_inc(s_stg, 1)
                which = len(sources)
                act.wait_ge(s_xtp, done)
                act.sem_inc(tick, 1)
                ins = A.activation(xt[:, 0, 0:P], bank[0][:, 0:P], ACT.Copy)
                if which == 2:
                    ins = A.activation(xt_y[:, 0, :], bank[1][:, 0:P], ACT.Copy)
                ins.then_inc(s_xtc, 1)

            edges_g = lambda t3_, g: t3_[:, bass.ds(g * GT, GT), 0:D]
            act.wait_ge(s_grp, 1)
            with act.Fori(0, NG) as g:
                transposed((edges_g(XS3, g), edges_g(XD3, g)), g + 1)
            act.wait_ge(s_ei, 1)
            A.activation(z4t[:, :], z4t[:, :], ACT.Exp).then_inc(s_eo, 1)
            act.wait_ge(s_grp, 2)
            with act.Fori(0, NG) as g:
                transposed((edges_g(ROWS3, g),), g + NG + 1)
            for t in (XS, XD):
                norm(t[:, :], Y[:, :])
            act.wait_ge(s_grp, 3)
            with act.Fori(0, NG) as g:
                transposed((edges_g(XS3, g), edges_g(XD3, g)), g + 2 * NG + 1)
            act.wait_ge(s_ei, 2)
            A.activation(t1[:, :], t1[:, :], ACT.Tanh).then_inc(s_eo, 1)
            for t in (XS, XD, XD, XS):
                norm(t[:, :], Y[:, :])

        @block.tensor
        def _(pe):
            M = nc.tensor
            tick = s_tick[3]
            pe.wait_ge(s_cst2, 1)
            for c in range(NA_CH):
                last = M.matmul(bank[c][:, :], ident_h[:, :], zh[:, :], start=True, stop=False)
            last.then_inc(s_ohu, 4)
            with pe.Fori(0, NG) as i:
                for j in range(4):
                    pe.wait_ge(s_oh, i * 4 + j + 1)
                    pe.sem_inc(tick, 1)
                    for c in range(NA_CH):
                        M.matmul(bank[c][:, 0:NB_COL], oha[:, j, c * P:(c + 1) * P], ohb[:, j, :], start=False, stop=False)
                        last = M.matmul(bank[c][:, NB_COL:2 * NB_COL], oha2[:, j, c * P:(c + 1) * P], ohb2[:, j, :],
                                        start=False, stop=False)
                    last.then_inc(s_ohu, 1)
            for c in range(NA_CH):
                last = M.matmul(bank[c][:, :], ident_h[:, :], zh[:, :], start=False, stop=True)
            last.then_inc(s_hist, 1)
            pe.wait_ge(s_tot, 1)
            tk = tot[:, :, :].rearrange("p k c -> p (k c)")
            M.matmul(bank[4][:, 0:2 * NA_CH], up[:, :], tk, start=True, stop=True)
            M.matmul(bank[5][:, 0:2 * NA_CH], ones[:, :], tk, start=True, stop=True).then_inc(s_base, 1)

            pe.wait_ge(s_nt, 1)
            for b in range(2):
                last = M.matmul(bank[b][:, :], ident_h[:, :], zh[:, :], start=True, stop=True, skip_group_check=True)
            last.then_inc(s_gu, 1)
            chunk = lambda c: bank[c // 2][:, (c % 2) * NB_COL:(c % 2 + 1) * NB_COL]
            with pe.Fori(0, NG) as i:
                pe.wait_ge(s_oh, i + T + 1)
                pe.sem_inc(tick, 1)
                for j in range(4):
                    if j >= 2:
                        pe.wait_ge(s_ohTc, i * 4 + j - 1)
                        pe.sem_inc(tick, 1)
                    for c in range(NA_CH):
                        last = M.transpose(bank[2 + j % 2][:, :].bitcast(F16)[:, c * P:(c + 1) * P],
                                           oha[:, j, c * P:(c + 1) * P], ident_h[:, :])
                    last.then_inc(s_ohT, 1)
                for j in range(4):
                    last = M.transpose(bank[4][:, j * P:(j + 1) * P], kcol[:, j:j + 1].to_broadcast([P, P]),
                                       ident[:, :])
                last.then_inc(s_kt, 1)
                pe.wait_ge(s_ohTc, i * 4 + 4)
                pe.sem_inc(tick, 1)
                for j in range(4):
                    g = bank[5 + j // 2][:, (j % 2) * NB_COL:(j % 2 + 1) * NB_COL]
                    for c in range(NA_CH):
                        for m, part in enumerate((rhi, rlo)):
                            last = M.matmul(g, ohaT[:, j, c * P:(c + 1) * P], part[:, c, :], start=c == 0 and m == 0,
                                            stop=c == NA_CH - 1 and m == 1)
                last.then_inc(s_g, 1)
                for j in range(4):
                    for c in range(NA_CH):
                        last = M.matmul(chunk(c), oha[:, j, c * P:(c + 1) * P], ohb[:, j, :], start=False,
                                        stop=j == 3, skip_group_check=True)
                last.then_inc(s_ru, 1)
                pe.wait_ge(s_rc, i + 1)
                pe.sem_inc(s_gu, 1)
            def key_rows(n):
                pe.wait_ge(s_trw, n)
                M.transpose(bank[4][:, 0:P], tl[:, 0:1].to_broadcast([P, P]), ident[:, :])
                M.transpose(bank[5][:, 0:P], tl[:, 1:2].to_broadcast([P, P]), ident[:, :]).then_inc(s_tr, 1)

            def carry(link, width, n):
                pe.wait_ge(s_tail, n)
                M.matmul(bank[7][:, 0:width], link[:, :], tl[:, 0:width], start=True, stop=True).then_inc(s_carry, 1)

            key_rows(1)
            carry(dcar, D, 1)
            with pe.Fori(0, K_STEPS - 1) as k:
                pe.wait_ge(s_tail, k + 2)
                pe.sem_inc(tick, 1)
                M.matmul(bank[7][:, 0:D], dcar[:, :], tl[:, :], start=True, stop=True).then_inc(s_carry, 1)
            carry(dbak, D, K_STEPS + 1)

            pe.wait_ge(s_wb, 1)
            pe.wait_ge(s_grp, 1)
            with pe.Fori(0, NG) as g:
                pe.wait_ge(s_mmu, g + 1)
                pe.wait_ge(s_stg, g + 1)
                pe.sem_inc(tick, 1)
                M.transpose(bank[0][:, 0:P], xg[:, 0, :], ident[:, :])
                M.transpose(bank[1][:, 0:P], xg[:, 1, :], ident[:, :]).then_inc(s_xtp, 1)
                pe.wait_ge(s_xtc, g + 1)
                pe.sem_inc(tick, 1)
                M.matmul(bank[6][:, 0:GT * NH], xt[:, 0, 0:P], bdu[:, 0, :], start=True, stop=False)
                M.matmul(bank[6][:, 0:GT * NH], xt_y[:, 0, :], bdu[:, 1, :], start=False, stop=True).then_inc(s_mm, 1)

            key_rows(2)
            pe.wait_ge(s_trw, 3)
            for h in range(NH):
                last = M.transpose(bank[4][:, h * P:(h + 1) * P], tl[:, h:h + 1].to_broadcast([P, P]), ident[:, :])
            last.then_inc(s_tr, 1)
            carry(sbak, NH, K_STEPS + 2)
            carry(scar, NH, K_STEPS + 3)
            carry(sbak, NH, K_STEPS + 4)
            pe.wait_ge(s_grp, 2)
            with pe.Fori(0, NG) as g:
                pe.wait_ge(s_mmu, g + NG + 1)
                pe.wait_ge(s_stg, g + NG + 1)
                pe.sem_inc(tick, 1)
                M.transpose(bank[0][:, 0:P], xg[:, 0, :], ident[:, :]).then_inc(s_xtp, 1)
                pe.wait_ge(s_xtc, g + NG + 1)
                pe.sem_inc(tick, 1)
                M.matmul(bank[6][:, :], xt[:, 0, 0:P], bd1[:, :], start=True, stop=True).then_inc(s_mm, 1)
            carry(scar, D, K_STEPS + 5)

            pe.wait_ge(s_grp, 3)
            u0 = 2 * NG
            with pe.Fori(0, NG) as g:
                pe.wait_ge(s_mmu, g * (1 + GT) + u0 + 1)
                pe.wait_ge(s_stg, g + 2 * NG + 1)
                pe.sem_inc(tick, 1)
                M.transpose(bank[0][:, 0:P], xg[:, 0, :], ident[:, :])
                M.transpose(bank[1][:, 0:P], xg[:, 1, :], ident[:, :]).then_inc(s_xtp, 1)
                pe.wait_ge(s_xtc, g + 2 * NG + 1)
                pe.sem_inc(tick, 1)
                M.matmul(bank[6][:, 0:GT * 2 * D], xt[:, 0, 0:P], bdx[:, :], start=True, stop=True)
                M.matmul(bank[5][:, 0:GT * D], xt_y[:, 0, :], bdy[:, :], start=True, stop=True).then_inc(s_mm, 1)
                for j in range(GT):
                    if j >= 2:
                        pe.wait_ge(s_mmu, g * (1 + GT) + u0 + j + 1)
                        pe.sem_inc(tick, 1)
                    M.matmul(bank[3 + j % 2][:, :], xt[:, 0, 0:P], bw[:, j, :], start=True, stop=True).then_inc(s_mm, 1)
            carry(dcar, D, K_STEPS + 6)
            carry(dcar, D, K_STEPS + 7)


_INS = ['x', 'src', 'dst', 'edge_type_86', 'edge_weight', 'L1_gnn_w', 'L1_gnn_fc_w', 'L1_gnn_fc_b', 'L1_gnn_bias',
        'L2_gnn_weight', 'L2_gnn_w_comp', 'L2_gnn_self_loop_weight', 'L2_gnn_A1_w', 'L2_gnn_A1_b', 'L2_gnn_A2_w',
        'L2_gnn_A2_b', 'L2_gnn_rel_emb']
_OUTS = [((100000, 32), 'float32')]


def kernel(**inputs):
    import numpy as _np
    import concourse.bacc as _bacc
    from concourse import mybir as _mybir
    from concourse.bass_utils import run_bass_kernel_spmd as _run

    nc = _bacc.Bacc("TRN2", target_bir_lowering=False, num_devices=1)
    arrays, args = {}, []
    for name in _INS:
        a = _np.ascontiguousarray(inputs[name])
        arrays[f"in_{name}_dram"] = a
        args.append(nc.dram_tensor(f"in_{name}_dram", a.shape, _mybir.dt.from_np(a.dtype), kind="ExternalInput").ap())
    for i, (shape, dtype) in enumerate(_OUTS):
        dt = _mybir.dt.from_np(_np.dtype(dtype))
        args.append(nc.dram_tensor(f"out_{i}_dram", shape, dt, kind="ExternalOutput").ap())
    gnn_resnorm(nc, *args)
    r = _run(nc, [arrays], core_ids=[0])
    return r.results[0]["out_0_dram"]
```

```python
from contextlib import ExitStack, contextmanager

import concourse.bass as bass
from concourse import mybir

ALU = mybir.AluOpType
ACT = mybir.ActivationFunctionType
AX = mybir.AxisListType
F32 = mybir.dt.float32
F16 = mybir.dt.float16
I32 = mybir.dt.int32

P = 128
BIG = 1.0e30
EPS = 1e-5


class Steps:

    def __init__(self, eng, sem, trips=None):
        self.eng, self.sem, self.n, self.off, self.trips, self.dyn = eng, sem, 0, None, trips, 0

    def plus(self, a, b):
        return b if a is None else a + b

    def do(self, ins):
        ins.then_inc(self.sem, 1)
        self.n += 1

    def wait(self, behind=0):
        v = self.off
        if self.dyn:
            v = self.plus(v, self.trips * self.dyn)
        self.eng.wait_ge(self.sem, self.plus(v, self.n - behind))

    def seq(self, ins):
        self.do(ins)
        self.wait()

    @contextmanager
    def loop(self, count, per, dyn=0):
        start, dstart, outer = self.n, self.dyn, self.off
        with self.eng.Fori(0, count) as i:
            self.off = self.plus(outer, i * per if not dyn else i * self.trips * dyn + i * per)
            yield i
            assert (self.n - start, self.dyn - dstart) == (per, dyn), f"a round has {self.n - start}, {self.dyn - dstart}"
            self.off = outer
        self.n, self.dyn = start + per * count, dstart + dyn * count

    @contextmanager
    def trip_loop(self, per):
        start, outer = self.n, self.off
        with self.eng.Fori(0, self.trips) as i:
            self.off = self.plus(outer, i * per)
            yield i
            assert self.n - start == per, f"a round has {self.n - start} steps"
            self.off = outer
        self.n, self.dyn = start, self.dyn + per


def gnn_resnorm(nc, x, src, dst, etype, eweight, w1, fc_w, fc_b, bias1, w2, w_comp, w_self, A1w, A1b, A2w, A2b,
                rel_emb, out):
    N, D = x.shape
    E = src.shape[0]
    T = -(-E // P)
    EP = P * T
    LASTV = E - (P - 1) * T
    NH = w1.shape[0]
    NB = w2.shape[0]
    NR = w_comp.shape[0]
    NB_COL = 256
    NA_CH = -(-(N + 1) // (NB_COL * P))
    NT_ROWS = NA_CH * P * NB_COL
    CU = 4
    CW = 200
    LW = CW + 2 * CU
    TW = D + 4
    ZERO_DMAS = 11
    ZROW = P * CW
    U = 14
    ROUNDS = T // (2 * U)
    LAND = 16 * U
    RW = 48
    ROW1 = 40
    K_STEPS = 10
    ALPHA = 0.1
    OOB = 2 * N
    NODE_P = 125
    NROWS = N // NODE_P
    CH = 20
    CR = NROWS // CH
    GT = 4
    NG = T // GT
    assert T % (2 * U) == 0 and T % GT == 0 and D == 32 and NROWS % CH == 0 and NG % 2 == 1

    ctx = ExitStack()
    with ctx:
        sb = lambda name, shape, dt=F32: ctx.enter_context(nc.sbuf_tensor(name, shape, dt))
        sem = lambda name: ctx.enter_context(nc.semaphore(name))

        nt_d = nc.dram_tensor("node_table", (NT_ROWS, 4), F32).ap()
        agg_d = nc.dram_tensor("appnp_table", (ZROW + 1, D), F32).ap()
        att_d = nc.dram_tensor("attention_table", (ZROW + 1, D), F32).ap()
        rgcn_d = nc.dram_tensor("rgcn_table", (ZROW + 1, D), F32).ap()
        full_d = nc.dram_tensor("sums_by_edge", (ZROW + 1, TW), F32).ap()
        list_d = [nc.dram_tensor("sums_by_list0", (ZROW + 1, TW), F32).ap(),
                  nc.dram_tensor("sums_by_list1", (ZROW + 1, D), F32).ap()]
        pay_d = [nc.dram_tensor(f"payload{v}", (ZROW + 1, 4), F32).ap() for v in range(2)]
        exp_d = [nc.dram_tensor(f"list{v}_values_by_edge", (EP, D), F32).ap() for v in range(2)]
        rel_d = nc.dram_tensor("relation_table", (NR, RW), F32).ap()
        row_d = nc.dram_tensor("rows_by_src", (EP, ROW1), F32).ap()

        bank = [ctx.enter_context(nc.psum_tensor(f"bank{i}", [P, 512], F32)) for i in range(8)]

        XS = sb("XS", [P, T * D])
        XDW, YW, SW = sb("XDW", [P, CW * D]), sb("YW", [P, CW * D]), sb("SW", [P, CW * D])
        XD, Y, S = XDW[:, 0:T * D], YW[:, 0:T * D], SW[:, 0:T * D]
        RB = sb("RB", [P, T * RW])
        RC0 = 2 * U
        v3 = lambda t, w=D: t.rearrange("p (t d) -> p t d", d=w)
        XS3, XD3, Y3, S3 = v3(XS[:, :]), v3(XD[:, :]), v3(Y[:, :]), v3(S[:, :])
        REL3 = v3(RB[:, :], RW)
        ROWS = RB[:, 0:T * ROW1]
        ROWS3 = v3(ROWS, ROW1)
        ring = sb("ring", [P, 2, U * RW])
        ridx = sb("ridx", [P, 2, U], I32)

        e_i = lambda name: sb(name, [P, T], I32)
        e_f = lambda name: sb(name, [P, T], F32)
        srci, dsti, etyi = e_i("srci"), e_i("dsti"), e_i("etyi")
        ew = e_f("ew")
        srcf, dstf = e_f("srcf"), e_f("dstf")
        tmpi = e_i("tmpi")
        a_s, b_s, a_d, b_d = e_f("a_s"), e_f("b_s"), e_f("a_d"), e_f("b_d")
        xsi, xdi = e_i("xsi"), e_i("xdi")
        gin, gout_s, gout_d, posi = e_i("gin"), e_i("gout_s"), e_i("gout_d"), e_i("posi")
        osi, odi = xsi, xdi
        c1, c2, c3, ginf = e_f("c1"), e_f("c2"), e_f("c3"), b_s
        t1w = sb("t1w", [P, CW])[:, :]
        posf = e_f("posf")
        q_f = e_f("q_f")
        dmask, dfirst, dend = e_f("dmask"), e_f("dfirst"), e_f("dend")
        smask, sfirst, send, ks = a_s, b_s, a_d, b_d
        t1, t2, t3 = e_f("t1"), e_f("t2"), e_f("t3")

        S16 = S.bitcast(F16).rearrange("p (t k d) -> p t k d", k=2, d=D)

        iota_h = sb("iota_h", [P, NA_CH * P], F16)
        ident = sb("ident", [P, P])
        ident_h = sb("ident_h", [P, P], F16)
        up = sb("up", [P, P])
        low = sb("low", [P, P])
        ones = sb("ones", [P, P])
        dcar, dbak = sb("dcar", [P, P]), sb("dbak", [P, P])
        scar, sbak = sb("scar", [P, P]), sb("sbak", [P, P])
        sneg = sb("sneg", [P, P])
        zrow = sb("zrow", [P, TW])
        ROOTS = {"norm": (1.0, EPS), "first": (1.0, EPS / (1 + ALPHA) ** 2), "all": (1 + EPS * (1 + EPS) / 4, EPS ** 3 / 4)}
        eps_t = {kind: sb(f"eps_{kind}", [P, 1]) for kind in ROOTS}

        AW = NA_CH * P
        halves, at = XD.bitcast(F16), 0

        def half(n):
            nonlocal at
            at += 4 * n
            return halves[:, at - 4 * n:at].rearrange("p (j n) -> p j n", j=4)

        oha, ohb, oha2, ohb2 = half(AW), half(NB_COL), half(AW), half(NB_COL)
        junk = XD[:, at // 2:at // 2 + 10 * P + 4 * NB_COL]
        emask = XD[:, at // 2 + junk.shape[1]:at // 2 + junk.shape[1] + 4 * P]
        assert at // 2 + junk.shape[1] + 4 * P <= T * D
        halves, at = SW[:, :].bitcast(F16), 16 * T
        ohaT, rhi, rlo = [half(AW), half(AW)], [half(NB_COL), half(NB_COL)], [half(NB_COL), half(NB_COL)]
        assert at <= 2 * CW * D
        ohas, ohbs = (oha, oha2), (ohb, ohb2)
        zh = sb("zh", [P, 512], F16)
        cnt4 = sb("cnt4", [P, 4])
        rk4 = sb("rk4", [P, 4])
        kcol = sb("kcol", [P, 2, 4])
        z4w, e4w = sb("z4w", [P, CW * 4]), sb("e4w", [P, CW * 4])
        PAY = [z4w, e4w]
        Z0 = RB[:, 0:CW * TW].rearrange("p (j w) -> p j w", w=TW)
        FULL = RB[:, 0:T * TW].rearrange("p (j w) -> p j w", w=TW)
        lists = RB[:, CW * TW:CW * TW + 10 * LW].rearrange("p (k j) -> p k j", k=10)
        assert CW * TW + 10 * LW <= T * RW
        lkey, lval, lmask, lfirst, lnext, lact, lcnt = (lists[:, k, :] for k in range(7))
        lidx, lidx2, lq = (lists[:, k, :].bitcast(I32) for k in range(7, 10))
        cring = sb("cring", [P, 2, CU * TW])
        cidx = sb("cidx", [P, 2, CU], I32)
        y4 = sb("y4", [P, CU, D])
        zr = sb("zr", [P, CU + 1, D])
        oring, oidx = (z4w[:, 0:U * D], e4w[:, 0:U * D]), sb("oidx", [P, 2, U], I32)
        rr = c1
        vs, rs = sb("vs", [P, RC0]), sb("rs", [P, RC0])
        m8 = sb("m8", [P, 8])
        ramp_c = sb("ramp_c", [P, LW])
        tm = sb("tm", [P, 1])
        pb = sb("pb", [P, 2])
        trips_i = [sb(f"trips{v}", [P, 1], I32) for v in range(2)]
        zrow4 = sb("zrow4", [1, 4])
        dneg = sb("dneg", [P, P])
        tot = sb("tot", [P, 2, NA_CH])
        base = sb("base", [P, 2, NA_CH])
        TB = NA_CH * NB_COL
        HC, IC = Y[:, 0:2 * TB], Y[:, 2 * TB:4 * TB]
        NTB = RB[:, 0:4 * TB]
        z4t, e4t = z4w[:, 0:T * NH], e4w[:, 0:T * NH]
        z43, e43 = v3(z4t[:, :], NH), v3(e4t[:, :], NH)
        NS3, ND3 = v3(S[:, 0:4 * T], 4), v3(S[:, 4 * T:8 * T], 4)

        wcat = sb("wcat", [P, NH * D])
        wsd = sb("wsd", [P, 2 * D])
        ua = sb("ua", [P, 2, NH])
        udiag = sb("udiag", [D, 2 * NH * D])
        bd1 = sb("bd1", [P, GT * NH * D])
        bdy = sb("bdy", [P, GT * D])
        wf = sb("wf", [P, NB * D])
        w16 = sb("w16", [P, (NB + 2) * D], F16)
        aw = sb("aw", [P, 3 * D])
        b_bias, b_b1, b_b2 = sb("b_bias", [P, D]), sb("b_b1", [P, D]), sb("b_b2", [P, D])
        b_fcb = sb("b_fcb", [P, 1])
        bc = sb("bc", [P, D])
        bm = sb("bm", [P, 1])
        xt = sb("xt", [P, 2, P])
        x16 = sb("x16", [P, 2, GT * P], F16)
        xs16 = sb("xs16", [P, 2, GT * P], F16)
        xg = sb("xg", [P, 2, P])
        prods = sb("prods", [P, 2, 512])
        prod = prods[:, 0, :]
        pr2, pq2, sc4 = sb("pr2", [P, GT * D]), sb("pq2", [P, GT * D]), sb("sc4", [P, GT])
        car = sb("car", [P, D])
        tl = sb("tl", [P, D])

        RC = 2 * U
        sq_s = RB[:, 0:2 * RC * D]
        lp_s = RB[:, 2 * RC * D:(2 + NH) * RC * D]
        roots = sb("roots", [P, 2 * RC])
        u_all = sb("u_all", [P, 2 * NH * D])

        nx, nsq = sb("nx", [P, CR * D])[:, :], RB[:, 0:CR * D]
        nr1 = roots[:, 0:CR]
        nx3, nsq3 = v3(nx), v3(nsq)

        s_pad = sem("padding_set")
        s_in = sem("edges_loaded")
        s_w = sem("weights_loaded")
        s_bd = sem("basis_weights_loaded")
        s_relt = sem("relation_table_written")
        s_zr = sem("zero_row_set")
        s_ztab = sem("zero_rows_written")
        s_const = sem("pool_constants_ready")
        s_cst2 = sem("masks_ready")
        s_ids = sem("node_indices_ready")
        s_slot = sem("ring_slot_ready")
        s_land = [[sem(f"landed{f}{h}") for h in range(2)] for f in range(2)]
        s_tick = [sem(f"tick_{e}") for e in ("pool", "act", "dve", "pe", "sp")]
        s_oh = sem("onehots_ready")
        s_ohu = sem("onehots_used")
        s_hist = sem("histogram_done")
        s_tot = sem("totals_ready")
        s_base = sem("bases_ready")
        s_nt = sem("node_table_ready")
        s_ntw = sem("node_table_written")
        s_actp = sem("act_passes_done")
        s_dve = sem("dve_steps")
        s_ohT = sem("onehots_transposed")
        s_ohTc = sem("transposed_copied")
        s_kt = sem("keys_transposed")
        s_g = sem("counts_gathered")
        s_eq = sem("keys_compared")
        s_gu = sem("counts_read")
        s_ru = sem("running_counts_updated")
        s_rhi = sem("high_parts_ready")
        s_rc = sem("low_parts_ready")
        s_tr = sem("row_of_keys_ready")
        s_trw = sem("row_of_keys_wanted")
        s_tail = sem("tails_ready")
        s_carry = sem("carries_ready")
        s_tab = sem("table_tile_ready")
        s_tabw = sem("table_written")
        s_sri = sem("degrees_ready")
        s_sro = sem("degree_roots_ready")
        s_ri = sem("root_wanted")
        s_nin = sem("node_chunk_loaded")
        s_nok = sem("node_chunk_done")
        s_nout = sem("node_chunk_written")
        s_grp = sem("group_source_ready")
        s_mm = sem("attention_vectors_ready")
        s_row = sem("src_rows_loaded")
        s_sct = sem("rows_scattered")
        s_wb = sem("blocks_built")
        s_ei = sem("exponentials_wanted")
        s_eo = sem("exponentials_ready")
        s_lslot = [sem(f"list{v}_slot_ready") for v in range(2)]
        s_lland = [[sem(f"list{v}_landed{h}") for h in range(2)] for v in range(2)]
        s_lst = [sem(f"list{v}_steps") for v in range(2)]
        s_trips = [sem(f"trips{v}_ready") for v in range(2)]
        s_ltab = [sem(f"list{v}_sums_ready") for v in range(2)]
        s_ltabw = [sem(f"list{v}_sums_written") for v in range(2)]
        s_pay = [sem(f"payload{v}_ready") for v in range(2)]
        s_payw = [sem(f"payload{v}_written") for v in range(2)]
        s_oslot, s_oland = sem("out_src_slot_ready"), [sem(f"out_src_written{b}") for b in range(2)]
        s_full = sem("sums_by_edge_ready")
        s_fullw = sem("sums_by_edge_written")
        s_expz = sem("zeros_ready")
        s_expzw = sem("zeros_written")
        s_exp = sem("list_values_scattered")
        s_expl = sem("list_values_loaded")
        s_stg = [sem(f"group_staged{k}") for k in range(2)]
        s_xtp = [sem(f"group_transposed{k}") for k in range(2)]
        s_xtc = [sem(f"transposed_group_copied{k}") for k in range(2)]
        s_hp, s_hpu = sem("head_products_ready"), sem("head_products_used")
        s_xy, s_xyu = sem("relation_terms_ready"), sem("relation_terms_used")
        s_self = sem("self_loop_terms_copied")
        s_msg, s_msgu = sem("basis_products_ready"), sem("basis_products_used")

        NODE_STEPS = 14
        block = ctx.enter_context(nc.Block())
        edges = lambda a: a[0:(P - 1) * T].rearrange("(p t) -> p t", t=T)
        edges_last = lambda a: a[(P - 1) * T:E].rearrange("(p t) -> p t", p=1)
        dense = lambda a, w: a[0:EP, :].rearrange("(p t) d -> p (t d)", t=T)

        PASS_X_SRC, PASS_NT_SRC, PASS_NT_DST, PASS_L0 = range(4)
        PASS_X_DST = PASS_L0 + 1
        PASS_ROW, PASS_ATT_SRC, PASS_ATT_DST, PASS_REL, PASS_RGCN, PASS_OUT_DST = \
            range(PASS_X_DST + 1, PASS_X_DST + 7)

        def family(n):
            return (0, n) if n < PASS_ROW else (1, n - PASS_ROW)

        def slot_count(n, i, h):
            return 2 * ROUNDS * n + 2 * i + h + 1

        def land_count(n, i):
            return LAND * (ROUNDS * family(n)[1] + i + 1)

        def list_slot_count(a, b, n):
            return n * 2 * a + 2 * b + 1 if isinstance(a, int) and a else (2 * b + 1 if isinstance(a, int) else
                                                                            n * a * 2 + b * 2 + 1)

        def list_dma(pool, v, n, a, b, w, table, scatter=False):
            with pool.Fori(0, n) as i:
                for h in range(2):
                    pool.wait_ge(s_lslot[v], i * 2 + (list_slot_count(a, b, n) + h))
                    pool.sem_inc(s_tick[0], 1)
                    for j in range(CU):
                        off = bass.IndirectOffsetOnAxis(ap=cidx[:, h, j:j + 1], axis=0)
                        row = cring[:, h, j * w:(j + 1) * w]
                        if scatter:
                            pool.indirect_dma_start(out=table, out_offset=off, in_=row, in_offset=None,
                                                    bounds_check=EP - 1, oob_is_err=False).then_inc(s_lland[v][h], 16)
                        else:
                            pool.indirect_dma_start(out=row, out_offset=None, in_=table,
                                                    in_offset=off).then_inc(s_lland[v][h], 16)

        def ring_row(h, j, w):
            return ring[:, h, j * w:(j + 1) * w]

        def dma_pass(pool, n, w, table, scatter=False, limit=None, k=0, f=None, round_end=None):
            f = family(n)[0] if f is None else f
            with pool.Fori(0, ROUNDS) as i:
                for h in range(2):
                    pool.wait_ge(s_slot, i * 2 + k * (2 * ROUNDS) + slot_count(n, 0, h))
                    pool.sem_inc(s_tick[0], 1)
                    for j in range(U):
                        off = bass.IndirectOffsetOnAxis(ap=ridx[:, h, j:j + 1], axis=0)
                        if scatter:
                            pool.indirect_dma_start(out=table, out_offset=off, in_=ring_row(h, j, w), in_offset=None,
                                                    bounds_check=limit, oob_is_err=False).then_inc(s_land[f][h], 16)
                        else:
                            pool.indirect_dma_start(out=ring_row(h, j, w), out_offset=None, in_=table,
                                                    in_offset=off).then_inc(s_land[f][h], 16)
                if round_end:
                    round_end(i)

        def ring_pass(eng, tick, n, fill, take, k=0, f=None):
            f = family(n)[0] if f is None else f
            for h in range(2):
                fill(0, h).then_inc(s_slot, 1)
            with eng.Fori(0, ROUNDS - 1) as i:
                for h in range(2):
                    eng.wait_ge(s_land[f][h], i * LAND + k * (LAND * ROUNDS) + land_count(n, 0))
                    eng.sem_inc(tick, 1)
                    take(i, h)
                    fill(i + 1, h).then_inc(s_slot, 1)
            for h in range(2):
                eng.wait_ge(s_land[f][h], k * (LAND * ROUNDS) + land_count(n, ROUNDS - 1))
                eng.sem_inc(tick, 1)
                take(ROUNDS - 1, h).then_inc(s_actp, 1)

        RG, CREDIT = RC // GT, 2
        MSG0 = CREDIT * GT

        def done(g):
            return g + (CREDIT + 1)

        def free(g, j):
            return g + (CREDIT if j == 0 else CREDIT - 1)

        def groups(eng, body, round_end=None):
            with eng.Fori(0, ROUNDS - 1) as i:
                for j in range(RG):
                    body(i * RG + j, j, False)
                if round_end:
                    round_end(i)
            for j in range(RG):
                body((ROUNDS - 1) * RG + j, j, j == RG - 1)

        def cols(tile, i, h, w=1):
            return tile[:, bass.ds(i * (2 * U * w) + h * U * w, U * w)]

        @block.sync
        def _(sp):
            sp.wait_ge(s_pad, 1)
            for a, t in ((src, srci), (dst, dsti), (etype, etyi), (eweight, ew)):
                sp.dma_start(t[0:P - 1, :], edges(a)).then_inc(s_in, 16)
                sp.dma_start(t[P - 1:P, 0:LASTV], edges_last(a)).then_inc(s_in, 16)
            sp.dma_start(rel_d[:, 0:NB], w_comp).then_inc(s_relt, 16)
            sp.dma_start(rel_d[:, NB:NB + D], rel_emb).then_inc(s_relt, 16)
            for j in range(4):
                sp.dma_start(wcat[32 * j:32 * j + 32, :].rearrange("i (h o) -> i h o", h=NH),
                             w1.rearrange("h i o -> i h o")).then_inc(s_w, 16)
                with nc.allow_non_contiguous_dma(reason="transposed 32 x 32 weights"):
                    sp.dma_start(aw[32 * j:32 * j + 32, 0:D], A1w.rearrange("o i -> i o")).then_inc(s_w, 16)
                    sp.dma_start(aw[32 * j:32 * j + 32, D:2 * D], A2w.rearrange("o i -> i o")).then_inc(s_w, 16)
                sp.dma_start(aw[32 * j:32 * j + 32, 2 * D:3 * D], w_self).then_inc(s_w, 16)
            sp.dma_start(wsd[:, :], fc_w[0, :].partition_broadcast(P)).then_inc(s_w, 16)
            sp.dma_start(b_bias[:, :], bias1.partition_broadcast(P)).then_inc(s_w, 16)
            sp.dma_start(b_b1[:, :], A1b.partition_broadcast(P)).then_inc(s_w, 16)
            sp.dma_start(b_b2[:, :], A2b.partition_broadcast(P)).then_inc(s_w, 16)
            sp.dma_start(b_fcb[:, :], fc_b.partition_broadcast(P)).then_inc(s_w, 16)
            for j in range(4):
                sp.dma_start(wf[32 * j:32 * j + 32, :].rearrange("i (b o) -> i b o", b=NB),
                             w2.rearrange("b i o -> i b o")).then_inc(s_bd, 16)
            sp.wait_ge(s_zr, 1)
            for tab in (agg_d, att_d, rgcn_d, full_d, *list_d):
                sp.dma_start(tab[ZROW:ZROW + 1, :], zrow[0:1, 0:tab.shape[1]]).then_inc(s_ztab, 16)
            for tab in pay_d:
                sp.dma_start(tab[ZROW:ZROW + 1, :], zrow4[:, :]).then_inc(s_ztab, 16)
            sp.wait_ge(s_expz, 1)
            for tab in exp_d:
                sp.dma_start(dense(tab, D), Y).then_inc(s_expzw, 16)
            for tab in (agg_d, att_d, rgcn_d, full_d, pay_d[0]):
                gap = (ZROW - EP) * tab.shape[1] // P
                sp.dma_start(tab[EP:ZROW, :].rearrange("(p r) w -> p (r w)", p=P), YW[:, 0:gap]).then_inc(s_expzw, 16)
            for tab in list_d:
                flat = tab[0:ZROW, :].rearrange("(p j) w -> p (j w)", p=P)
                width = CW * tab.shape[1]
                for at_ in range(0, width, width // 2):
                    sp.dma_start(flat[:, at_:at_ + width // 2], YW[:, 0:width // 2]).then_inc(s_expzw, 16)
            sp.wait_ge(s_nt, 1)
            for c in range(NA_CH):
                sp.dma_start(nt_d[c * P * NB_COL:(c + 1) * P * NB_COL, :].rearrange("(p b) f -> p (b f)", p=P),
                             NTB[:, c * NB_COL * 4:(c + 1) * NB_COL * 4]).then_inc(s_ntw, 16)

            def node_chunk(c):
                rows = lambda a: a.rearrange("(p r) d -> p (r d)", p=NODE_P)[:, bass.ds(c * (CR * D), CR * D)]
                sp.dma_start(nx[0:NODE_P, :], rows(x)).then_inc(s_nin, 16)
                sp.wait_ge(s_nok, c + 1)
                sp.sem_inc(s_tick[4], 1)
                sp.dma_start(rows(out), nx[0:NODE_P, :]).then_inc(s_nout, 16)
                sp.wait_ge(s_nout, c * 16 + 16)
                sp.sem_inc(s_tick[4], 1)

            def write_table(tab, n, k=0):
                sp.wait_ge(s_tab, k + n)
                sp.sem_inc(s_tick[4], 1)
                sp.dma_start(dense(tab, D), S[:, :]).then_inc(s_tabw, 16)

            wide = lambda tab, w, n: tab[0:P * n, :].rearrange("(p j) w -> p (j w)", p=P)
            sp.wait_ge(s_pay[0], 1)
            sp.dma_start(wide(pay_d[0], 4, T), PAY[0][:, 0:T * 4]).then_inc(s_payw[0], 16)
            sp.wait_ge(s_full, 1)
            sp.dma_start(wide(full_d, TW, T), RB[:, 0:T * TW]).then_inc(s_fullw, 16)

            def write_list(v, n, tile, w, k=0):
                sp.wait_ge(s_ltab[v], k + 1)
                sp.sem_inc(s_tick[4], 1)
                rw = 2 * CU * w
                with sp.Fori(0, n) as i:
                    sp.dma_start(wide(list_d[v], w, CW)[:, bass.ds(i * rw, rw)],
                                 tile[:, bass.ds(i * rw, rw)]).then_inc(s_ltabw[v], 16)

            sp.wait_ge(s_trips[0], 1)
            n0 = sp.value_load(trips_i[0][0:1, 0:1], min_val=1, max_val=CW // (2 * CU))
            write_list(0, n0, RB, TW)
            sp.wait_ge(s_pay[1], 1)
            sp.dma_start(wide(pay_d[1], 4, CW), PAY[0][:, :]).then_inc(s_payw[1], 16)
            sp.wait_ge(s_trips[1], 1)
            n1 = sp.value_load(trips_i[1][0:1, 0:1], min_val=1, max_val=CW // (2 * CU))
            with sp.Fori(0, K_STEPS - 3) as k:
                write_list(1, n1, SW, D, k)
            sp.wait_ge(s_exp, 1)
            sp.dma_start(S, dense(exp_d[0], D)).then_inc(s_expl, 16)
            sp.dma_start(XD, dense(exp_d[1], D)).then_inc(s_expl, 16)
            write_table(agg_d, 1)
            with sp.Fori(0, ROUNDS) as c:
                node_chunk(c)
            sp.wait_ge(s_sct, 1)
            sp.dma_start(ROWS, dense(row_d, ROW1)).then_inc(s_row, 16)
            write_table(att_d, 2)
            with sp.Fori(0, CH - ROUNDS) as c:
                node_chunk(c + ROUNDS)
            write_table(rgcn_d, 3)

        @block.gpsimd
        def _(pool):
            pool.memset(ident[:, :], 0.0).then_inc(s_const, 1)
            pool.memset(ones[:, :], 1.0).then_inc(s_const, 1)
            pool.memset(up[:, :], 1.0).then_inc(s_const, 1)
            pool.memset(low[:, :], 1.0).then_inc(s_const, 1)
            pool.iota(q_f[:, :], pattern=[[1, T]], base=0, channel_multiplier=T,
                      allow_small_or_imprecise_dtypes=True).then_inc(s_const, 1)
            pool.iota(iota_h[:, :], pattern=[[1, NA_CH * P]], base=0, channel_multiplier=0,
                      allow_small_or_imprecise_dtypes=True).then_inc(s_const, 1)
            pool.wait_ge(s_const, 6)
            pool.affine_select(out=ident[:, :], in_=ident[:, :], compare_op=ALU.not_equal, fill=1.0, base=0,
                               pattern=[[-1, P]], channel_multiplier=1).then_inc(s_const, 1)
            pool.affine_select(out=up[:, :], in_=up[:, :], compare_op=ALU.is_gt, fill=0.0, base=0,
                               pattern=[[1, P]], channel_multiplier=-1).then_inc(s_const, 1)
            pool.affine_select(out=low[:, :], in_=low[:, :], compare_op=ALU.is_gt, fill=0.0, base=0,
                               pattern=[[-1, P]], channel_multiplier=1).then_inc(s_const, 1)
            pool.iota(ramp_c[:, :], pattern=[[-1, LW]], base=CW, channel_multiplier=0,
                      allow_small_or_imprecise_dtypes=True).then_inc(s_const, 1)
            pool.iota(pb[:, 0:1], pattern=[[1, 1]], base=0, channel_multiplier=CW,
                      allow_small_or_imprecise_dtypes=True).then_inc(s_const, 1)
            pool.iota(pb[:, 1:2], pattern=[[1, 1]], base=CW, channel_multiplier=T,
                      allow_small_or_imprecise_dtypes=True).then_inc(s_const, 1)
            dma_pass(pool, PASS_X_SRC, D, x[:, :])
            pool.wait_ge(s_ntw, 16 * NA_CH)
            dma_pass(pool, PASS_NT_SRC, 4, nt_d[:, :])
            dma_pass(pool, PASS_NT_DST, 4, nt_d[:, :])
            pool.wait_ge(s_ztab, 16 * 8)
            pool.wait_ge(s_expzw, 16 * ZERO_DMAS)
            pool.wait_ge(s_payw[0], 16)
            pool.wait_ge(s_trips[0], 1)
            n0 = pool.value_load(trips_i[0][0:1, 0:1], min_val=1, max_val=CW // (2 * CU))
            list_dma(pool, 0, n0, 0, 0, 4, pay_d[0][:, :])
            pool.wait_ge(s_fullw, 16)
            list_dma(pool, 0, n0, 1, 1, TW, full_d[:, :])
            list_dma(pool, 0, n0, 2, 2, D, exp_d[0][:, :], scatter=True)
            pool.wait_ge(s_payw[1], 16)
            pool.wait_ge(s_trips[1], 1)
            n1 = pool.value_load(trips_i[1][0:1, 0:1], min_val=1, max_val=CW // (2 * CU))
            list_dma(pool, 1, n1, 0, 0, 4, pay_d[1][:, :])
            pool.wait_ge(s_ltabw[0], n0 * 16)
            pool.sem_inc(s_tick[0], 1)
            list_dma(pool, 1, n1, 1, 1, TW, list_d[0][:, :])
            with pool.Fori(0, K_STEPS - 3) as k:
                pool.wait_ge(s_ltabw[1], k * n1 * 16 + n1 * 16)
                pool.sem_inc(s_tick[0], 1)
                list_dma(pool, 1, n1, k + 2, k + 2, D, list_d[1][:, :])
            list_dma(pool, 1, n1, K_STEPS - 1, K_STEPS - 1, D, exp_d[1][:, :], scatter=True)
            pool.wait_ge(s_tabw, 16)
            dma_pass(pool, PASS_L0, D, agg_d[:, :])
            dma_pass(pool, PASS_X_DST, D, x[:, :])
            dma_pass(pool, PASS_ROW, ROW1, row_d[:, :], scatter=True)
            pool.wait_ge(s_tabw, 32)
            dma_pass(pool, PASS_ATT_SRC, D, att_d[:, :])
            dma_pass(pool, PASS_ATT_DST, D, att_d[:, :])
            pool.wait_ge(s_relt, 32)

            def out_src_slot(n, b):
                pool.wait_ge(s_oslot, n + 1)
                pool.sem_inc(s_tick[0], 1)
                for t in range(U):
                    pool.indirect_dma_start(out=out[:, :], out_offset=bass.IndirectOffsetOnAxis(
                        ap=oidx[:, b, t:t + 1], axis=0), in_=oring[b][:, t * D:(t + 1) * D], in_offset=None,
                        bounds_check=N - 1, oob_is_err=False).then_inc(s_oland[b], 16)

            pool.wait_ge(s_nout, 16 * CH)
            dma_pass(pool, PASS_REL, RW, rel_d[:, :], round_end=lambda i: out_src_slot(i, 0))
            with pool.Fori(0, (ROUNDS - 1) // 2) as k:
                for b in (1, 0):
                    out_src_slot(k * 2 + (ROUNDS + 1 - b), b)
            out_src_slot(2 * ROUNDS - 1, 1)
            pool.wait_ge(s_tabw, 48)
            dma_pass(pool, PASS_RGCN, D, rgcn_d[:, :])
            dma_pass(pool, PASS_OUT_DST, D, out[:, :], scatter=True, limit=N - 1)
            for b in range(2):
                pool.wait_ge(s_oland[b], 16 * U * ((3 * ROUNDS - 1) // 2 if b == 0 else (ROUNDS + 1) // 2))
            for h in range(2):
                pool.wait_ge(s_land[1][h], land_count(PASS_OUT_DST, ROUNDS - 1))

        def bc3(ap, n):
            return ap.unsqueeze(2).to_broadcast([ap.shape[0], ap.shape[1], n])

        def mid(ap, n):
            return ap.unsqueeze(1).to_broadcast([ap.shape[0], n, ap.shape[1]])

        @block.vector
        def _(dve):
            st = Steps(dve, s_dve)
            tick = s_tick[2]
            V = nc.vector

            st.do(V.memset(srci[:, :], N))
            st.do(V.memset(dsti[:, :], N))
            st.do(V.memset(etyi[:, :], 0))
            st.do(V.memset(ew[:, :], 0.0))
            st.wait()
            dve.sem_inc(s_pad, 1)
            st.do(V.memset(zrow[:, :], 0.0))
            st.do(V.memset(zrow4[:, :], 0.0))
            st.do(V.memset(YW[:, :], 0.0))
            st.wait()
            st.do(V.memset(zrow[:, D:D + 1], float(ZROW)))
            st.do(V.memset(zrow4[:, 0:1], float(ZROW)))
            st.do(V.memset(zrow4[:, 2:3], -1.0))
            st.do(V.memset(zrow4[:, 3:4], float(OOB)))
            st.wait()
            dve.sem_inc(s_zr, 1)
            dve.sem_inc(s_expz, 1)
            st.do(V.memset(roots[:, :], 1.0))
            st.do(V.memset(bd1[:, :], 0.0))
            st.do(V.memset(bdy[:, :], 0.0))
            for kind, (_, eps) in ROOTS.items():
                st.do(V.memset(eps_t[kind][:, :], eps))
            st.do(V.memset(zh[:, :], 0.0))
            st.wait()

            dve.wait_ge(s_in, 16 * 8)
            st.do(V.tensor_scalar(srcf[:, :], srci[:, :], 0.0, None, ALU.add))
            st.do(V.tensor_scalar(dstf[:, :], dsti[:, :], 0.0, None, ALU.add))
            st.do(V.tensor_scalar(xsi[:, :], srci[:, :], float(N - 1), None, ALU.min))
            st.do(V.tensor_scalar(xdi[:, :], dsti[:, :], float(N - 1), None, ALU.min))
            st.wait()
            dve.sem_inc(s_ids, 1)
            for key, a, b in ((srci, a_s, b_s), (dsti, a_d, b_d)):
                st.seq(V.tensor_scalar(tmpi[:, :], key[:, :], NB_COL.bit_length() - 1, None, ALU.logical_shift_right))
                st.seq(V.tensor_scalar(a[:, :], tmpi[:, :], 0.0, None, ALU.add))
                st.seq(V.tensor_scalar(tmpi[:, :], key[:, :], NB_COL - 1, None, ALU.bitwise_and))
                st.seq(V.tensor_scalar(b[:, :], tmpi[:, :], 0.0, None, ALU.add))

            dve.wait_ge(s_const, 12)
            st.do(V.tensor_copy(ident_h[:, :], ident[:, :]))
            st.do(V.memset(emask[:, 0:3 * P], 1.0))
            st.do(V.tensor_copy(emask[:, 3 * P:4 * P], low[:, :]))
            st.wait()
            dve.sem_inc(s_cst2, 1)

            with dve.Fori(0, NG) as i:
                for j in range(4):
                    col = lambda t: t[:, bass.ds(i * 4 + j, 1)]
                    dve.wait_ge(s_ohu, i * 4 + j + 1)
                    dve.sem_inc(tick, 1)
                    V.tensor_scalar(oha[:, j, :], iota_h[:, :], col(a_d), None, ALU.is_equal)
                    V.tensor_scalar(ohb[:, j, :], iota_h[:, 0:NB_COL], col(b_d), None, ALU.is_equal)
                    V.tensor_scalar(oha2[:, j, :], iota_h[:, :], col(a_s), None, ALU.is_equal)
                    V.tensor_scalar(ohb2[:, j, :], iota_h[:, 0:NB_COL], col(b_s), None,
                                    ALU.is_equal).then_inc(s_oh, 1)
            dve.wait_ge(s_hist, 1)
            dve.wait_ge(s_expzw, 16 * ZERO_DMAS)
            hc = lambda tile, k, c: tile[:, k * TB + c * NB_COL:k * TB + (c + 1) * NB_COL]
            for k in range(2):
                for c in range(NA_CH):
                    st.do(V.tensor_scalar(hc(HC, k, c), bank[c][:, k * NB_COL:(k + 1) * NB_COL], 0.0, None, ALU.add))
            st.wait()
            for k in range(2):
                for c in range(NA_CH):
                    st.do(V.tensor_tensor_scan(hc(IC, k, c), ones[:, 0:1].to_broadcast([P, NB_COL]), hc(HC, k, c),
                                               0.0, ALU.mult, ALU.add))
            st.wait()
            for k in range(2):
                st.do(V.tensor_copy(tot[:, k, :], IC[:, k * TB:(k + 1) * TB].rearrange(
                    "p (c b) -> p c b", b=NB_COL)[:, :, NB_COL - 1]))
            st.wait()
            dve.sem_inc(s_tot, 1)
            dve.wait_ge(s_base, 1)
            st.do(V.tensor_copy(base[:, :, :], bank[4][:, 0:2 * NA_CH].rearrange("p (k c) -> p k c", k=2)))
            st.do(V.tensor_copy(tot[:, :, :], bank[5][:, 0:2 * NA_CH].rearrange("p (k c) -> p k c", k=2)))
            st.wait()
            for c in range(1, NA_CH):
                for e in range(c):
                    st.seq(V.tensor_tensor(base[:, :, c:c + 1], base[:, :, c:c + 1], tot[:, :, e:e + 1], ALU.add))
            for k in range(2):
                for c in range(NA_CH):
                    st.do(V.tensor_scalar(hc(IC, k, c), hc(IC, k, c), base[:, k, c:c + 1], float(-1 - ZROW), ALU.add,
                                          ALU.add))
            st.wait()
            nt = NTB.rearrange("p (n f) -> p n f", f=4)
            for k in range(2):
                h, e = HC[:, k * TB:(k + 1) * TB], IC[:, k * TB:(k + 1) * TB]
                st.do(V.tensor_copy(nt[:, :, 2 * k + 1], h))
                st.seq(V.scalar_tensor_tensor(out=e, in0=h, scalar=0.0, in1=e, op0=ALU.is_gt, op1=ALU.mult))
                st.do(V.tensor_scalar(nt[:, :, 2 * k], e, float(ZROW), None, ALU.add))
            st.wait()
            dve.sem_inc(s_nt, 1)

            st.do(V.memset(rhi[0], 0.0))
            st.do(V.memset(rlo[0], 0.0))
            RANK_STEPS = 8 + 1 + 8 + 2 + 1

            def batch_cols(t, i, n=4, j=0):
                return t[:, bass.ds(i * 4 + j, n)]

            def rank_onehots(i, b):
                for j in range(4):
                    st.do(V.tensor_scalar(ohas[b][:, j, :], iota_h[:, :], batch_cols(a_s, i, 1, j), None, ALU.is_equal))
                    st.do(V.tensor_scalar(ohbs[b][:, j, :], iota_h[:, 0:NB_COL], batch_cols(b_s, i, 1, j), None,
                                          ALU.is_equal))
                st.do(V.tensor_scalar(kcol[:, b, :], batch_cols(srcf, i), 0.0, None, ALU.add))
                st.wait()
                dve.sem_inc(s_oh, 1)

            def rank_batch(i, b, last=False):
                if not last:
                    rank_onehots(i + 1, 1 - b)
                dve.wait_ge(s_kt, i + 1)
                dve.sem_inc(tick, 1)
                at_ = 0
                for j in range(4):
                    n = (j + 1) * P
                    st.do(V.scalar_tensor_tensor(out=junk[:, at_:at_ + n], in0=bank[4 + 3 * b][:, 0:n],
                                                 scalar=batch_cols(srcf, i, 1, j), in1=emask[:, 4 * P - n:4 * P],
                                                 op0=ALU.is_equal, op1=ALU.mult, accum_out=rk4[:, j:j + 1]))
                    at_ += n
                st.wait()
                dve.sem_inc(s_eq, 1)
                if not last:
                    dve.wait_ge(s_rhi, i + 1)
                    dve.sem_inc(tick, 1)
                    for k in range(2):
                        pair = lambda t: t[1 - b][:, 2 * k:2 * k + 2, :].rearrange("p c n -> p (c n)")
                        st.do(V.tensor_tensor(pair(rlo), bank[k][:, :], pair(rhi), ALU.subtract))
                    st.wait()
                    dve.sem_inc(s_rc, 1)
                dve.wait_ge(s_g, i + 1)
                dve.sem_inc(tick, 1)
                for j in range(4):
                    g = bank[5 + j // 2][:, (j % 2) * NB_COL:(j % 2 + 1) * NB_COL]
                    st.do(V.scalar_tensor_tensor(out=junk[:, at_:at_ + NB_COL], in0=g, scalar=1.0, in1=ohbs[b][:, j, :],
                                                 op0=ALU.mult, op1=ALU.mult, accum_out=cnt4[:, j:j + 1]))
                    at_ += NB_COL
                st.wait()
                dve.sem_inc(s_gu, 1)
                st.seq(V.tensor_tensor(batch_cols(posf, i), cnt4[:, :], rk4[:, :], ALU.add))

            def stepped_ring_pass(n, fill, take, per, round_work=None, extra=0, last_work=None, between=None,
                                  before_fill=None):
                f = family(n)[0]
                if before_fill:
                    before_fill(0)
                for h in range(2):
                    fill(0, h).then_inc(s_slot, 1)
                if between:
                    between()
                with st.loop(ROUNDS - 1, 2 * per + extra) as i:
                    if before_fill:
                        before_fill(i + 1)
                    for h in range(2):
                        dve.wait_ge(s_land[f][h], i * LAND + land_count(n, 0))
                        dve.sem_inc(tick, 1)
                        take(i, h)
                        fill(i + 1, h).then_inc(s_slot, 1)
                    if round_work:
                        round_work(i)
                for h in range(2):
                    dve.wait_ge(s_land[f][h], land_count(n, ROUNDS - 1))
                    dve.sem_inc(tick, 1)
                    take(ROUNDS - 1, h)
                if last_work:
                    last_work(ROUNDS - 1)

            def fill_idx(idx):
                return lambda i, h: V.tensor_scalar(ridx[:, h, :], cols(idx, i, h), 0.0, None, ALU.add)

            def slot(h, w=D):
                return ring[:, h, 0:U * w]

            def copy_take(dest, w=D):
                def take(i, h):
                    st.do(V.tensor_scalar(cols(dest, i, h, w), slot(h, w), 0.0, None, ALU.add))
                    st.wait()
                    dve.sem_inc(tick, 1)
                return take

            assert NG == 2 * 4 * (ROUNDS - 1) + 1
            dve.wait_ge(s_actp, 2)
            st.wait()
            dve.sem_inc(s_rc, 1)
            dve.sem_inc(s_eq, 1)
            dve.sem_inc(s_gu, 1)
            rank_onehots(0, 0)

            def ranks_from(start):
                def work(i):
                    for c in range(4):
                        rank_batch(i * 4 + (start + c), c % 2)
                return work

            stepped_ring_pass(PASS_NT_SRC, fill_idx(srci), copy_take(S[:, 0:4 * T], 4), 1, ranks_from(0),
                              4 * RANK_STEPS)
            stepped_ring_pass(PASS_NT_DST, fill_idx(dsti), copy_take(S[:, 4 * T:8 * T], 4), 1,
                              ranks_from(4 * (ROUNDS - 1)), 4 * RANK_STEPS)
            rank_batch(NG - 1, 0, last=True)
            st.wait()

            st.do(V.tensor_copy(gin[:, :], NS3[:, :, 0]))
            st.do(V.tensor_copy(ginf[:, :], NS3[:, :, 0]))
            st.do(V.tensor_copy(gout_s[:, :], NS3[:, :, 2]))
            st.do(V.tensor_copy(gout_d[:, :], ND3[:, :, 2]))
            st.do(V.tensor_tensor(t1[:, :], NS3[:, :, 2], NS3[:, :, 3], ALU.subtract))
            st.wait()
            st.seq(V.scalar_tensor_tensor(out=posf[:, :], in0=t1[:, :], scalar=1.0, in1=posf[:, :], op0=ALU.add,
                                          op1=ALU.add))
            st.do(V.tensor_copy(posi[:, :], posf[:, :]))
            st.do(V.tensor_tensor(dend[:, :], ND3[:, :, 0], q_f[:, :], ALU.is_equal))
            st.do(V.tensor_tensor(t1[:, :], NS3[:, :, 2], posf[:, :], ALU.is_equal))
            st.do(V.tensor_scalar(t2[:, :], NS3[:, :, 1], 0.0, None, ALU.is_equal))
            st.wait()
            st.seq(V.tensor_tensor(t1[:, :], t1[:, :], t2[:, :], ALU.mult))
            for flag, key, dest in ((t1, srcf, osi), (dend, dstf, odi)):
                st.seq(V.scalar_tensor_tensor(out=t2[:, :], in0=key[:, :], scalar=float(-OOB), in1=flag[:, :],
                                              op0=ALU.add, op1=ALU.mult))
                if dest is osi:
                    st.seq(V.tensor_scalar(t3[:, :], t2[:, :], float(OOB), None, ALU.add))
                else:
                    st.seq(V.tensor_scalar(posf[:, :], t2[:, :], float(OOB), None, ALU.add))
            st.do(V.tensor_scalar(t1[:, :], NS3[:, :, 1], 1.0, None, ALU.max))
            st.do(V.tensor_scalar(t2[:, :], NS3[:, :, 3], 1.0, None, ALU.max))
            st.do(V.tensor_scalar(c3[:, :], ND3[:, :, 1], 1.0, None, ALU.max))
            st.wait()
            dve.sem_inc(s_sri, 1)
            dve.wait_ge(s_sro, 1)
            st.do(V.reciprocal(t1[:, :], t1[:, :]))
            st.do(V.reciprocal(t2[:, :], t2[:, :]))
            st.seq(V.reciprocal(c3[:, :], c3[:, :]))
            st.do(V.tensor_scalar(c3[:, :], c3[:, :], 1.0 - ALPHA, None, ALU.mult))
            st.do(V.scalar_tensor_tensor(out=c1[:, :], in0=t1[:, :], scalar=1.0 - ALPHA, in1=t2[:, :], op0=ALU.mult,
                                         op1=ALU.mult))
            st.do(V.tensor_scalar(c2[:, :], t2[:, :], ALPHA, None, ALU.mult))

            def segments(key, mask, first, fcar, fbak, neg=None, n=0):
                st.do(V.tensor_tensor(mask[:, 1:T], key[:, 1:T], key[:, 0:T - 1], ALU.is_equal))
                st.do(V.memset(mask[:, 0:1], 0.0))
                st.do(V.tensor_scalar(first[:, :], key[:, :], key[:, 0:1], None, ALU.is_equal))
                st.do(V.tensor_copy(tl[:, 0:1], key[:, 0:1]))
                st.do(V.tensor_copy(tl[:, 1:2], key[:, T - 1:T]))
                st.wait()
                dve.sem_inc(s_trw, 1)
                dve.wait_ge(s_tr, n + 1)
                st.do(V.scalar_tensor_tensor(out=fcar[:, :], in0=bank[4][:, 0:P], scalar=tl[:, 1:2], in1=up[:, :],
                                             op0=ALU.is_equal, op1=ALU.mult))
                st.do(V.scalar_tensor_tensor(out=fbak[:, :], in0=bank[5][:, 0:P], scalar=tl[:, 0:1], in1=low[:, :],
                                             op0=ALU.is_equal, op1=ALU.mult))
                if neg is not None:
                    st.wait()
                    st.seq(V.tensor_scalar(neg[:, :], fbak[:, :], 1.0, BIG, ALU.subtract, ALU.mult))
                st.wait()

            ncarry = [0]

            def carries():
                dve.sem_inc(s_tail, 1)
                ncarry[0] += 1
                dve.wait_ge(s_carry, ncarry[0])

            def segment_sums(src3, dst3, width, mask, first):
                for d in range(width):
                    st.do(V.tensor_tensor_scan(dst3[:, :, d], mask[:, :], src3[:, :, d], 0.0, ALU.mult, ALU.add))
                st.wait()
                st.seq(V.tensor_scalar(tl[:, 0:width], dst3[:, T - 1, :], 0.0, None, ALU.add))
                carries()
                st.seq(V.tensor_copy(car[:, 0:width], bank[7][:, 0:width]))
                for d in range(width):
                    st.do(V.scalar_tensor_tensor(out=dst3[:, :, d], in0=first[:, :], scalar=car[:, d:d + 1],
                                                 in1=dst3[:, :, d], op0=ALU.mult, op1=ALU.add))
                st.wait()

            def spread_back(t3_, width, mask_end, key):
                st.seq(V.tensor_scalar(t1[:, :], mask_end[:, :], -1.0, 1.0, ALU.mult, ALU.add))
                st.seq(V.tensor_tensor(t3_, t3_, bc3(mask_end[:, :], width), ALU.mult))
                for d in range(width):
                    st.do(V.tensor_tensor_scan(t3_[:, ::-1, d], t1[:, ::-1], t3_[:, ::-1, d], 0.0, ALU.mult, ALU.add))
                st.do(V.tensor_scalar(t2[:, :], key[:, :], key[:, T - 1:T], None, ALU.is_equal))
                st.wait()
                st.do(V.tensor_scalar(tl[:, 0:width], t3_[:, 0, :], 0.0, None, ALU.add))
                st.do(V.tensor_scalar(t2[:, :], t2[:, :], t1[:, T - 1:T], None, ALU.mult))
                st.wait()
                carries()
                st.seq(V.tensor_copy(car[:, 0:width], bank[7][:, 0:width]))
                for d in range(width):
                    st.do(V.scalar_tensor_tensor(out=t3_[:, :, d], in0=t2[:, :], scalar=car[:, d:d + 1],
                                                 in1=t3_[:, :, d], op0=ALU.mult, op1=ALU.add))
                st.wait()

            def root():
                dve.sem_inc(s_ri, 1)
                st.n += 1
                st.wait()
                dve.sem_inc(tick, 1)

            def chunk(t, i, w=D):
                return t[:, bass.ds(i * (RC * w), RC * w)].rearrange("p (t d) -> p t d", d=w)

            cols2 = lambda t, i: t[:, bass.ds(i * RC, RC)]

            def norm_chunk(tiles, i, ratio=None):
                k = len(tiles)
                part = lambda t, m: t[:, m * RC:(m + 1) * RC]
                sq = lambda m: sq_s[:, m * RC * D:(m + 1) * RC * D].rearrange("p (t d) -> p t d", d=D)
                dve.sem_inc(tick, 1)
                for m, t in enumerate(tiles):
                    st.do(V.tensor_reduce(part(roots, m), chunk(t, i), AX.X, ALU.add))
                st.wait()
                dve.sem_inc(tick, 1)
                st.seq(V.tensor_scalar(roots[:, 0:k * RC], roots[:, 0:k * RC], 1.0 / D, None, ALU.mult))
                for m, t in enumerate(tiles):
                    st.do(V.tensor_tensor(chunk(t, i), chunk(t, i), bc3(part(roots, m), D), ALU.subtract))
                st.wait()
                for m, t in enumerate(tiles):
                    st.do(V.tensor_tensor(sq(m), chunk(t, i), chunk(t, i), ALU.mult))
                st.wait()
                dve.sem_inc(tick, 1)
                for m, t in enumerate(tiles):
                    st.do(V.tensor_reduce(part(roots, m), sq(m), AX.X, ALU.add))
                st.wait()
                if ratio is not None:
                    st.seq(V.tensor_copy(vs[:, :], part(roots, 0)))
                root()
                if ratio is not None:
                    st.seq(V.tensor_copy(rs[:, :], part(roots, 0)))
                st.seq(V.reciprocal(roots[:, 0:k * RC], roots[:, 0:k * RC]))
                for m, t in enumerate(tiles):
                    st.do(V.tensor_tensor(chunk(t, i), chunk(t, i), bc3(part(roots, m), D), ALU.mult))
                st.wait()
                if ratio is not None:
                    st.seq(V.tensor_copy(part(roots, 0), vs[:, :]))
                    root()
                    st.seq(V.reciprocal(part(roots, 0), part(roots, 0)))
                    st.seq(V.tensor_tensor(cols2(ratio, i), part(roots, 0), rs[:, :], ALU.mult))

            def logits_chunk(t, k, i):
                shape = [P, RC, NH, D]
                lp = lp_s.rearrange("p (t h d) -> p t h d", h=NH, d=D)
                u = u_all[:, k * NH * D:(k + 1) * NH * D].rearrange("p (h d) -> p h d", h=NH)
                st.seq(V.tensor_tensor(lp, chunk(t, i).unsqueeze(2).to_broadcast(shape),
                                       u.unsqueeze(1).to_broadcast(shape), ALU.mult))
                dve.sem_inc(tick, 1)
                z = chunk((z4t, e4t)[k], i, NH)
                st.seq(V.tensor_reduce(z, lp, AX.X, ALU.add))

            st.do(V.tensor_copy(osi[:, :], t3[:, :]))
            st.wait()
            st.do(V.tensor_copy(t3[:, :], t2[:, :]))
            segments(dstf, dmask, dfirst, dcar, dbak, neg=dneg, n=0)
            nrow = [1]

            def column_max(out_, neg=None):
                st.wait()
                dve.sem_inc(s_trw, 1)
                nrow[0] += 1
                dve.wait_ge(s_tr, nrow[0])
                if neg is None:
                    st.seq(V.tensor_reduce(out_, bank[4][:, 0:P], AX.X, ALU.max))
                else:
                    st.seq(V.tensor_tensor(prod[:, 0:P], bank[4][:, 0:P], neg[:, :], ALU.add))
                    st.seq(V.tensor_reduce(out_, prod[:, 0:P], AX.X, ALU.max))

            CS = [None, None]

            flat4 = lambda t, i, h: t[:, bass.ds(i * (2 * CU * D) + h * (CU * D), CU * D)]

            @contextmanager
            def both_loops(a, b, count, per, dyn):
                an, bd, ao, bo = a.n, b.dyn, a.off, b.off
                with dve.Fori(0, count) as k:
                    a.off, b.off = k * per, k * b.trips * dyn
                    yield k
                    assert (a.n - an, b.dyn - bd) == (per, dyn), (a.n - an, b.dyn - bd)
                    a.off, b.off = ao, bo
                a.n, b.dyn = an + per * count, bd + dyn * count

            def make_list(v, act, n, to_row, stride):
                st.seq(V.tensor_reduce(tl[:, 0:1], act[:, 0:n], AX.X, ALU.add))
                column_max(car[:, 0:1])
                st.seq(V.tensor_scalar(trips_i[v][:, :], car[:, 0:1], float(2 * CU - 1), None, ALU.add))
                st.seq(V.tensor_scalar(trips_i[v][:, :], trips_i[v][:, :], 3, None, ALU.logical_shift_right))
                st.seq(V.tensor_scalar(trips_i[v][:, :], trips_i[v][:, :], 1, None, ALU.max))
                dve.sem_inc(s_trips[v], 1)
                trips = dve.value_load(trips_i[v][0:1, 0:1], min_val=1, max_val=CW // (2 * CU))
                CS[v] = cs = Steps(dve, s_lst[v], trips)
                st.do(V.memset(lkey, 0.0))
                st.do(V.memset(lval, 0.0))
                st.wait()
                st.seq(V.tensor_tensor(lkey[:, 0:n], act[:, 0:n], ramp_c[:, 0:n], ALU.mult))
                with cs.trip_loop(3) as i:
                    cs.seq(V.max(m8[:, :], lkey[:, 0:CW]))
                    dve.sem_inc(tick, 1)
                    cs.seq(V.match_replace(lkey[:, 0:CW], m8[:, :], lkey[:, 0:CW], 0.0))
                    dve.sem_inc(tick, 1)
                    cs.seq(V.tensor_scalar(lval[:, bass.ds(i * 8, 8)], m8[:, :], 0.0, None, ALU.add))
                    dve.sem_inc(tick, 1)
                st.seq(V.tensor_scalar(lact, lval, -1.0, to_row, ALU.mult, ALU.add))
                st.seq(V.tensor_scalar(lact, lact, stride, None, ALU.add))
                st.seq(V.scalar_tensor_tensor(out=lact, in0=lval, scalar=0.0, in1=lact, op0=ALU.is_gt, op1=ALU.mult))
                st.seq(V.tensor_scalar(lq, lact, float(ZROW), None, ALU.add))
                return cs

            def positions(cs_v, act, n, mask, first, scale_tail):
                st.seq(V.tensor_tensor_scan(lcnt[:, 0:n], ones[:, 0:1].to_broadcast([P, n]), act[:, 0:n], 0.0,
                                            ALU.mult, ALU.add))
                st.seq(V.scalar_tensor_tensor(out=lcnt[:, 0:n], in0=lcnt[:, 0:n], scalar=pb[:, 0:1], in1=act[:, 0:n],
                                              op0=ALU.add, op1=ALU.mult))
                st.seq(V.tensor_tensor_scan(lkey[:, 0:n], mask[:, 0:n], lcnt[:, 0:n], 0.0, ALU.mult, ALU.max))
                st.seq(V.tensor_scalar(tl[:, 0:1], lkey[:, n - 1:n], scale_tail, None, ALU.mult))
                column_max(car[:, 0:1], dneg)
                st.seq(V.scalar_tensor_tensor(out=lkey[:, 0:n], in0=first[:, 0:n], scalar=car[:, 0:1],
                                              in1=lkey[:, 0:n], op0=ALU.mult, op1=ALU.max))
                st.seq(V.tensor_scalar(lcnt[:, 0:n], lkey[:, 0:n], float(-1 - ZROW), None, ALU.add))
                st.seq(V.scalar_tensor_tensor(out=lcnt[:, 0:n], in0=lkey[:, 0:n], scalar=0.0, in1=lcnt[:, 0:n],
                                              op0=ALU.is_gt, op1=ALU.mult))
                st.seq(V.tensor_scalar(lcnt[:, 0:n], lcnt[:, 0:n], float(ZROW), None, ALU.add))

            def list_gather(v, cs, m, idx, take, per):
                n = cs.trips
                fill = lambda i, h: V.tensor_scalar(
                    cidx[:, h, :], idx[:, h * CU:(h + 1) * CU] if isinstance(i, int) else
                    idx[:, bass.ds(i * (2 * CU) + h * CU, CU)], 0.0, None, ALU.add)
                for h in range(2):
                    fill(0, h).then_inc(s_lslot[v], 1)
                with cs.trip_loop(2 * per) as i:
                    for h in range(2):
                        dve.wait_ge(s_lland[v][h], i * (16 * CU) + (16 * CU) + (m * n * (16 * CU) if not isinstance(m, int) or m else 0))
                        dve.sem_inc(tick, 1)
                        take(i, h)
                        fill(i + 1, h).then_inc(s_lslot[v], 1)
                dve.wait_ge(s_lslot[v], (m * n * 2 if not isinstance(m, int) or m else 0) + n * 2 + m * 2 + 2)
                dve.sem_inc(tick, 1)

            def list_scatter(v, cs, a, b, fill):
                n = cs.trips
                with dve.Fori(0, n) as i:
                    for h in range(2):
                        fill(i, h)
                        V.tensor_scalar(cidx[:, h, :], lidx[:, bass.ds(i * (2 * CU) + h * CU, CU)], 0.0, None,
                                        ALU.add).then_inc(s_lslot[v], 1)
                    for h in range(2):
                        dve.wait_ge(s_lland[v][h], n * (16 * CU * a) + i * (16 * CU) + 16 * CU)
                    dve.sem_inc(tick, 1)

            chunk4 = lambda t, i, h, w: t[:, bass.ds(i * (2 * CU * w) + h * (CU * w), CU * w)].rearrange(
                "p (j w) -> p j w", w=w)

            def pay_take(v, cs):
                def take(i, h):
                    cs.seq(V.tensor_scalar(chunk4(PAY[v], i, h, 4), cring[:, h, 0:CU * 4].rearrange(
                        "p (j w) -> p j w", w=4), 0.0, None, ALU.add))
                    dve.sem_inc(tick, 1)
                return take

            def list_masks(v):
                key = PAY[v][:, :].rearrange("p (j w) -> p j w", w=4)[:, :, 2]
                st.do(V.tensor_tensor(lmask[:, 1:CW], key[:, 1:CW], key[:, 0:CW - 1], ALU.is_equal))
                st.do(V.memset(lmask[:, 0:1], 0.0))
                st.do(V.tensor_scalar(lkey[:, 0:CW], key, 0.0, None, ALU.is_lt))
                st.do(V.tensor_scalar(lfirst[:, 0:CW], key, dstf[:, 0:1], None, ALU.is_equal))
                st.do(V.tensor_reduce(tm[:, :], key, AX.X, ALU.max))
                st.wait()
                st.do(V.tensor_tensor(lmask[:, 0:CW], lmask[:, 0:CW], lkey[:, 0:CW], ALU.max))
                st.do(V.tensor_scalar(tm[:, :], tm[:, :], dstf[:, T - 1:T], None, ALU.is_equal))
                st.wait()

            def row_take(v, cs, w, z, zw, total, first):
                pay3 = lambda i, h: chunk4(PAY[v], i, h, 4)[:, :, 1]
                r = lambda h: cring[:, h, 0:CU * w].rearrange("p (j w) -> p j w", w=w)

                def take(i, h):
                    cs.seq(V.tensor_tensor(y4[:, :, :], r(h)[:, :, 0:D], pay3(i, h).unsqueeze(2).to_broadcast(
                        [P, CU, D]), ALU.mult))
                    dve.sem_inc(tick, 1)
                    if z is not None:
                        for j in range(CU):
                            cs.seq(V.scalar_tensor_tensor(
                                out=zr[:, j + 1, :], in0=zr[:, j, :],
                                scalar=lmask[:, bass.ds(i * (2 * CU) + h * CU + j, 1)], in1=y4[:, j, :],
                                op0=ALU.mult, op1=ALU.add))
                            dve.sem_inc(tick, 1)
                        cs.do(V.tensor_scalar(chunk4(z, i, h, zw)[:, :, 0:D], zr[:, 1:CU + 1, :], 0.0, None, ALU.add))
                        cs.do(V.tensor_scalar(zr[:, 0, :], zr[:, CU, :], 0.0, None, ALU.add))
                    if w == TW:
                        cs.do(V.tensor_scalar(lnext[:, bass.ds(i * (2 * CU) + h * CU, CU)], r(h)[:, :, D], 0.0, None,
                                              ALU.add))
                    t = chunk4(total, i, h, D)
                    if first:
                        cs.do(V.tensor_scalar(t, y4[:, :, :], 0.0, None, ALU.add))
                    else:
                        cs.do(V.tensor_tensor(t, t, y4[:, :, :], ALU.add))
                    cs.wait()
                    dve.sem_inc(tick, 1)
                return take

            def list_carry(v, cs, z, zw, count):
                st.seq(V.tensor_scalar(tl[:, 0:D], zr[:, 0, :], tm[:, 0:1], None, ALU.mult))
                dve.sem_inc(s_tail, 1)
                dve.wait_ge(s_carry, count)
                dve.sem_inc(tick, 1)
                st.seq(V.tensor_scalar(car[:, :], bank[7][:, 0:D], 0.0, None, ALU.add))
                dve.sem_inc(tick, 1)
                pr8 = prod[:, 0:2 * CU * D].rearrange("p (j w) -> p j w", w=D)
                with cs.trip_loop(2) as i:
                    f = lfirst[:, bass.ds(i * (2 * CU), 2 * CU)].unsqueeze(2).to_broadcast([P, 2 * CU, D])
                    zz = z[:, bass.ds(i * (2 * CU * zw), 2 * CU * zw)].rearrange("p (j w) -> p j w", w=zw)[:, :, 0:D]
                    cs.seq(V.tensor_tensor(pr8, f, mid(car[:, 0:D], 2 * CU), ALU.mult))
                    dve.sem_inc(tick, 1)
                    cs.seq(V.tensor_tensor(zz, zz, pr8, ALU.add))
                    dve.sem_inc(tick, 1)

            st.seq(V.tensor_tensor(Y3, XS3, bc3(c2[:, :], D), ALU.mult))
            segment_sums(Y3, S3, D, dmask, dfirst)
            st.do(V.tensor_scalar(t1[:, :], ginf[:, :], float(ZROW), None, ALU.is_lt))
            st.do(V.tensor_scalar(t2[:, :], srcf[:, :], float(N), None, ALU.is_lt))
            st.wait()
            st.seq(V.tensor_tensor(t1[:, :], t1[:, :], t2[:, :], ALU.mult))
            cs = make_list(0, t1, T, pb[:, 1:2], float(-ZROW))
            pay3 = PAY[0][:, 0:T * 4].rearrange("p (j w) -> p j w", w=4)
            st.do(V.tensor_copy(pay3[:, :, 0], ginf[:, :]))
            st.do(V.tensor_copy(pay3[:, :, 1], c1[:, :]))
            st.do(V.tensor_copy(pay3[:, :, 2], dstf[:, :]))
            st.do(V.tensor_copy(pay3[:, :, 3], q_f[:, :]))
            st.wait()
            dve.sem_inc(s_pay[0], 1)
            st.do(V.memset(tm[:, :], 1.0))
            st.wait()
            positions(cs, t1, T, dmask, dfirst, tm[:, 0:1])
            st.do(V.tensor_copy(FULL[:, :, 0:D], S3))
            st.do(V.tensor_copy(FULL[:, :, D], lcnt[:, 0:T]))
            st.do(V.memset(FULL[:, :, D + 1:TW], 0.0))
            st.wait()
            dve.sem_inc(s_full, 1)
            dve.wait_ge(s_payw[0], 16)
            st.seq(V.memset(PAY[0][:, :], -1.0))
            list_gather(0, cs, 0, lq, pay_take(0, cs), 1)
            list_masks(0)
            p0 = PAY[0][:, :].rearrange("p (j w) -> p j w", w=4)
            for t in (lidx, lidx2):
                st.do(V.memset(t, ZROW))
            st.do(V.memset(lnext, float(ZROW)))
            st.wait()
            st.do(V.tensor_copy(lidx2[:, 0:CW], p0[:, :, 0]))
            st.do(V.tensor_copy(lidx[:, 0:CW], p0[:, :, 3]))
            dve.wait_ge(s_fullw, 16)
            st.do(V.memset(zr[:, :, :], 0.0))
            st.do(V.memset(RB[:, 0:CW * TW], 0.0))
            st.wait()
            list_gather(0, cs, 1, lidx2, row_take(0, cs, TW, RB[:, 0:CW * TW], TW, YW, True), 9)
            ncarry[0] += 1
            list_carry(0, cs, RB[:, 0:CW * TW], TW, ncarry[0])
            st.seq(V.tensor_scalar(t1w, lnext[:, 0:CW], float(ZROW), None, ALU.is_lt))
            positions(cs, t1w, CW, lmask, lfirst, tm[:, 0:1])
            st.do(V.tensor_copy(Z0[:, :, D], lcnt[:, 0:CW]))
            st.do(V.tensor_copy(p0[:, :, 0], lnext[:, 0:CW]))
            st.wait()
            dve.sem_inc(s_ltab[0], 1)
            dve.sem_inc(s_pay[1], 1)

            def fill0(i, h):
                V.tensor_scalar(cring[:, h, 0:CU * D].rearrange("p (j w) -> p j w", w=D), chunk4(YW, i, h, D), 0.0,
                                None, ALU.add)

            list_scatter(0, cs, 2, 2, fill0)
            st.seq(V.memset(PAY[1][:, :], -1.0))
            cs = make_list(1, t1w, CW, pb[:, 0:1], float(CW - ZROW))
            list_gather(1, cs, 0, lq, pay_take(1, cs), 1)
            list_masks(1)
            p1 = PAY[1][:, :].rearrange("p (j w) -> p j w", w=4)
            for t in (lidx, lidx2):
                st.do(V.memset(t, ZROW))
            st.do(V.memset(lnext, float(ZROW)))
            st.wait()
            st.do(V.tensor_copy(lidx2[:, 0:CW], p1[:, :, 0]))
            st.do(V.tensor_copy(lidx[:, 0:CW], p1[:, :, 3]))
            st.do(V.memset(zr[:, :, :], 0.0))
            st.do(V.memset(S, 0.0))
            st.wait()
            list_gather(1, cs, 1, lidx2, row_take(1, cs, TW, SW, D, XDW, True), 9)
            ncarry[0] += 1
            list_carry(1, cs, SW, D, ncarry[0])
            st.seq(V.tensor_copy(lidx2, lnext))
            dve.sem_inc(s_ltab[1], 1)
            with both_loops(st, cs, K_STEPS - 4, 3, 18) as k:
                st.seq(V.memset(zr[:, :, :], 0.0))
                list_gather(1, cs, k + 2, lidx2, row_take(1, cs, D, SW, D, XDW, False), 8)
                list_carry(1, cs, SW, D, k + (ncarry[0] + 1))
                dve.sem_inc(s_ltab[1], 1)
            ncarry[0] += K_STEPS - 4
            list_gather(1, cs, K_STEPS - 2, lidx2, row_take(1, cs, D, None, D, YW, True), 2)

            def fill1(i, h):
                V.scalar_tensor_tensor(out=cring[:, h, 0:CU * D], in0=flat4(YW, i, h), scalar=10.0,
                                       in1=flat4(XDW, i, h), op0=ALU.mult, op1=ALU.add)

            list_scatter(1, cs, K_STEPS - 1, K_STEPS - 1, fill1)
            dve.sem_inc(s_exp, 1)
            st.seq(V.tensor_tensor(Y3, XS3, bc3(c2[:, :], D), ALU.mult))
            dve.wait_ge(s_expl, 32)
            st.seq(V.tensor_tensor(Y, Y, S, ALU.add))
            st.seq(V.tensor_tensor(Y, Y, XD, ALU.add))
            segment_sums(Y3, S3, D, dmask, dfirst)
            dve.sem_inc(s_tab, 1)

            def node_chunk(c):
                x3, q3, m = nx3[0:NODE_P], nsq3[0:NODE_P], [nr1[0:NODE_P, :]]
                wide = lambda t: t.unsqueeze(2).to_broadcast([NODE_P, CR, D])
                dve.wait_ge(s_nin, c * 16 + 16)
                dve.sem_inc(tick, 1)
                st.seq(V.tensor_reduce(m[0], x3, AX.X, ALU.add))
                st.seq(V.tensor_scalar(m[0], m[0], 1.0 / D, None, ALU.mult))
                st.seq(V.tensor_tensor(x3, x3, wide(m[0]), ALU.subtract))
                st.seq(V.tensor_tensor(q3, x3, x3, ALU.mult))
                st.seq(V.tensor_reduce(m[0], q3, AX.X, ALU.add))
                root()
                st.seq(V.reciprocal(m[0], m[0]))
                st.seq(V.tensor_tensor(x3, x3, wide(m[0]), ALU.mult))
                st.seq(V.tensor_tensor(x3, x3, mid(bc[0:NODE_P, :], CR), ALU.add))
                st.seq(V.tensor_tensor(q3, x3, x3, ALU.mult))
                st.seq(V.tensor_reduce(m[0], q3, AX.X, ALU.add))
                root()
                st.seq(V.reciprocal(m[0], m[0]))
                st.do(V.tensor_tensor(x3, x3, wide(m[0]), ALU.mult))
                st.wait()
                dve.sem_inc(s_nok, 1)

            dve.wait_ge(s_w, 16 * (4 * 4 + 5))
            dve.wait_ge(s_bd, 16 * 4)
            st.seq(V.tensor_reduce(bm[:, :], b_bias[:, :], AX.X, ALU.add))
            st.seq(V.tensor_scalar(bm[:, :], bm[:, :], -1.0 / D, None, ALU.mult))
            st.seq(V.tensor_scalar(bc[:, :], b_bias[:, :], bm[:, 0:1], None, ALU.add))
            for k in range(2):
                st.seq(V.tensor_tensor(prod[:, 0:NH * D].rearrange("p (h o) -> p h o", h=NH),
                                       wcat[:, :].rearrange("p (h o) -> p h o", h=NH),
                                       mid(wsd[:, k * D:(k + 1) * D], NH), ALU.mult))
                st.seq(V.tensor_reduce(ua[:, k, :], prod[:, 0:NH * D].rearrange("p (h o) -> p h o", h=NH), AX.X,
                                       ALU.add))
            for k in range(2):
                for h in range(NH):
                    m = (k * NH + h) * D
                    st.do(V.tensor_scalar(udiag[:, m:m + D], ident[0:D, 0:D], ua[0:D, k, h:h + 1], None, ALU.mult))
            for j in range(GT):
                r = slice(32 * j, 32 * j + 32)
                st.do(V.tensor_scalar(bd1[r, j * NH * D:(j + 1) * NH * D], wcat[r, :], 1.0 / NH, None, ALU.mult))
                for at_, w in ((0, wf[r, :]), (NB * D, aw[r, 0:D]), ((NB + 1) * D, aw[r, 2 * D:3 * D])):
                    part = w16[r, at_:at_ + w.shape[1]]
                    st.seq(V.tensor_copy(part, w))
                    if j >= 2:
                        st.seq(V.tensor_tensor(part, w, part, ALU.subtract))
                st.do(V.tensor_copy(bdy[r, j * D:(j + 1) * D], aw[r, D:2 * D]))
            st.wait()
            dve.sem_inc(s_wb, 1)

            dve.wait_ge(s_mm, 1)
            st.seq(V.tensor_copy(u_all[:, :], bank[6][:, 0:2 * NH * D]))
            st.seq(V.reciprocal(t2[:, :], t3[:, :]))
            st.seq(V.tensor_tensor(c1[:, :], c1[:, :], t2[:, :], ALU.mult))

            def last_take(i, h):
                xs = cols(XS, i, h, D)
                y = prod[:, 0:U * D]
                st.seq(V.tensor_tensor(y.rearrange("p (t d) -> p t d", d=D), slot(h).rearrange(
                    "p (t d) -> p t d", d=D), cols(c1, i, h).unsqueeze(2).to_broadcast([P, U, D]), ALU.mult))
                st.seq(V.scalar_tensor_tensor(out=xs, in0=xs, scalar=1 + ALPHA, in1=y, op0=ALU.mult, op1=ALU.add))
                dve.sem_inc(tick, 1)

            def x1_src(i):
                norm_chunk((XS,), i)
                logits_chunk(XS, 0, i)

            def spread_sums():
                dve.wait_ge(s_tabw, 16)
                spread_back(S3, D, dend, dstf)
                st.seq(V.tensor_tensor(S3, S3, bc3(c3[:, :], D), ALU.mult))

            stepped_ring_pass(PASS_L0, fill_idx(gin), last_take, 2, x1_src, 8 + 2, x1_src, spread_sums)

            def first_take(i, h):
                st.seq(V.scalar_tensor_tensor(out=cols(XD, i, h, D), in0=slot(h), scalar=1 + ALPHA,
                                              in1=cols(S, i, h, D), op0=ALU.mult, op1=ALU.add))
                dve.sem_inc(tick, 1)

            def x1_dst(i):
                norm_chunk((XD,), i)
                logits_chunk(XD, 1, i)

            stepped_ring_pass(PASS_X_DST, fill_idx(xdi), first_take, 1, x1_dst, 8 + 2, x1_dst)
            st.do(V.tensor_copy(odi[:, :], posf[:, :]))
            st.seq(V.scalar_tensor_tensor(out=z4t[:, :], in0=z4t[:, :], scalar=b_fcb[:, 0:1], in1=e4t[:, :],
                                          op0=ALU.add, op1=ALU.add))
            st.seq(V.scalar_tensor_tensor(out=z4t[:, :], in0=z4t[:, :], scalar=0.2, in1=z4t[:, :], op0=ALU.mult,
                                          op1=ALU.max))

            def row_fill(i, h):
                r = ring[:, h, 0:U * ROW1].rearrange("p (t d) -> p t d", d=ROW1)
                V.tensor_scalar(r[:, :, 0:D], cols(XD, i, h, D).rearrange("p (t d) -> p t d", d=D), 0.0, None, ALU.add)
                V.tensor_scalar(r[:, :, D:D + NH], cols(z4t, i, h, NH).rearrange("p (t d) -> p t d", d=NH), 0.0, None,
                                ALU.add)
                V.tensor_scalar(r[:, :, D + NH:D + NH + 1], cols(srcf, i, h).unsqueeze(2), 0.0, None, ALU.add)
                V.tensor_scalar(r[:, :, D + NH + 1:ROW1], cols(srcf, i, h).unsqueeze(2).to_broadcast([P, U, 3]), 0.0,
                                None, ALU.mult)
                return V.tensor_scalar(ridx[:, h, :], cols(posi, i, h), 0.0, None, ALU.add)

            stepped_ring_pass(PASS_ROW, row_fill, lambda i, h: None, 0, node_chunk, NODE_STEPS, node_chunk)
            dve.sem_inc(s_sct, 1)
            dve.wait_ge(s_row, 16)

            ksrc = ROWS3[:, :, D + NH]
            st.seq(V.tensor_scalar(ks[:, :], ksrc, 0.0, None, ALU.add))
            segments(ks, smask, sfirst, scar, sbak, neg=sneg, n=5)
            st.do(V.tensor_scalar(send[:, 0:T - 1], smask[:, 1:T], -1.0, 1.0, ALU.mult, ALU.add))
            st.do(V.tensor_reduce(bm[:, :], scar[:, :], AX.X, ALU.max))
            st.wait()
            st.seq(V.tensor_scalar(send[:, T - 1:T], bm[:, :], -1.0, 1.0, ALU.mult, ALU.add))
            st.seq(V.tensor_scalar(t1[:, :], smask[:, :], 1.0, BIG, ALU.subtract, ALU.mult))
            zlog = ROWS3[:, :, D:D + NH]
            for h in range(NH):
                st.do(V.tensor_tensor_scan(e43[:, :, h], t1[:, :], zlog[:, :, h], -BIG, ALU.add, ALU.max))
            st.wait()
            st.seq(V.tensor_scalar(tl[:, 0:NH], e43[:, T - 1, :], 0.0, None, ALU.add))
            dve.sem_inc(s_trw, 1)
            dve.wait_ge(s_tr, 7)
            st.seq(V.tensor_tensor(prod[:, :].rearrange("p (h m) -> p h m", h=NH),
                                   bank[4][:, :].rearrange("p (h m) -> p h m", h=NH), mid(sneg[:, :], NH), ALU.add))
            st.seq(V.tensor_reduce(car[:, 0:NH], prod[:, :].rearrange("p (h m) -> p h m", h=NH), AX.X, ALU.max))
            st.seq(V.tensor_scalar(t1[:, :], sfirst[:, :], 1.0, BIG, ALU.subtract, ALU.mult))
            for h in range(NH):
                st.do(V.scalar_tensor_tensor(out=e43[:, :, h], in0=t1[:, :], scalar=car[:, h:h + 1], in1=e43[:, :, h],
                                             op0=ALU.add, op1=ALU.max))
            st.wait()
            spread_back(e43, NH, send, ks)
            st.seq(V.tensor_tensor(z43, zlog, e43, ALU.subtract))
            dve.sem_inc(s_ei, 1)
            dve.wait_ge(s_eo, 1)
            segment_sums(z43, e43, NH, smask, sfirst)
            spread_back(e43, NH, send, ks)
            st.seq(V.reciprocal(e4t[:, :], e4t[:, :]))
            st.seq(V.tensor_tensor(z43, z43, e43, ALU.mult))
            dve.sem_inc(s_hpu, CREDIT)
            dve.sem_inc(s_grp, 1)

            def head_sum(g, b):
                dve.sem_inc(tick, 1)
                st.do(V.tensor_reduce(Y[:, bass.ds(g * (GT * D), GT * D)].rearrange("p (t o) -> p t o", o=D),
                                      prods[:, b, :].rearrange("p (t h o) -> p t o h", h=NH, o=D), AX.X, ALU.add))

            with st.loop(ROUNDS, 2 * RG) as i:
                for j in range(RG):
                    g, b = i * RG + j, j % 2
                    dve.wait_ge(s_hp, done(g))
                    dve.sem_inc(tick, 1)
                    att = z4t[:, bass.ds(g * (GT * NH), GT * NH)]
                    st.wait()
                    st.do(V.tensor_tensor(prods[:, b, :].rearrange("p (th o) -> p th o", o=D),
                                          bank[6 + b][:, :].rearrange("p (th o) -> p th o", o=D),
                                          att.unsqueeze(2).to_broadcast([P, GT * NH, D]), ALU.mult))
                    if j:
                        head_sum(g - 1, 1 - b)
                        st.wait(1)
                        dve.sem_inc(s_hpu, 1)
                    else:
                        st.wait()
                        dve.sem_inc(s_hpu, 1)
                head_sum(i * RG + (RG - 1), (RG - 1) % 2)
                st.wait()
            segment_sums(Y3, S3, D, smask, sfirst)
            dve.sem_inc(s_tab, 1)

            def add_take(dest):
                def take(i, h):
                    st.do(V.tensor_tensor(cols(dest, i, h, D), cols(dest, i, h, D), slot(h), ALU.add))
                    st.wait()
                    dve.sem_inc(tick, 1)
                return take

            def x2_chunk(t, first, nodes=True):
                def work(i):
                    st.seq(V.tensor_tensor(chunk(t, i), chunk(t, i), mid(b_bias[:, :], RC), ALU.add))
                    norm_chunk((t,), i, rr if t is XS else None)
                    if t is XS:
                        hi, lo = (chunk16(i)[:, :, k, :] for k in range(2))
                        st.seq(V.tensor_scalar(hi, chunk(t, i), 0.0, None, ALU.add))
                        st.seq(V.tensor_tensor(lo, chunk(t, i), hi, ALU.subtract))
                    if nodes:
                        node_chunk(i + first)
                return work

            chunk16 = lambda i: S.bitcast(F16)[:, bass.ds(i * (RC * 2 * D), RC * 2 * D)].rearrange(
                "p (t k d) -> p t k d", k=2, d=D)

            stepped_ring_pass(PASS_ATT_SRC, fill_idx(gout_s), add_take(XS), 1, x2_chunk(XS, ROUNDS), 17 + NODE_STEPS,
                              x2_chunk(XS, ROUNDS), lambda: dve.wait_ge(s_tabw, 32))
            stepped_ring_pass(PASS_ATT_DST, fill_idx(gout_d), add_take(XD), 1, x2_chunk(XD, 2 * ROUNDS),
                              9 + NODE_STEPS, x2_chunk(XD, 0, nodes=False))
            assert CH == 3 * ROUNDS - 1
            def relation_groups(i):
                rel = chunk(RB, i, RW)[:, :, NB:RW]
                st.seq(V.tensor_tensor(rel, rel, mid(b_b2[:, :], RC), ALU.add))
                pr3 = pr2[:, :].rearrange("p (t o) -> p t o", t=GT)
                pq3 = pq2[:, :].rearrange("p (t o) -> p t o", t=GT)
                for j in range(RG):
                    g, b = i * RG + j, j % 2
                    xh = bank[6 + b][:, 0:256].rearrange("p (t o) -> p t o", t=GT)
                    yh = bank[6 + b][:, 256:256 + P].rearrange("p (t o) -> p t o", t=GT)
                    relg = RB[:, bass.ds(g * (GT * RW), GT * RW)].rearrange("p (t o) -> p t o", t=GT)

                    def basis_mult(c):
                        dve.wait_ge(s_msg, g * GT + (c + 1 + MSG0))
                        dve.sem_inc(tick, 1)
                        st.do(V.tensor_tensor(prods[:, c % 2, :].rearrange("p (b o) -> p b o", b=NB),
                                              bank[c][:, :].rearrange("p (b o) -> p b o", b=NB),
                                              relg[:, c, 0:NB].unsqueeze(2).to_broadcast([P, NB, D]), ALU.mult))

                    def basis_sum(c):
                        dve.sem_inc(tick, 1)
                        st.do(V.tensor_reduce(Y[:, bass.ds(g * (GT * D) + c * D, D)],
                                              prods[:, c % 2, :].rearrange("p (b o) -> p o b", b=NB), AX.X, ALU.add))

                    dve.wait_ge(s_xy, g + 1)
                    dve.sem_inc(tick, 1)
                    st.do(V.tensor_tensor(pr3, xh[:, :, 0:D], mid(b_b1[:, :], GT), ALU.add))
                    st.do(V.tensor_tensor(pq3, yh, relg[:, :, NB:RW], ALU.add))
                    st.wait(2)
                    basis_mult(0)
                    st.wait(1)
                    dve.sem_inc(s_xyu, 1)
                    st.do(V.tensor_tensor(pr3, pr3, pq3, ALU.mult))
                    basis_mult(1)
                    st.wait(2)
                    dve.sem_inc(s_msgu, 1)
                    basis_sum(0)
                    st.wait(2)
                    dve.sem_inc(tick, 1)
                    st.do(V.tensor_reduce(sc4[:, :], pr3, AX.X, ALU.add))
                    st.wait(1)
                    dve.sem_inc(s_msgu, 1)
                    basis_mult(2)
                    basis_sum(1)
                    st.wait(2)
                    st.do(V.tensor_scalar(t1[:, bass.ds(g * GT, GT)], sc4[:, :], 1.0 / D ** 0.5, 0.0, ALU.mult, ALU.max))
                    st.wait(1)
                    dve.sem_inc(s_msgu, 1)
                    basis_mult(3)
                    basis_sum(2)
                    st.wait(1)
                    dve.sem_inc(s_msgu, 1)
                    basis_sum(3)

            dve.sem_inc(s_xyu, CREDIT)
            dve.sem_inc(s_msgu, GT)
            dve.sem_inc(s_grp, 1)
            stepped_ring_pass(PASS_REL, fill_idx(etyi), copy_take(RB, RW), 1, relation_groups, 1 + 13 * RG,
                              relation_groups)
            dve.wait_ge(s_self, NG + 2)
            st.do(V.memset(tl[:, 0:1], 0.0))
            st.wait()
            dve.sem_inc(s_ei, 1)
            dve.wait_ge(s_eo, 2)
            st.seq(V.tensor_tensor(Y3, Y3, bc3(t1[:, :], D), ALU.mult))
            segment_sums(Y3, Y3, D, dmask, dfirst)
            st.seq(V.tensor_tensor(S[:, :], S[:, :], Y[:, :], ALU.add))
            st.seq(V.tensor_scalar(S[:, :], S[:, :], 0.0, None, ALU.max))
            dve.sem_inc(s_tab, 1)
            def x3_chunk(i):
                st.seq(V.tensor_tensor(chunk(XD, i), chunk(XD, i), chunk(S, i), ALU.add))
                norm_chunk((XS, XD), i)
                st.seq(V.tensor_tensor(chunk(Y, i), chunk(XS, i), cols2(ew, i).unsqueeze(2).to_broadcast([P, RC, D]),
                                       ALU.mult))

            stepped_ring_pass(PASS_RGCN, fill_idx(gin), add_take(XS), 1, x3_chunk, 2 + 13, x3_chunk,
                              lambda: dve.wait_ge(s_oslot, 2 * ROUNDS))
            dve.wait_ge(s_tabw, 48)
            segment_sums(Y3, S3, D, dmask, dfirst)

            def out_fill(rows, idx):
                def fill(i, h):
                    V.tensor_scalar(slot(h), cols(rows, i, h, D), 0.0, None, ALU.add)
                    return V.tensor_scalar(ridx[:, h, :], cols(idx, i, h), 0.0, None, ALU.add)
                return fill

            def out_dst(i):
                st.seq(V.scalar_tensor_tensor(out=chunk(XD, i), in0=chunk(XD, i), scalar=2.0, in1=chunk(S, i),
                                              op0=ALU.mult, op1=ALU.add))
                norm_chunk((XD,), i)

            stepped_ring_pass(PASS_OUT_DST, out_fill(XD, odi), lambda i, h: None, 0, extra=9, before_fill=out_dst)

        @block.scalar
        def _(act):
            A = nc.scalar
            tick = s_tick[1]

            def act_pass(n, idx, dest, w):
                ring_pass(act, tick, n,
                          lambda i, h: A.activation(ridx[:, h, :], cols(idx, i, h), ACT.Copy),
                          lambda i, h: A.activation(cols(dest, i, h, w), ring[:, h, 0:U * w], ACT.Copy))

            act.wait_ge(s_ids, 1)
            act_pass(PASS_X_SRC, xsi, XS, D)
            def copy_transposed(i, b):
                act.wait_ge(s_ohT, i + 1)
                act.sem_inc(tick, 1)
                for k in range(2):
                    last = A.activation(ohaT[b][:, 2 * k:2 * k + 2, :].rearrange("p j n -> p (j n)"),
                                        bank[2 + k][:, :].bitcast(F16), ACT.Copy)
                last.then_inc(s_ohTc, 1)

            copy_transposed(0, 0)
            with act.Fori(0, NG // 2) as k:
                for b in range(2):
                    i = k * 2 + b
                    act.wait_ge(s_ru, i + 1)
                    act.sem_inc(tick, 1)
                    for m in range(2):
                        last = A.activation(rhi[1 - b][:, 2 * m:2 * m + 2, :].rearrange("p c n -> p (c n)"),
                                            bank[m][:, :], ACT.Copy)
                    last.then_inc(s_rhi, 1)
                    copy_transposed(i + 1, 1 - b)
            act.wait_ge(s_sri, 1)
            A.activation(t1[:, :], t1[:, :], ACT.Sqrt)
            A.activation(t2[:, :], t2[:, :], ACT.Sqrt)
            A.activation(c3[:, :], c3[:, :], ACT.Sqrt).then_inc(s_sro, 1)

            n_roots = 0

            def take_roots(kinds, count):
                nonlocal n_roots
                with act.Fori(0, count) as k:
                    for m, kind in enumerate(kinds):
                        act.wait_ge(s_ri, k * len(kinds) + (n_roots + m + 1))
                        act.sem_inc(tick, 1)
                        A.activation(roots[:, :], roots[:, :], ACT.Sqrt, scale=ROOTS[kind][0] / D,
                                     bias=eps_t[kind][:, 0:1]).then_inc(s_dve, 1)
                n_roots += count * len(kinds)

            node_kinds = ("first", "all")
            take_roots(("norm",), 2 * ROUNDS)
            take_roots(node_kinds, ROUNDS)

            edges_g = lambda t3_, g: t3_[:, bass.ds(g * GT, GT), 0:D]

            def stage(k, t3_, g, j):
                act.wait_ge(s_xtp[k], free(g, j))
                act.sem_inc(tick, 1)
                if k == 1:
                    A.activation(xs16[:, j % 2, :].rearrange("p (t r m) -> p t r m", r=2, m=2 * D),
                                 S.bitcast(F16)[:, bass.ds(g * (GT * 2 * D), GT * 2 * D)].rearrange(
                                     "p (t m) -> p t m", m=2 * D).unsqueeze(2).to_broadcast([P, GT, 2, 2 * D]), ACT.Copy)
                A.activation(xg[:, j % 2, :].rearrange("p (t d) -> p t d", d=D), edges_g(t3_, g),
                             ACT.Copy).then_inc(s_stg[k], 1)

            act.wait_ge(s_ei, 1)
            A.activation(z4t[:, :], z4t[:, :], ACT.Exp).then_inc(s_eo, 1)
            act.wait_ge(s_grp, 1)

            act.sem_inc(s_xtc[0], CREDIT)
            stage(0, ROWS3, 0, 0)

            def attention_group(g, j, last):
                if not last:
                    stage(0, ROWS3, g + 1, (j + 1) % RG)
                act.wait_ge(s_xtp[0], done(g))
                act.wait_ge(s_hp, free(g, j))
                act.sem_inc(tick, 1)
                A.activation(xt[:, j % 2, :], bank[j % 2][:, 0:P], ACT.Copy).then_inc(s_xtc[0], 1)

            groups(act, attention_group)
            take_roots(("norm", "all") + node_kinds, ROUNDS)
            take_roots(("norm",) + node_kinds, ROUNDS - 1)
            take_roots(("norm",), 1)
            act.wait_ge(s_grp, 2)
            act.sem_inc(s_xtc[1], CREDIT)
            act.sem_inc(s_self, CREDIT)
            stage(1, XD3, 0, 0)

            def relation_group(g, j, last):
                b = j % 2
                if not last:
                    stage(1, XD3, g + 1, (j + 1) % RG)
                act.wait_ge(s_xtp[1], done(g))
                act.wait_ge(s_msg, free(g, j) * GT)
                act.sem_inc(tick, 1)
                A.activation(x16[:, b, :], bank[4 + b][:, 0:256].bitcast(F16), ACT.Copy)
                A.activation(xt[:, b, :], bank[4 + b][:, 256:256 + P], ACT.Copy).then_inc(s_xtc[1], 1)
                act.wait_ge(s_xyu, done(g))
                act.sem_inc(tick, 1)
                A.activation(S[:, bass.ds(g * (GT * D), GT * D)].rearrange("p (t o) -> p t o", t=GT),
                             bank[6 + b][:, 0:256].rearrange("p (t o) -> p t o", t=GT)[:, :, D:2 * D],
                             ACT.Copy).then_inc(s_self, 1)

            def out_src_fill(slot_, b):
                for t in range(U):
                    A.activation(oring[b][:, t * D:(t + 1) * D], XS[:, bass.ds(slot_ * (U * D) + t * D, D)], ACT.Copy,
                                 scale=rr[:, bass.ds(slot_ * U + t, 1)])
                A.activation(oidx[:, b, :], osi[:, bass.ds(slot_ * U, U)], ACT.Copy).then_inc(s_oslot, 1)

            def out_src_round(i):
                act.wait_ge(s_oland[0], i * (16 * U) + 16 * U)
                act.sem_inc(tick, 1)
                out_src_fill(i + 1, 0)

            out_src_fill(0, 0)
            groups(act, relation_group, out_src_round)
            out_src_fill(ROUNDS, 1)
            act.wait_ge(s_ei, 2)
            A.activation(t1[:, :], t1[:, :], ACT.Tanh).then_inc(s_eo, 1)
            with act.Fori(0, (ROUNDS - 1) // 2) as k:
                for b in range(2):
                    act.wait_ge(s_oland[b], k * (16 * U) + (1 if b else ROUNDS) * 16 * U)
                    act.sem_inc(tick, 1)
                    out_src_fill(k * 2 + (ROUNDS + 1 + b), b)
            take_roots(("norm",), 2 * ROUNDS)

        @block.tensor
        def _(pe):
            M = nc.tensor
            tick = s_tick[3]
            pe.wait_ge(s_cst2, 1)
            for c in range(NA_CH):
                last = M.matmul(bank[c][:, :], ident_h[:, :], zh[:, :], start=True, stop=False)
            last.then_inc(s_ohu, 4)
            with pe.Fori(0, NG) as i:
                for j in range(4):
                    pe.wait_ge(s_oh, i * 4 + j + 1)
                    pe.sem_inc(tick, 1)
                    for c in range(NA_CH):
                        M.matmul(bank[c][:, 0:NB_COL], oha[:, j, c * P:(c + 1) * P], ohb[:, j, :], start=False, stop=False)
                        last = M.matmul(bank[c][:, NB_COL:2 * NB_COL], oha2[:, j, c * P:(c + 1) * P], ohb2[:, j, :],
                                        start=False, stop=False)
                    last.then_inc(s_ohu, 1)
            for c in range(NA_CH):
                last = M.matmul(bank[c][:, :], ident_h[:, :], zh[:, :], start=False, stop=True)
            last.then_inc(s_hist, 1)
            pe.wait_ge(s_tot, 1)
            tk = tot[:, :, :].rearrange("p k c -> p (k c)")
            M.matmul(bank[4][:, 0:2 * NA_CH], up[:, :], tk, start=True, stop=True)
            M.matmul(bank[5][:, 0:2 * NA_CH], ones[:, :], tk, start=True, stop=True).then_inc(s_base, 1)

            pe.wait_ge(s_nt, 1)
            for b in range(2):
                last = M.matmul(bank[b][:, :], ident_h[:, :], zh[:, :], start=True, stop=True, skip_group_check=True)
            chunk = lambda c: bank[c // 2][:, (c % 2) * NB_COL:(c % 2 + 1) * NB_COL]

            def rank_transposes(i, b):
                pe.wait_ge(s_oh, i + (T + 1))
                pe.wait_ge(s_eq, i + (1 if isinstance(i, int) else 0))
                pe.sem_inc(tick, 1)
                for j in range(4):
                    for c in range(NA_CH):
                        n = (j % 2) * AW + c * P
                        last = M.transpose(bank[2 + j // 2][:, :].bitcast(F16)[:, n:n + P],
                                           ohas[b][:, j, c * P:(c + 1) * P], ident_h[:, :])
                last.then_inc(s_ohT, 1)
                for j in range(4):
                    last = M.transpose(bank[4 + 3 * b][:, j * P:(j + 1) * P],
                                       kcol[:, b, j:j + 1].to_broadcast([P, P]), ident[:, :])
                last.then_inc(s_kt, 1)

            def rank_counts(i, b):
                pe.wait_ge(s_rc, i + 1)
                pe.sem_inc(tick, 1)
                for j in range(4):
                    for c in range(NA_CH):
                        last = M.matmul(chunk(c), ohas[b][:, j, c * P:(c + 1) * P], ohbs[b][:, j, :], start=False,
                                        stop=j == 3, skip_group_check=True)
                last.then_inc(s_ru, 1)
                pe.wait_ge(s_ohTc, i + 1)
                pe.wait_ge(s_gu, i + 1)
                pe.sem_inc(tick, 1)
                for j in range(4):
                    g = bank[5 + j // 2][:, (j % 2) * NB_COL:(j % 2 + 1) * NB_COL]
                    for c in range(NA_CH):
                        for m, part in enumerate((rhi, rlo)):
                            last = M.matmul(g, ohaT[b][:, j, c * P:(c + 1) * P], part[b][:, c, :],
                                            start=c == 0 and m == 0, stop=c == NA_CH - 1 and m == 1)
                last.then_inc(s_g, 1)

            rank_transposes(0, 0)
            with pe.Fori(0, NG // 2) as k:
                for b in range(2):
                    rank_counts(k * 2 + b, b)
                    rank_transposes(k * 2 + (b + 1), 1 - b)
            rank_counts(NG - 1, 0)

            def key_rows(n):
                pe.wait_ge(s_trw, n)
                M.transpose(bank[4][:, 0:P], tl[:, 0:1].to_broadcast([P, P]), ident[:, :])
                M.transpose(bank[5][:, 0:P], tl[:, 1:2].to_broadcast([P, P]), ident[:, :]).then_inc(s_tr, 1)

            def carry(link, width, n):
                pe.wait_ge(s_tail, n)
                M.matmul(bank[7][:, 0:width], link[:, :], tl[:, 0:width], start=True, stop=True).then_inc(s_carry, 1)

            def column_row(n):
                pe.wait_ge(s_trw, n)
                M.transpose(bank[4][:, 0:P], tl[:, 0:1].to_broadcast([P, P]), ident[:, :]).then_inc(s_tr, 1)

            key_rows(1)
            carry(dcar, D, 1)
            column_row(2)
            column_row(3)
            carry(dcar, D, 2)
            column_row(4)
            column_row(5)
            carry(dcar, D, 3)
            with pe.Fori(0, K_STEPS - 4) as k:
                pe.wait_ge(s_tail, k + 4)
                pe.sem_inc(tick, 1)
                M.matmul(bank[7][:, 0:D], dcar[:, :], tl[:, :], start=True, stop=True).then_inc(s_carry, 1)
            carry(dcar, D, K_STEPS)
            pe.wait_ge(s_wb, 1)
            M.matmul(bank[6][:, 0:2 * NH * D], ones[0:D, :], udiag[:, :], start=True, stop=True).then_inc(s_mm, 1)
            carry(dbak, D, K_STEPS + 1)


            key_rows(6)
            pe.wait_ge(s_trw, 7)
            for h in range(NH):
                last = M.transpose(bank[4][:, h * P:(h + 1) * P], tl[:, h:h + 1].to_broadcast([P, P]), ident[:, :])
            last.then_inc(s_tr, 1)
            carry(sbak, NH, K_STEPS + 2)
            carry(scar, NH, K_STEPS + 3)
            carry(sbak, NH, K_STEPS + 4)
            pe.wait_ge(s_grp, 1)
            pe.sem_inc(s_xtp[0], CREDIT)
            pe.sem_inc(s_hp, CREDIT)

            def attention_transpose(g, j):
                pe.wait_ge(s_stg[0], g + 1)
                pe.wait_ge(s_xtc[0], free(g, j))
                pe.sem_inc(tick, 1)
                M.transpose(bank[j % 2][:, 0:P], xg[:, j % 2, :], ident[:, :]).then_inc(s_xtp[0], 1)

            def attention_group(g, j, last):
                if not last:
                    attention_transpose(g + 1, (j + 1) % RG)
                pe.wait_ge(s_xtc[0], done(g))
                pe.wait_ge(s_hpu, free(g, j))
                pe.sem_inc(tick, 1)
                M.matmul(bank[6 + j % 2][:, :], xt[:, j % 2, :], bd1[:, :], start=True, stop=True).then_inc(s_hp, 1)

            attention_transpose(0, 0)
            groups(pe, attention_group)
            carry(scar, D, K_STEPS + 5)

            pe.wait_ge(s_grp, 2)
            pe.sem_inc(s_xtp[1], CREDIT)
            pe.sem_inc(s_msg, MSG0)

            def relation_transpose(g, j):
                b = j % 2
                pe.wait_ge(s_stg[1], g + 1)
                pe.wait_ge(s_xtc[1], free(g, j))
                pe.sem_inc(tick, 1)
                for c in range(GT):
                    M.transpose(bank[4 + b][:, 0:256].bitcast(F16)[:, c * P:(c + 1) * P],
                                xs16[:, b, c * P:(c + 1) * P], ident_h[:, :])
                M.transpose(bank[4 + b][:, 256:256 + P], xg[:, b, :], ident[:, :]).then_inc(s_xtp[1], 1)

            def relation_group(g, j, last):
                b = j % 2
                if not last:
                    relation_transpose(g + 1, (j + 1) % RG)
                pe.wait_ge(s_xtc[1], done(g))
                pe.wait_ge(s_self, free(g, j))
                pe.sem_inc(tick, 1)
                for c in range(GT):
                    M.matmul(bank[6 + b][:, c * 2 * D:(c + 1) * 2 * D], x16[:, b, c * P:(c + 1) * P],
                             w16[:, NB * D:(NB + 2) * D], start=True, stop=True)
                M.matmul(bank[6 + b][:, 256:256 + P], xt[:, b, :], bdy[:, :], start=True, stop=True).then_inc(s_xy, 1)
                for c in range(GT):
                    pe.wait_ge(s_msgu, g * GT + (c + 1))
                    pe.sem_inc(tick, 1)
                    M.matmul(bank[c][:, :], x16[:, b, c * P:(c + 1) * P], w16[:, 0:NB * D], start=True,
                             stop=True).then_inc(s_msg, 1)

            relation_transpose(0, 0)
            groups(pe, relation_group)
            carry(dcar, D, K_STEPS + 6)
            carry(dcar, D, K_STEPS + 7)


_INS = ['x', 'src', 'dst', 'edge_type_86', 'edge_weight', 'L1_gnn_w', 'L1_gnn_fc_w', 'L1_gnn_fc_b', 'L1_gnn_bias',
        'L2_gnn_weight', 'L2_gnn_w_comp', 'L2_gnn_self_loop_weight', 'L2_gnn_A1_w', 'L2_gnn_A1_b', 'L2_gnn_A2_w',
        'L2_gnn_A2_b', 'L2_gnn_rel_emb']
_OUTS = [((100000, 32), 'float32')]


def kernel(**inputs):
    import numpy as _np
    import concourse.bacc as _bacc
    from concourse import mybir as _mybir
    from concourse.bass_utils import run_bass_kernel_spmd as _run

    nc = _bacc.Bacc("TRN2", target_bir_lowering=False, num_devices=1)
    arrays, args = {}, []
    for name in _INS:
        a = _np.ascontiguousarray(inputs[name])
        arrays[f"in_{name}_dram"] = a
        args.append(nc.dram_tensor(f"in_{name}_dram", a.shape, _mybir.dt.from_np(a.dtype), kind="ExternalInput").ap())
    for i, (shape, dtype) in enumerate(_OUTS):
        dt = _mybir.dt.from_np(_np.dtype(dtype))
        args.append(nc.dram_tensor(f"out_{i}_dram", shape, dt, kind="ExternalOutput").ap())
    gnn_resnorm(nc, *args)
    r = _run(nc, [arrays], core_ids=[0])
    return r.results[0]["out_0_dram"]
```

```python
from contextlib import ExitStack, contextmanager

import concourse.bass as bass
from concourse import mybir

ALU = mybir.AluOpType
ACT = mybir.ActivationFunctionType
AX = mybir.AxisListType
F32 = mybir.dt.float32
F16 = mybir.dt.float16
I32 = mybir.dt.int32

P = 128
BIG = 1.0e30
EPS = 1e-5


class Steps:

    def __init__(self, eng, sem, trips=None):
        self.eng, self.sem, self.n, self.off, self.trips, self.dyn = eng, sem, 0, None, trips, 0

    def plus(self, a, b):
        return b if a is None else a + b

    def do(self, ins):
        ins.then_inc(self.sem, 1)
        self.n += 1

    def wait(self, behind=0):
        v = self.off
        if self.dyn:
            v = self.plus(v, self.trips * self.dyn)
        self.eng.wait_ge(self.sem, self.plus(v, self.n - behind))

    def seq(self, ins):
        self.do(ins)
        self.wait()

    @contextmanager
    def loop(self, count, per, dyn=0):
        start, dstart, outer = self.n, self.dyn, self.off
        with self.eng.Fori(0, count) as i:
            self.off = self.plus(outer, i * per if not dyn else i * self.trips * dyn + i * per)
            yield i
            assert (self.n - start, self.dyn - dstart) == (per, dyn), f"a round has {self.n - start}, {self.dyn - dstart}"
            self.off = outer
        self.n, self.dyn = start + per * count, dstart + dyn * count

    @contextmanager
    def trip_loop(self, per):
        start, outer = self.n, self.off
        with self.eng.Fori(0, self.trips) as i:
            self.off = self.plus(outer, i * per)
            yield i
            assert self.n - start == per, f"a round has {self.n - start} steps"
            self.off = outer
        self.n, self.dyn = start, self.dyn + per


def gnn_resnorm(nc, x, src, dst, etype, eweight, w1, fc_w, fc_b, bias1, w2, w_comp, w_self, A1w, A1b, A2w, A2b,
                rel_emb, out):
    N, D = x.shape
    E = src.shape[0]
    T = -(-E // P)
    EP = P * T
    LASTV = E - (P - 1) * T
    NH = w1.shape[0]
    NB = w2.shape[0]
    NR = w_comp.shape[0]
    NB_COL = 256
    NA_CH = -(-(N + 1) // (NB_COL * P))
    NT_ROWS = NA_CH * P * NB_COL
    CU = 4
    CW = 200
    LW = CW + 2 * CU
    TW = D + 4
    ZERO_DMAS = 11
    ZROW = P * CW
    U = 14
    ROUNDS = T // (2 * U)
    LAND = 16 * U
    RW = 48
    ROW1 = 40
    K_STEPS = 10
    ALPHA = 0.1
    OOB = 2 * N
    NODE_P = 125
    NROWS = N // NODE_P
    CH = 20
    CR = NROWS // CH
    GT = 4
    NG = T // GT
    assert K_STEPS - 4 == ROUNDS - 1 and T % (2 * U) == 0 and T % GT == 0 and D == 32 and NROWS % CH == 0 and NG % 2 == 1

    ctx = ExitStack()
    with ctx:
        sb = lambda name, shape, dt=F32: ctx.enter_context(nc.sbuf_tensor(name, shape, dt))
        sem = lambda name: ctx.enter_context(nc.semaphore(name))

        nt_d = nc.dram_tensor("node_table", (NT_ROWS, 4), F32).ap()
        agg_d = nc.dram_tensor("appnp_table", (ZROW + 1, D), F32).ap()
        att_d = nc.dram_tensor("attention_table", (ZROW + 1, D), F32).ap()
        rgcn_d = nc.dram_tensor("rgcn_table", (ZROW + 1, D), F32).ap()
        full_d = nc.dram_tensor("sums_by_edge", (ZROW + 1, TW), F32).ap()
        list_d = [nc.dram_tensor("sums_by_list0", (ZROW + 1, TW), F32).ap(),
                  nc.dram_tensor("sums_by_list1", (ZROW + 1, D), F32).ap()]
        pay_d = [nc.dram_tensor(f"payload{v}", (ZROW + 1, 4), F32).ap() for v in range(2)]
        exp_d = [nc.dram_tensor(f"list{v}_values_by_edge", (EP, D), F32).ap() for v in range(2)]
        rel_d = nc.dram_tensor("relation_table", (NR, RW), F32).ap()
        row_d = nc.dram_tensor("rows_by_src", (EP, ROW1), F32).ap()

        bank = [ctx.enter_context(nc.psum_tensor(f"bank{i}", [P, 512], F32)) for i in range(8)]

        XS = sb("XS", [P, T * D])
        XD, YW, SW = sb("XD", [P, T * D]), sb("YW", [P, CW * D]), sb("SW", [P, CW * D])
        Y, S = YW[:, 0:T * D], SW[:, 0:T * D]
        RB = sb("RB", [P, T * RW])
        RC0 = 2 * U
        v3 = lambda t, w=D: t.rearrange("p (t d) -> p t d", d=w)
        XS3, XD3, Y3, S3 = v3(XS[:, :]), v3(XD[:, :]), v3(Y[:, :]), v3(S[:, :])
        ROWS = RB[:, 0:T * ROW1]
        ROWS3 = v3(ROWS, ROW1)
        ring = sb("ring", [P, 2, U * RW])
        ridx = sb("ridx", [P, 2, U], I32)

        e_i = lambda name: sb(name, [P, T], I32)
        e_f = lambda name: sb(name, [P, T], F32)
        srci, dsti, etyi = e_i("srci"), e_i("dsti"), e_i("etyi")
        ew = e_f("ew")
        srcf, dstf = e_f("srcf"), e_f("dstf")
        tmpi = e_i("tmpi")
        a_s, b_s, a_d, b_d = e_f("a_s"), e_f("b_s"), e_f("a_d"), e_f("b_d")
        xsi, xdi = e_i("xsi"), e_i("xdi")
        gin, gout_s, gout_d, posi = e_i("gin"), e_i("gout_s"), e_i("gout_d"), e_i("posi")
        osi, odi = xsi, xdi
        c1, c2, c3, ginf = e_f("c1"), e_f("c2"), e_f("c3"), b_s
        t1w = sb("t1w", [P, CW])[:, :]
        posf = e_f("posf")
        q_f = e_f("q_f")
        dmask, dfirst, dend = e_f("dmask"), e_f("dfirst"), e_f("dend")
        smask, sfirst, send, ks = a_s, b_s, a_d, b_d
        t1, t2, t3 = e_f("t1"), e_f("t2"), e_f("t3")

        iota_h = sb("iota_h", [P, NA_CH * P], F16)
        ident = sb("ident", [P, P])
        ident_h = sb("ident_h", [P, P], F16)
        up = sb("up", [P, P])
        low = sb("low", [P, P])
        ones = sb("ones", [P, P])
        dcar, dbak = sb("dcar", [P, P]), sb("dbak", [P, P])
        scar, sbak = sb("scar", [P, P]), sb("sbak", [P, P])
        sneg = sb("sneg", [P, P])
        zrow = sb("zrow", [P, TW])
        ROOTS = {"norm": (1.0, EPS), "first": (1.0, EPS / (1 + ALPHA) ** 2), "all": (1 + EPS * (1 + EPS) / 4, EPS ** 3 / 4)}
        eps_t = {kind: sb(f"eps_{kind}", [P, 1]) for kind in ROOTS}

        AW = NA_CH * P
        halves, at = YW[:, :].bitcast(F16), 0

        def half(n):
            nonlocal at
            at += 4 * n
            return halves[:, at - 4 * n:at].rearrange("p (j n) -> p j n", j=4)

        oha, ohb, oha2, ohb2 = half(AW), half(NB_COL), half(AW), half(NB_COL)
        junk = YW[:, at // 2:at // 2 + 10 * P + 4 * NB_COL]
        emask = YW[:, at // 2 + junk.shape[1]:at // 2 + junk.shape[1] + 4 * P]
        assert at // 2 + junk.shape[1] + 4 * P <= CW * D and at // 2 + junk.shape[1] >= 4 * NA_CH * NB_COL
        halves, at = SW[:, :].bitcast(F16), 16 * T
        ohaT, rhi, rlo = [half(AW), half(AW)], [half(NB_COL), half(NB_COL)], [half(NB_COL), half(NB_COL)]
        assert at <= 2 * CW * D
        ohas, ohbs = (oha, oha2), (ohb, ohb2)
        zh = sb("zh", [P, 512], F16)
        cnt4 = sb("cnt4", [P, 4])
        rk4 = sb("rk4", [P, 4])
        kcol = sb("kcol", [P, 2, 4])
        z4w, e4w = sb("z4w", [P, CW * 4]), sb("e4w", [P, CW * 4])
        PAY = [z4w, e4w]
        Z0 = RB[:, 0:CW * TW].rearrange("p (j w) -> p j w", w=TW)
        FULL = RB[:, 0:T * TW].rearrange("p (j w) -> p j w", w=TW)
        lists = RB[:, CW * TW:CW * TW + 10 * LW].rearrange("p (k j) -> p k j", k=10)
        assert CW * TW + 10 * LW <= T * RW
        lkey, lval, lmask, lfirst, lnext, lact, lcnt = (lists[:, k, :] for k in range(7))
        lidx, lidx2, lq = (lists[:, k, :].bitcast(I32) for k in range(7, 10))
        cring = sb("cring", [P, 2, CU * TW])
        pring, pidx = sb("pring", [P, 2, U * 4]), sb("pidx", [P, 2, U], I32)
        cidx = sb("cidx", [P, 2, CU], I32)
        y4 = sb("y4", [P, CU, D])
        zr = sb("zr", [P, CU + 1, D])
        oring, oidx = (z4w[:, 0:U * D], e4w[:, 0:U * D]), sb("oidx", [P, 2, U], I32)
        rr = c1
        vs, rs = sb("vs", [P, RC0]), sb("rs", [P, RC0])
        m8 = sb("m8", [P, 8])
        ramp_c = sb("ramp_c", [P, LW])
        tm = sb("tm", [P, 1])
        pb = sb("pb", [P, 2])
        trips_i = [sb(f"trips{v}", [P, 1], I32) for v in range(2)]
        zrow4 = sb("zrow4", [1, 4])
        dneg = sb("dneg", [P, P])
        tot = sb("tot", [P, 2, NA_CH])
        base = sb("base", [P, 2, NA_CH])
        TB = NA_CH * NB_COL
        HC, IC = Y[:, 0:2 * TB], Y[:, 2 * TB:4 * TB]
        NTB = RB[:, 0:4 * TB]
        z4t, e4t = z4w[:, 0:T * NH], e4w[:, 0:T * NH]
        z43, e43 = v3(z4t[:, :], NH), v3(e4t[:, :], NH)
        NS3 = v3(S[:, 0:4 * T], 4)

        wcat = sb("wcat", [P, NH * D])
        wsd = sb("wsd", [P, 2 * D])
        ua = sb("ua", [P, 2, NH])
        udiag = sb("udiag", [D, 2 * NH * D])
        bd1 = sb("bd1", [P, GT * NH * D])
        bdy = sb("bdy", [P, GT * D])
        wf = sb("wf", [P, NB * D])
        w16 = sb("w16", [P, (NB + 2) * D], F16)
        aw = sb("aw", [P, 3 * D])
        b_bias, b_b1, b_b2 = sb("b_bias", [P, D]), sb("b_b1", [P, D]), sb("b_b2", [P, D])
        b_fcb = sb("b_fcb", [P, 1])
        bc = sb("bc", [P, D])
        bm = sb("bm", [P, 1])
        xt = sb("xt", [P, 2, P])
        x16 = sb("x16", [P, 2, GT * P], F16)
        xs16 = sb("xs16", [P, 2, GT * P], F16)
        xg = sb("xg", [P, 2, P])
        prods = sb("prods", [P, 2, 512])
        prod = prods[:, 0, :]
        pr2, pq2, sc4 = sb("pr2", [P, GT * D]), sb("pq2", [P, GT * D]), sb("sc4", [P, GT])
        car = sb("car", [P, D])
        tl = sb("tl", [P, D])

        RC = 2 * U
        sq_s = RB[:, 0:2 * RC * D]
        lp_s = RB[:, 2 * RC * D:(2 + NH) * RC * D]
        roots = sb("roots", [P, 2 * RC])
        u_all = sb("u_all", [P, 2 * NH * D])

        nx, nsq = sb("nx", [P, CR * D])[:, :], Y[:, 0:CR * D]
        nr1 = roots[:, 0:CR]
        nx3, nsq3 = v3(nx), v3(nsq)

        s_pad = sem("padding_set")
        s_in = sem("edges_loaded")
        s_w = sem("weights_loaded")
        s_bd = sem("basis_weights_loaded")
        s_relt = sem("relation_table_written")
        s_zr = sem("zero_row_set")
        s_ztab = sem("zero_rows_written")
        s_const = sem("pool_constants_ready")
        s_cst2 = sem("masks_ready")
        s_ids = sem("node_indices_ready")
        s_slot = sem("ring_slot_ready")
        s_land = [[sem(f"landed{f}{h}") for h in range(2)] for f in range(2)]
        s_tick = [sem(f"tick_{e}") for e in ("pool", "act", "dve", "pe", "sp")]
        s_oh = sem("onehots_ready")
        s_ohu = sem("onehots_used")
        s_hist = sem("histogram_done")
        s_tot = sem("totals_ready")
        s_base = sem("bases_ready")
        s_nt = sem("node_table_ready")
        s_ntw = sem("node_table_written")
        s_actp = sem("act_passes_done")
        s_dve = sem("dve_steps")
        s_ohT = sem("onehots_transposed")
        s_ohTc = sem("transposed_copied")
        s_kt = sem("keys_transposed")
        s_g = sem("counts_gathered")
        s_eq = sem("keys_compared")
        s_gu = sem("counts_read")
        s_ru = sem("running_counts_updated")
        s_rhi = sem("high_parts_ready")
        s_rc = sem("low_parts_ready")
        s_tr = sem("row_of_keys_ready")
        s_trw = sem("row_of_keys_wanted")
        s_tail = sem("tails_ready")
        s_carry = sem("carries_ready")
        s_tab = sem("table_tile_ready")
        s_tabw = sem("table_written")
        s_sri = sem("degrees_ready")
        s_sro = sem("degree_roots_ready")
        s_ri = sem("root_wanted")
        s_nin = sem("node_chunk_loaded")
        s_nok = sem("node_chunk_done")
        s_nout = sem("node_chunk_written")
        s_grp = sem("group_source_ready")
        s_mm = sem("attention_vectors_ready")
        s_row = sem("src_rows_loaded")
        s_sct = sem("rows_scattered")
        s_wb = sem("blocks_built")
        s_ei = sem("exponentials_wanted")
        s_eo = sem("exponentials_ready")
        s_lslot = [sem(f"list{v}_slot_ready") for v in range(2)]
        s_lland = [[sem(f"list{v}_landed{h}") for h in range(2)] for v in range(2)]
        s_lst = [sem(f"list{v}_steps") for v in range(2)]
        s_trips = [sem(f"trips{v}_ready") for v in range(2)]
        s_ltab = [sem(f"list{v}_sums_ready") for v in range(2)]
        s_ltabw = [sem(f"list{v}_sums_written") for v in range(2)]
        s_pay = [sem(f"payload{v}_ready") for v in range(2)]
        s_payw = [sem(f"payload{v}_written") for v in range(2)]
        s_oslot, s_oland = sem("out_src_slot_ready"), [sem(f"out_src_written{b}") for b in range(2)]
        s_pfill, s_ptake = sem("own_indices_ready"), sem("own_rows_taken")
        s_pland = [sem(f"own_rows_landed{h}") for h in range(2)]
        s_actgo, s_pay0 = sem("list0_ready_for_act"), sem("list0_rows_taken")
        s_full = sem("sums_by_edge_ready")
        s_fullw = sem("sums_by_edge_written")
        s_expz = sem("zeros_ready")
        s_expzw = sem("zeros_written")
        s_exp = sem("list_values_scattered")
        s_expl = sem("list_values_loaded")
        s_stg = [sem(f"group_staged{k}") for k in range(2)]
        s_xtp = [sem(f"group_transposed{k}") for k in range(2)]
        s_xtc = [sem(f"transposed_group_copied{k}") for k in range(2)]
        s_hp, s_hpu = sem("head_products_ready"), sem("head_products_used")
        s_xy, s_xyu = sem("relation_terms_ready"), sem("relation_terms_used")
        s_self = sem("self_loop_terms_copied")
        s_msg, s_msgu = sem("basis_products_ready"), sem("basis_products_used")

        NODE_STEPS = 14
        block = ctx.enter_context(nc.Block())
        edges = lambda a: a[0:(P - 1) * T].rearrange("(p t) -> p t", t=T)
        edges_last = lambda a: a[(P - 1) * T:E].rearrange("(p t) -> p t", p=1)
        dense = lambda a, w: a[0:EP, :].rearrange("(p t) d -> p (t d)", t=T)

        PASS_X_SRC, PASS_NT_SRC, PASS_X_DST, PASS_L0 = range(4)
        PASS_ROW, PASS_ATT_SRC, PASS_ATT_DST, PASS_REL, PASS_RGCN, PASS_OUT_DST = \
            range(PASS_L0 + 1, PASS_L0 + 7)

        def family(n):
            return (0, n) if n < PASS_ROW else (1, n - PASS_ROW)

        def slot_count(n, i, h):
            return 2 * ROUNDS * n + 2 * i + h + 1

        def land_count(n, i):
            return LAND * (ROUNDS * family(n)[1] + i + 1)

        def list_slot_count(a, b, n):
            return b * 2 + 1 + n_times(n, a, 2)

        def n_times(n, a, per):
            return 0 if isinstance(a, int) and a == 0 else n * a * per

        def list_dma(pool, v, n, a, b, w, table, scatter=False):
            with pool.Fori(0, n) as i:
                for h in range(2):
                    pool.wait_ge(s_lslot[v], i * 2 + (list_slot_count(a, b, n) + h))
                    pool.sem_inc(s_tick[0], 1)
                    for j in range(CU):
                        off = bass.IndirectOffsetOnAxis(ap=cidx[:, h, j:j + 1], axis=0)
                        row = cring[:, h, j * w:(j + 1) * w]
                        if scatter:
                            pool.indirect_dma_start(out=table, out_offset=off, in_=row, in_offset=None,
                                                    bounds_check=EP - 1, oob_is_err=False).then_inc(s_lland[v][h], 16)
                        else:
                            pool.indirect_dma_start(out=row, out_offset=None, in_=table,
                                                    in_offset=off).then_inc(s_lland[v][h], 16)

        def ring_row(h, j, w):
            return ring[:, h, j * w:(j + 1) * w]

        def dma_pass(pool, n, w, table, scatter=False, limit=None, k=0, f=None, round_end=None):
            f = family(n)[0] if f is None else f
            with pool.Fori(0, ROUNDS) as i:
                for h in range(2):
                    pool.wait_ge(s_slot, i * 2 + k * (2 * ROUNDS) + slot_count(n, 0, h))
                    pool.sem_inc(s_tick[0], 1)
                    for j in range(U):
                        off = bass.IndirectOffsetOnAxis(ap=ridx[:, h, j:j + 1], axis=0)
                        if scatter:
                            pool.indirect_dma_start(out=table, out_offset=off, in_=ring_row(h, j, w), in_offset=None,
                                                    bounds_check=limit, oob_is_err=False).then_inc(s_land[f][h], 16)
                        else:
                            pool.indirect_dma_start(out=ring_row(h, j, w), out_offset=None, in_=table,
                                                    in_offset=off).then_inc(s_land[f][h], 16)
                if round_end:
                    round_end(i)

        def ring_pass(eng, tick, n, fill, take, k=0, f=None):
            f = family(n)[0] if f is None else f
            for h in range(2):
                fill(0, h).then_inc(s_slot, 1)
            with eng.Fori(0, ROUNDS - 1) as i:
                for h in range(2):
                    eng.wait_ge(s_land[f][h], i * LAND + k * (LAND * ROUNDS) + land_count(n, 0))
                    eng.sem_inc(tick, 1)
                    take(i, h)
                    fill(i + 1, h).then_inc(s_slot, 1)
            for h in range(2):
                eng.wait_ge(s_land[f][h], k * (LAND * ROUNDS) + land_count(n, ROUNDS - 1))
                eng.sem_inc(tick, 1)
                take(ROUNDS - 1, h).then_inc(s_actp, 1)

        RG, CREDIT = RC // GT, 2
        MSG0 = CREDIT * GT

        def done(g):
            return g + (CREDIT + 1)

        def free(g, j):
            return g + (CREDIT if j == 0 else CREDIT - 1)

        def groups(eng, body, round_end=None):
            with eng.Fori(0, ROUNDS - 1) as i:
                for j in range(RG):
                    body(i * RG + j, j, False)
                if round_end:
                    round_end(i)
            for j in range(RG):
                body((ROUNDS - 1) * RG + j, j, j == RG - 1)

        def cols(tile, i, h, w=1):
            return tile[:, bass.ds(i * (2 * U * w) + h * U * w, U * w)]

        @block.sync
        def _(sp):
            sp.wait_ge(s_pad, 1)
            for a, t in ((src, srci), (dst, dsti), (etype, etyi), (eweight, ew)):
                sp.dma_start(t[0:P - 1, :], edges(a)).then_inc(s_in, 16)
                sp.dma_start(t[P - 1:P, 0:LASTV], edges_last(a)).then_inc(s_in, 16)
            sp.dma_start(rel_d[:, 0:NB], w_comp).then_inc(s_relt, 16)
            sp.dma_start(rel_d[:, NB:NB + D], rel_emb).then_inc(s_relt, 16)
            for j in range(4):
                sp.dma_start(wcat[32 * j:32 * j + 32, :].rearrange("i (h o) -> i h o", h=NH),
                             w1.rearrange("h i o -> i h o")).then_inc(s_w, 16)
                with nc.allow_non_contiguous_dma(reason="transposed 32 x 32 weights"):
                    sp.dma_start(aw[32 * j:32 * j + 32, 0:D], A1w.rearrange("o i -> i o")).then_inc(s_w, 16)
                    sp.dma_start(aw[32 * j:32 * j + 32, D:2 * D], A2w.rearrange("o i -> i o")).then_inc(s_w, 16)
                sp.dma_start(aw[32 * j:32 * j + 32, 2 * D:3 * D], w_self).then_inc(s_w, 16)
            sp.dma_start(wsd[:, :], fc_w[0, :].partition_broadcast(P)).then_inc(s_w, 16)
            sp.dma_start(b_bias[:, :], bias1.partition_broadcast(P)).then_inc(s_w, 16)
            sp.dma_start(b_b1[:, :], A1b.partition_broadcast(P)).then_inc(s_w, 16)
            sp.dma_start(b_b2[:, :], A2b.partition_broadcast(P)).then_inc(s_w, 16)
            sp.dma_start(b_fcb[:, :], fc_b.partition_broadcast(P)).then_inc(s_w, 16)
            for j in range(4):
                sp.dma_start(wf[32 * j:32 * j + 32, :].rearrange("i (b o) -> i b o", b=NB),
                             w2.rearrange("b i o -> i b o")).then_inc(s_bd, 16)
            sp.wait_ge(s_zr, 1)
            for tab in (agg_d, att_d, rgcn_d, full_d, *list_d):
                sp.dma_start(tab[ZROW:ZROW + 1, :], zrow[0:1, 0:tab.shape[1]]).then_inc(s_ztab, 16)
            for tab in pay_d:
                sp.dma_start(tab[ZROW:ZROW + 1, :], zrow4[:, :]).then_inc(s_ztab, 16)
            sp.wait_ge(s_expz, 1)
            for tab in exp_d:
                sp.dma_start(dense(tab, D), RB[:, 0:T * D]).then_inc(s_expzw, 16)
            for tab in (agg_d, att_d, rgcn_d, full_d, pay_d[0]):
                gap = (ZROW - EP) * tab.shape[1] // P
                sp.dma_start(tab[EP:ZROW, :].rearrange("(p r) w -> p (r w)", p=P), RB[:, 0:gap]).then_inc(s_expzw, 16)
            for tab in list_d:
                flat = tab[0:ZROW, :].rearrange("(p j) w -> p (j w)", p=P)
                width = CW * tab.shape[1]
                for at_ in range(0, width, width // 2):
                    sp.dma_start(flat[:, at_:at_ + width // 2], RB[:, 0:width // 2]).then_inc(s_expzw, 16)
            sp.wait_ge(s_nt, 1)
            for c in range(NA_CH):
                sp.dma_start(nt_d[c * P * NB_COL:(c + 1) * P * NB_COL, :].rearrange("(p b) f -> p (b f)", p=P),
                             NTB[:, c * NB_COL * 4:(c + 1) * NB_COL * 4]).then_inc(s_ntw, 16)

            node_rows = lambda a, c: a.rearrange("(p r) d -> p (r d)", p=NODE_P)[:, bass.ds(c * (CR * D), CR * D)]

            def node_load(c):
                sp.dma_start(nx[0:NODE_P, :], node_rows(x, c)).then_inc(s_nin, 16)

            def node_store(c):
                sp.wait_ge(s_nok, c + 1)
                sp.sem_inc(s_tick[4], 1)
                sp.dma_start(node_rows(out, c), nx[0:NODE_P, :]).then_inc(s_nout, 16)
                sp.wait_ge(s_nout, c * 16 + 16)
                sp.sem_inc(s_tick[4], 1)

            def node_chunk(c):
                node_load(c)
                node_store(c)

            def write_table(tab, n, k=0):
                sp.wait_ge(s_tab, k + n)
                sp.sem_inc(s_tick[4], 1)
                sp.dma_start(dense(tab, D), S[:, :]).then_inc(s_tabw, 16)

            wide = lambda tab, w, n: tab[0:P * n, :].rearrange("(p j) w -> p (j w)", p=P)
            sp.wait_ge(s_pay[0], 1)
            sp.dma_start(wide(pay_d[0], 4, T), PAY[1][:, 0:T * 4]).then_inc(s_payw[0], 16)
            sp.wait_ge(s_full, 1)
            sp.dma_start(wide(full_d, TW, T), RB[:, 0:T * TW]).then_inc(s_fullw, 16)

            def write_list(v, n, tile, w, k=0):
                sp.wait_ge(s_ltab[v], k + 1)
                sp.sem_inc(s_tick[4], 1)
                rw = 2 * CU * w
                with sp.Fori(0, n) as i:
                    sp.dma_start(wide(list_d[v], w, CW)[:, bass.ds(i * rw, rw)],
                                 tile[:, bass.ds(i * rw, rw)]).then_inc(s_ltabw[v], 16)

            sp.wait_ge(s_trips[0], 1)
            n0 = sp.value_load(trips_i[0][0:1, 0:1], min_val=1, max_val=CW // (2 * CU))
            write_list(0, n0, RB, TW)
            sp.wait_ge(s_pay[1], 1)
            sp.dma_start(wide(pay_d[1], 4, CW), PAY[0][:, :]).then_inc(s_payw[1], 16)
            sp.wait_ge(s_trips[1], 1)
            n1 = sp.value_load(trips_i[1][0:1, 0:1], min_val=1, max_val=CW // (2 * CU))
            write_list(1, n1, SW, D)
            for h in range(2):
                sp.wait_ge(s_lland[0][h], n0 * (16 * CU * 3))
                sp.sem_inc(s_tick[4], 1)
            sp.wait_ge(s_ltabw[0], n0 * 16)
            sp.sem_inc(s_tick[4], 1)
            sp.dma_start(RB[:, 0:T * D], dense(exp_d[0], D)).then_inc(s_expl, 16)
            with sp.Fori(0, K_STEPS - 4) as k:
                write_list(1, n1, SW, D, k + 1)
            sp.wait_ge(s_exp, 1)
            sp.dma_start(Y, dense(exp_d[1], D)).then_inc(s_expl, 16)
            write_table(agg_d, 1)
            with sp.Fori(0, ROUNDS - 1) as c:
                node_chunk(c)
            node_load(ROUNDS - 1)
            sp.wait_ge(s_sct, 1)
            sp.dma_start(ROWS, dense(row_d, ROW1)).then_inc(s_row, 16)
            node_store(ROUNDS - 1)
            write_table(att_d, 2)
            with sp.Fori(0, CH - ROUNDS) as c:
                node_chunk(c + ROUNDS)
            write_table(rgcn_d, 3)

        @block.gpsimd
        def _(pool):
            pool.memset(ident[:, :], 0.0).then_inc(s_const, 1)
            pool.memset(ones[:, :], 1.0).then_inc(s_const, 1)
            pool.memset(up[:, :], 1.0).then_inc(s_const, 1)
            pool.memset(low[:, :], 1.0).then_inc(s_const, 1)
            pool.iota(q_f[:, :], pattern=[[1, T]], base=0, channel_multiplier=T,
                      allow_small_or_imprecise_dtypes=True).then_inc(s_const, 1)
            pool.iota(iota_h[:, :], pattern=[[1, NA_CH * P]], base=0, channel_multiplier=0,
                      allow_small_or_imprecise_dtypes=True).then_inc(s_const, 1)
            pool.wait_ge(s_const, 6)
            pool.affine_select(out=ident[:, :], in_=ident[:, :], compare_op=ALU.not_equal, fill=1.0, base=0,
                               pattern=[[-1, P]], channel_multiplier=1).then_inc(s_const, 1)
            pool.affine_select(out=up[:, :], in_=up[:, :], compare_op=ALU.is_gt, fill=0.0, base=0,
                               pattern=[[1, P]], channel_multiplier=-1).then_inc(s_const, 1)
            pool.affine_select(out=low[:, :], in_=low[:, :], compare_op=ALU.is_gt, fill=0.0, base=0,
                               pattern=[[-1, P]], channel_multiplier=1).then_inc(s_const, 1)
            pool.iota(ramp_c[:, :], pattern=[[-1, LW]], base=CW, channel_multiplier=0,
                      allow_small_or_imprecise_dtypes=True).then_inc(s_const, 1)
            pool.iota(pb[:, 0:1], pattern=[[1, 1]], base=0, channel_multiplier=CW,
                      allow_small_or_imprecise_dtypes=True).then_inc(s_const, 1)
            pool.iota(pb[:, 1:2], pattern=[[1, 1]], base=CW, channel_multiplier=T,
                      allow_small_or_imprecise_dtypes=True).then_inc(s_const, 1)
            dma_pass(pool, PASS_X_SRC, D, x[:, :])
            pool.wait_ge(s_ntw, 16 * NA_CH)
            dma_pass(pool, PASS_NT_SRC, 4, nt_d[:, :])
            dma_pass(pool, PASS_X_DST, D, x[:, :])
            pool.wait_ge(s_ztab, 16 * 8)
            pool.wait_ge(s_expzw, 16 * ZERO_DMAS)
            pool.wait_ge(s_payw[0], 16)
            pool.wait_ge(s_trips[0], 1)
            n0 = pool.value_load(trips_i[0][0:1, 0:1], min_val=1, max_val=CW // (2 * CU))
            list_dma(pool, 0, n0, 0, 0, 4, pay_d[0][:, :])
            pool.wait_ge(s_fullw, 16)
            list_dma(pool, 0, n0, 1, 1, TW, full_d[:, :])
            list_dma(pool, 0, n0, 2, 2, D, exp_d[0][:, :], scatter=True)
            pool.wait_ge(s_payw[1], 16)
            pool.wait_ge(s_trips[1], 1)
            n1 = pool.value_load(trips_i[1][0:1, 0:1], min_val=1, max_val=CW // (2 * CU))
            list_dma(pool, 1, n1, 0, 0, 4, pay_d[1][:, :])
            pool.wait_ge(s_ltabw[0], n0 * 16)
            pool.sem_inc(s_tick[0], 1)
            list_dma(pool, 1, n1, 1, 1, TW, list_d[0][:, :])

            own_cols = lambda t, n: t[:, bass.ds(n * U, U)]

            def own_start(n, b):
                pool.tensor_copy(out=pidx[:, b, :], in_=own_cols(dsti, n)).then_inc(s_pfill, 1)
                pool.wait_ge(s_pfill, n + 1)
                pool.sem_inc(s_tick[0], 1)
                for j in range(U):
                    pool.indirect_dma_start(out=pring[:, b, j * 4:(j + 1) * 4], out_offset=None, in_=nt_d[:, :],
                                            in_offset=bass.IndirectOffsetOnAxis(ap=pidx[:, b, j:j + 1], axis=0)
                                            ).then_inc(s_pland[b], 16)

            def own_take(n, b, rounds):
                pool.wait_ge(s_pland[b], rounds * (16 * U))
                pool.sem_inc(s_tick[0], 1)
                pool.tensor_copy(out=own_cols(gout_d, n),
                                 in_=pring[:, b, :].rearrange("p (t f) -> p t f", f=4)[:, :, 2]).then_inc(s_ptake, 1)

            def own_next(taken, b, rounds, n):
                own_take(taken, b, rounds)
                pool.wait_ge(s_ptake, taken + 1)
                pool.sem_inc(s_tick[0], 1)
                own_start(n, b)

            own_start(0, 0)
            with pool.Fori(0, K_STEPS - 4) as k:
                pool.wait_ge(s_ltabw[1], k * n1 * 16 + n1 * 16)
                pool.sem_inc(s_tick[0], 1)
                list_dma(pool, 1, n1, k + 2, k + 2, D, list_d[1][:, :])
                own_next(k, 0, k + 1, k + 1)
            pool.wait_ge(s_ltabw[1], n1 * (16 * (K_STEPS - 3)))
            pool.sem_inc(s_tick[0], 1)
            list_dma(pool, 1, n1, K_STEPS - 2, K_STEPS - 2, D, list_d[1][:, :])
            list_dma(pool, 1, n1, K_STEPS - 1, K_STEPS - 1, D, exp_d[1][:, :], scatter=True)
            pool.wait_ge(s_tabw, 16)
            dma_pass(pool, PASS_L0, D, agg_d[:, :])
            dma_pass(pool, PASS_ROW, ROW1, row_d[:, :], scatter=True)
            own_start(ROUNDS, 1)
            with pool.Fori(0, (ROUNDS - 1) // 2) as m:
                for b in range(2):
                    own_next(m * 2 + (ROUNDS - 1 + b), b, m + (1 if b else ROUNDS), m * 2 + (ROUNDS + 1 + b))
            for b, rounds in ((0, (3 * ROUNDS - 1) // 2), (1, (ROUNDS + 1) // 2)):
                own_take(2 * ROUNDS - 2 + b, b, rounds)
            pool.wait_ge(s_tabw, 32)
            dma_pass(pool, PASS_ATT_SRC, D, att_d[:, :])
            dma_pass(pool, PASS_ATT_DST, D, att_d[:, :])
            pool.wait_ge(s_relt, 32)

            def out_src_slot(n, b):
                pool.wait_ge(s_oslot, n + 1)
                pool.sem_inc(s_tick[0], 1)
                for t in range(U):
                    pool.indirect_dma_start(out=out[:, :], out_offset=bass.IndirectOffsetOnAxis(
                        ap=oidx[:, b, t:t + 1], axis=0), in_=oring[b][:, t * D:(t + 1) * D], in_offset=None,
                        bounds_check=N - 1, oob_is_err=False).then_inc(s_oland[b], 16)

            pool.wait_ge(s_nout, 16 * CH)
            dma_pass(pool, PASS_REL, RW, rel_d[:, :], round_end=lambda i: out_src_slot(i, 0))
            with pool.Fori(0, (ROUNDS - 1) // 2) as k:
                for b in (1, 0):
                    out_src_slot(k * 2 + (ROUNDS + 1 - b), b)
            out_src_slot(2 * ROUNDS - 1, 1)
            pool.wait_ge(s_tabw, 48)
            dma_pass(pool, PASS_RGCN, D, rgcn_d[:, :])
            dma_pass(pool, PASS_OUT_DST, D, out[:, :], scatter=True, limit=N - 1)
            for b in range(2):
                pool.wait_ge(s_oland[b], 16 * U * ((3 * ROUNDS - 1) // 2 if b == 0 else (ROUNDS + 1) // 2))
            for h in range(2):
                pool.wait_ge(s_land[1][h], land_count(PASS_OUT_DST, ROUNDS - 1))

        def bc3(ap, n):
            return ap.unsqueeze(2).to_broadcast([ap.shape[0], ap.shape[1], n])

        def mid(ap, n):
            return ap.unsqueeze(1).to_broadcast([ap.shape[0], n, ap.shape[1]])

        @block.vector
        def _(dve):
            st = Steps(dve, s_dve)
            tick = s_tick[2]
            V = nc.vector

            st.do(V.memset(srci[:, :], N))
            st.do(V.memset(dsti[:, :], N))
            st.do(V.memset(etyi[:, :], 0))
            st.do(V.memset(ew[:, :], 0.0))
            st.wait()
            dve.sem_inc(s_pad, 1)
            st.do(V.memset(zrow[:, :], 0.0))
            st.do(V.memset(zrow4[:, :], 0.0))
            st.do(V.memset(RB[:, 0:CW * D], 0.0))
            st.wait()
            st.do(V.memset(zrow[:, D:D + 1], float(ZROW)))
            st.do(V.memset(zrow4[:, 0:1], float(ZROW)))
            st.do(V.memset(zrow4[:, 2:3], -1.0))
            st.do(V.memset(zrow4[:, 3:4], float(OOB)))
            st.wait()
            dve.sem_inc(s_zr, 1)
            dve.sem_inc(s_expz, 1)
            st.do(V.memset(roots[:, :], 1.0))
            st.do(V.memset(bd1[:, :], 0.0))
            st.do(V.memset(bdy[:, :], 0.0))
            for kind, (_, eps) in ROOTS.items():
                st.do(V.memset(eps_t[kind][:, :], eps))
            st.do(V.memset(zh[:, :], 0.0))
            st.wait()

            dve.wait_ge(s_in, 16 * 8)
            st.do(V.tensor_scalar(srcf[:, :], srci[:, :], 0.0, None, ALU.add))
            st.do(V.tensor_scalar(dstf[:, :], dsti[:, :], 0.0, None, ALU.add))
            st.do(V.tensor_scalar(xsi[:, :], srci[:, :], float(N - 1), None, ALU.min))
            st.do(V.tensor_scalar(xdi[:, :], dsti[:, :], float(N - 1), None, ALU.min))
            st.wait()
            dve.sem_inc(s_ids, 1)
            for key, a, b in ((srci, a_s, b_s), (dsti, a_d, b_d)):
                st.seq(V.tensor_scalar(tmpi[:, :], key[:, :], NB_COL.bit_length() - 1, None, ALU.logical_shift_right))
                st.seq(V.tensor_scalar(a[:, :], tmpi[:, :], 0.0, None, ALU.add))
                st.seq(V.tensor_scalar(tmpi[:, :], key[:, :], NB_COL - 1, None, ALU.bitwise_and))
                st.seq(V.tensor_scalar(b[:, :], tmpi[:, :], 0.0, None, ALU.add))

            dve.wait_ge(s_const, 12)
            st.do(V.tensor_copy(ident_h[:, :], ident[:, :]))
            st.do(V.memset(emask[:, 0:3 * P], 1.0))
            st.do(V.tensor_copy(emask[:, 3 * P:4 * P], low[:, :]))
            st.wait()
            dve.sem_inc(s_cst2, 1)

            with dve.Fori(0, NG) as i:
                for j in range(4):
                    col = lambda t: t[:, bass.ds(i * 4 + j, 1)]
                    dve.wait_ge(s_ohu, i * 4 + j + 1)
                    dve.sem_inc(tick, 1)
                    V.tensor_scalar(oha[:, j, :], iota_h[:, :], col(a_d), None, ALU.is_equal)
                    V.tensor_scalar(ohb[:, j, :], iota_h[:, 0:NB_COL], col(b_d), None, ALU.is_equal)
                    V.tensor_scalar(oha2[:, j, :], iota_h[:, :], col(a_s), None, ALU.is_equal)
                    V.tensor_scalar(ohb2[:, j, :], iota_h[:, 0:NB_COL], col(b_s), None,
                                    ALU.is_equal).then_inc(s_oh, 1)
            dve.wait_ge(s_hist, 1)
            hc = lambda tile, k, c: tile[:, k * TB + c * NB_COL:k * TB + (c + 1) * NB_COL]
            for k in range(2):
                for c in range(NA_CH):
                    st.do(V.tensor_scalar(hc(HC, k, c), bank[c][:, k * NB_COL:(k + 1) * NB_COL], 0.0, None, ALU.add))
            st.wait()
            for k in range(2):
                for c in range(NA_CH):
                    st.do(V.tensor_tensor_scan(hc(IC, k, c), ones[:, 0:1].to_broadcast([P, NB_COL]), hc(HC, k, c),
                                               0.0, ALU.mult, ALU.add))
            st.wait()
            for k in range(2):
                st.do(V.tensor_copy(tot[:, k, :], IC[:, k * TB:(k + 1) * TB].rearrange(
                    "p (c b) -> p c b", b=NB_COL)[:, :, NB_COL - 1]))
            st.wait()
            dve.sem_inc(s_tot, 1)
            dve.wait_ge(s_base, 1)
            st.do(V.tensor_copy(base[:, :, :], bank[4][:, 0:2 * NA_CH].rearrange("p (k c) -> p k c", k=2)))
            st.do(V.tensor_copy(tot[:, :, :], bank[5][:, 0:2 * NA_CH].rearrange("p (k c) -> p k c", k=2)))
            st.wait()
            for c in range(1, NA_CH):
                for e in range(c):
                    st.seq(V.tensor_tensor(base[:, :, c:c + 1], base[:, :, c:c + 1], tot[:, :, e:e + 1], ALU.add))
            for k in range(2):
                for c in range(NA_CH):
                    st.do(V.tensor_scalar(hc(IC, k, c), hc(IC, k, c), base[:, k, c:c + 1], float(-1 - ZROW), ALU.add,
                                          ALU.add))
            st.wait()
            dve.wait_ge(s_expzw, 16 * ZERO_DMAS)
            nt = NTB.rearrange("p (n f) -> p n f", f=4)
            for k in range(2):
                h, e = HC[:, k * TB:(k + 1) * TB], IC[:, k * TB:(k + 1) * TB]
                st.do(V.tensor_copy(nt[:, :, 2 * k + 1], h))
                st.seq(V.scalar_tensor_tensor(out=e, in0=h, scalar=0.0, in1=e, op0=ALU.is_gt, op1=ALU.mult))
                st.do(V.tensor_scalar(nt[:, :, 2 * k], e, float(ZROW), None, ALU.add))
            st.wait()
            dve.sem_inc(s_nt, 1)

            st.do(V.memset(rhi[0], 0.0))
            st.do(V.memset(rlo[0], 0.0))
            RANK_STEPS = 8 + 1 + 8 + 2 + 1

            def batch_cols(t, i, n=4, j=0):
                return t[:, bass.ds(i * 4 + j, n)]

            def rank_onehots(i, b):
                for j in range(4):
                    st.do(V.tensor_scalar(ohas[b][:, j, :], iota_h[:, :], batch_cols(a_s, i, 1, j), None, ALU.is_equal))
                    st.do(V.tensor_scalar(ohbs[b][:, j, :], iota_h[:, 0:NB_COL], batch_cols(b_s, i, 1, j), None,
                                          ALU.is_equal))
                st.do(V.tensor_scalar(kcol[:, b, :], batch_cols(srcf, i), 0.0, None, ALU.add))
                st.wait()
                dve.sem_inc(s_oh, 1)

            def rank_batch(i, b, last=False):
                if not last:
                    rank_onehots(i + 1, 1 - b)
                dve.wait_ge(s_kt, i + 1)
                dve.sem_inc(tick, 1)
                at_ = 0
                for j in range(4):
                    n = (j + 1) * P
                    st.do(V.scalar_tensor_tensor(out=junk[:, at_:at_ + n], in0=bank[4 + 3 * b][:, 0:n],
                                                 scalar=batch_cols(srcf, i, 1, j), in1=emask[:, 4 * P - n:4 * P],
                                                 op0=ALU.is_equal, op1=ALU.mult, accum_out=rk4[:, j:j + 1]))
                    at_ += n
                st.wait()
                dve.sem_inc(s_eq, 1)
                if not last:
                    dve.wait_ge(s_rhi, i + 1)
                    dve.sem_inc(tick, 1)
                    for k in range(2):
                        pair = lambda t: t[1 - b][:, 2 * k:2 * k + 2, :].rearrange("p c n -> p (c n)")
                        st.do(V.tensor_tensor(pair(rlo), bank[k][:, :], pair(rhi), ALU.subtract))
                    st.wait()
                    dve.sem_inc(s_rc, 1)
                dve.wait_ge(s_g, i + 1)
                dve.sem_inc(tick, 1)
                for j in range(4):
                    g = bank[5 + j // 2][:, (j % 2) * NB_COL:(j % 2 + 1) * NB_COL]
                    st.do(V.scalar_tensor_tensor(out=junk[:, at_:at_ + NB_COL], in0=g, scalar=1.0, in1=ohbs[b][:, j, :],
                                                 op0=ALU.mult, op1=ALU.mult, accum_out=cnt4[:, j:j + 1]))
                    at_ += NB_COL
                st.wait()
                dve.sem_inc(s_gu, 1)
                st.seq(V.tensor_tensor(batch_cols(posf, i), cnt4[:, :], rk4[:, :], ALU.add))

            def stepped_ring_pass(n, fill, take, per, round_work=None, extra=0, last_work=None, between=None,
                                  before_fill=None, next_fill=None, filled=False, landed=None):
                f = family(n)[0]
                if before_fill and not filled:
                    before_fill(0)
                if not filled:
                    for h in range(2):
                        fill(0, h).then_inc(s_slot, 1)
                if between:
                    between()
                with st.loop(ROUNDS - 1, 2 * per + extra) as i:
                    if before_fill:
                        before_fill(i + 1)
                    for h in range(2):
                        dve.wait_ge(s_land[f][h], i * LAND + land_count(n, 0))
                        dve.sem_inc(tick, 1)
                        take(i, h)
                        fill(i + 1, h).then_inc(s_slot, 1)
                    if round_work:
                        round_work(i)
                for h in range(2):
                    dve.wait_ge(s_land[f][h], land_count(n, ROUNDS - 1))
                    dve.sem_inc(tick, 1)
                    take(ROUNDS - 1, h)
                    if next_fill:
                        next_fill(0, h).then_inc(s_slot, 1)
                if landed:
                    landed()
                if last_work:
                    last_work(ROUNDS - 1)

            def fill_idx(idx):
                return lambda i, h: V.tensor_scalar(ridx[:, h, :], cols(idx, i, h), 0.0, None, ALU.add)

            def slot(h, w=D):
                return ring[:, h, 0:U * w]

            def copy_take(dest, w=D):
                def take(i, h):
                    st.do(V.tensor_scalar(cols(dest, i, h, w), slot(h, w), 0.0, None, ALU.add))
                    st.wait()
                    dve.sem_inc(tick, 1)
                return take

            assert NG == 2 * 4 * (ROUNDS - 1) + 1
            dve.wait_ge(s_actp, 2)
            st.wait()
            dve.sem_inc(s_rc, 1)
            dve.sem_inc(s_eq, 1)
            dve.sem_inc(s_gu, 1)
            rank_onehots(0, 0)

            def ranks_from(start):
                def work(i):
                    for c in range(4):
                        rank_batch(i * 4 + (start + c), c % 2)
                return work

            stepped_ring_pass(PASS_NT_SRC, fill_idx(srci), copy_take(S[:, 0:4 * T], 4), 1, ranks_from(0),
                              4 * RANK_STEPS, next_fill=fill_idx(xdi))
            stepped_ring_pass(PASS_X_DST, fill_idx(xdi), copy_take(XD), 1,
                              ranks_from(4 * (ROUNDS - 1)), 4 * RANK_STEPS, filled=True)
            rank_batch(NG - 1, 0, last=True)
            st.wait()

            def segments(key, mask, first, fcar, fbak, neg=None, n=0):
                st.do(V.tensor_tensor(mask[:, 1:T], key[:, 1:T], key[:, 0:T - 1], ALU.is_equal))
                st.do(V.memset(mask[:, 0:1], 0.0))
                st.do(V.tensor_scalar(first[:, :], key[:, :], key[:, 0:1], None, ALU.is_equal))
                st.do(V.tensor_copy(tl[:, 0:1], key[:, 0:1]))
                st.do(V.tensor_copy(tl[:, 1:2], key[:, T - 1:T]))
                st.wait()
                dve.sem_inc(s_trw, 1)
                dve.wait_ge(s_tr, n + 1)
                st.do(V.scalar_tensor_tensor(out=fcar[:, :], in0=bank[4][:, 0:P], scalar=tl[:, 1:2], in1=up[:, :],
                                             op0=ALU.is_equal, op1=ALU.mult))
                st.do(V.scalar_tensor_tensor(out=fbak[:, :], in0=bank[5][:, 0:P], scalar=tl[:, 0:1], in1=low[:, :],
                                             op0=ALU.is_equal, op1=ALU.mult))
                if neg is not None:
                    st.wait()
                    st.seq(V.tensor_scalar(neg[:, :], fbak[:, :], 1.0, BIG, ALU.subtract, ALU.mult))
                st.wait()

            ncarry = [0]

            def carries():
                dve.sem_inc(s_tail, 1)
                ncarry[0] += 1
                dve.wait_ge(s_carry, ncarry[0])

            def segment_sums(src3, dst3, width, mask, first):
                for d in range(width):
                    st.do(V.tensor_tensor_scan(dst3[:, :, d], mask[:, :], src3[:, :, d], 0.0, ALU.mult, ALU.add))
                st.wait()
                st.seq(V.tensor_scalar(tl[:, 0:width], dst3[:, T - 1, :], 0.0, None, ALU.add))
                carries()
                st.seq(V.tensor_copy(car[:, 0:width], bank[7][:, 0:width]))
                for d in range(width):
                    st.do(V.scalar_tensor_tensor(out=dst3[:, :, d], in0=first[:, :], scalar=car[:, d:d + 1],
                                                 in1=dst3[:, :, d], op0=ALU.mult, op1=ALU.add))
                st.wait()

            def spread_back(t3_, width, mask_end, key):
                st.seq(V.tensor_scalar(t1[:, :], mask_end[:, :], -1.0, 1.0, ALU.mult, ALU.add))
                st.seq(V.tensor_tensor(t3_, t3_, bc3(mask_end[:, :], width), ALU.mult))
                for d in range(width):
                    st.do(V.tensor_tensor_scan(t3_[:, ::-1, d], t1[:, ::-1], t3_[:, ::-1, d], 0.0, ALU.mult, ALU.add))
                st.do(V.tensor_scalar(t2[:, :], key[:, :], key[:, T - 1:T], None, ALU.is_equal))
                st.wait()
                st.do(V.tensor_scalar(tl[:, 0:width], t3_[:, 0, :], 0.0, None, ALU.add))
                st.do(V.tensor_scalar(t2[:, :], t2[:, :], t1[:, T - 1:T], None, ALU.mult))
                st.wait()
                carries()
                st.seq(V.tensor_copy(car[:, 0:width], bank[7][:, 0:width]))
                for d in range(width):
                    st.do(V.scalar_tensor_tensor(out=t3_[:, :, d], in0=t2[:, :], scalar=car[:, d:d + 1],
                                                 in1=t3_[:, :, d], op0=ALU.mult, op1=ALU.add))
                st.wait()

            def segment_ends(mask, fcar, ends):
                st.do(V.tensor_scalar(ends[:, 0:T - 1], mask[:, 1:T], -1.0, 1.0, ALU.mult, ALU.add))
                st.do(V.tensor_reduce(tm[:, :], fcar[:, :], AX.X, ALU.max))
                st.wait()
                st.seq(V.tensor_scalar(ends[:, T - 1:T], tm[:, :], -1.0, 1.0, ALU.mult, ALU.add))

            st.do(V.tensor_copy(gin[:, :], NS3[:, :, 0]))
            st.do(V.tensor_copy(ginf[:, :], NS3[:, :, 0]))
            st.do(V.tensor_copy(gout_s[:, :], NS3[:, :, 2]))
            st.do(V.tensor_tensor(t1[:, :], NS3[:, :, 2], NS3[:, :, 3], ALU.subtract))
            st.wait()
            st.seq(V.scalar_tensor_tensor(out=posf[:, :], in0=t1[:, :], scalar=1.0, in1=posf[:, :], op0=ALU.add,
                                          op1=ALU.add))
            st.do(V.tensor_copy(posi[:, :], posf[:, :]))
            st.wait()
            st.do(V.tensor_scalar(t1[:, :], NS3[:, :, 1], 1.0, None, ALU.max))
            st.do(V.tensor_scalar(t2[:, :], NS3[:, :, 3], 1.0, None, ALU.max))
            st.wait()
            dve.sem_inc(s_sri, 1)
            dve.wait_ge(s_sro, 1)
            st.do(V.reciprocal(t1[:, :], t1[:, :]))
            st.seq(V.reciprocal(t2[:, :], t2[:, :]))
            st.do(V.scalar_tensor_tensor(out=c1[:, :], in0=t1[:, :], scalar=1.0 - ALPHA, in1=t2[:, :], op0=ALU.mult,
                                         op1=ALU.mult))
            st.do(V.tensor_scalar(c2[:, :], t2[:, :], ALPHA, None, ALU.mult))

            def root():
                dve.sem_inc(s_ri, 1)
                st.n += 1
                st.wait()
                dve.sem_inc(tick, 1)

            def chunk(t, i, w=D):
                return t[:, bass.ds(i * (RC * w), RC * w)].rearrange("p (t d) -> p t d", d=w)

            cols2 = lambda t, i: t[:, bass.ds(i * RC, RC)]

            def norm_chunk(tiles, i, ratio=None):
                k = len(tiles)
                part = lambda t, m: t[:, m * RC:(m + 1) * RC]
                sq = lambda m: sq_s[:, m * RC * D:(m + 1) * RC * D].rearrange("p (t d) -> p t d", d=D)
                dve.sem_inc(tick, 1)
                for m, t in enumerate(tiles):
                    st.do(V.tensor_reduce(part(roots, m), chunk(t, i), AX.X, ALU.add))
                st.wait()
                dve.sem_inc(tick, 1)
                st.seq(V.tensor_scalar(roots[:, 0:k * RC], roots[:, 0:k * RC], 1.0 / D, None, ALU.mult))
                for m, t in enumerate(tiles):
                    st.do(V.tensor_tensor(chunk(t, i), chunk(t, i), bc3(part(roots, m), D), ALU.subtract))
                st.wait()
                for m, t in enumerate(tiles):
                    st.do(V.tensor_tensor(sq(m), chunk(t, i), chunk(t, i), ALU.mult))
                st.wait()
                dve.sem_inc(tick, 1)
                for m, t in enumerate(tiles):
                    st.do(V.tensor_reduce(part(roots, m), sq(m), AX.X, ALU.add))
                st.wait()
                if ratio is not None:
                    st.seq(V.tensor_copy(vs[:, :], part(roots, 0)))
                root()
                if ratio is not None:
                    st.seq(V.tensor_copy(rs[:, :], part(roots, 0)))
                st.seq(V.reciprocal(roots[:, 0:k * RC], roots[:, 0:k * RC]))
                for m, t in enumerate(tiles):
                    st.do(V.tensor_tensor(chunk(t, i), chunk(t, i), bc3(part(roots, m), D), ALU.mult))
                st.wait()
                if ratio is not None:
                    st.seq(V.tensor_copy(part(roots, 0), vs[:, :]))
                    root()
                    st.seq(V.reciprocal(part(roots, 0), part(roots, 0)))
                    st.seq(V.tensor_tensor(cols2(ratio, i), part(roots, 0), rs[:, :], ALU.mult))

            def logits_chunk(t, k, i):
                shape = [P, RC, NH, D]
                lp = lp_s.rearrange("p (t h d) -> p t h d", h=NH, d=D)
                u = u_all[:, k * NH * D:(k + 1) * NH * D].rearrange("p (h d) -> p h d", h=NH)
                st.seq(V.tensor_tensor(lp, chunk(t, i).unsqueeze(2).to_broadcast(shape),
                                       u.unsqueeze(1).to_broadcast(shape), ALU.mult))
                dve.sem_inc(tick, 1)
                z = chunk((z4t, e4t)[k], i, NH)
                st.seq(V.tensor_reduce(z, lp, AX.X, ALU.add))

            st.do(V.tensor_copy(t3[:, :], t2[:, :]))
            st.wait()
            nrow = [0]

            def column_max(out_, neg=None):
                st.wait()
                dve.sem_inc(s_trw, 1)
                nrow[0] += 1
                dve.wait_ge(s_tr, nrow[0])
                if neg is None:
                    st.seq(V.tensor_reduce(out_, bank[4][:, 0:P], AX.X, ALU.max))
                else:
                    st.seq(V.tensor_tensor(prod[:, 0:P], bank[4][:, 0:P], neg[:, :], ALU.add))
                    st.seq(V.tensor_reduce(out_, prod[:, 0:P], AX.X, ALU.max))

            CS = [None, None]

            @contextmanager
            def both_loops(a, b, count, per, dyn):
                an, bd, ao, bo = a.n, b.dyn, a.off, b.off
                with dve.Fori(0, count) as k:
                    a.off, b.off = k * per, k * b.trips * dyn
                    yield k
                    assert (a.n - an, b.dyn - bd) == (per, dyn), (a.n - an, b.dyn - bd)
                    a.off, b.off = ao, bo
                a.n, b.dyn = an + per * count, bd + dyn * count

            def make_list(v, act, n, to_row, stride):
                st.seq(V.tensor_reduce(tl[:, 0:1], act[:, 0:n], AX.X, ALU.add))
                column_max(car[:, 0:1])
                st.seq(V.tensor_scalar(trips_i[v][:, :], car[:, 0:1], float(2 * CU - 1), None, ALU.add))
                st.seq(V.tensor_scalar(trips_i[v][:, :], trips_i[v][:, :], 3, None, ALU.logical_shift_right))
                st.seq(V.tensor_scalar(trips_i[v][:, :], trips_i[v][:, :], 1, None, ALU.max))
                dve.sem_inc(s_trips[v], 1)
                trips = dve.value_load(trips_i[v][0:1, 0:1], min_val=1, max_val=CW // (2 * CU))
                CS[v] = cs = Steps(dve, s_lst[v], trips)
                st.do(V.memset(lkey, 0.0))
                st.do(V.memset(lval, 0.0))
                st.wait()
                st.seq(V.tensor_tensor(lkey[:, 0:n], act[:, 0:n], ramp_c[:, 0:n], ALU.mult))
                with cs.trip_loop(3) as i:
                    cs.seq(V.max(m8[:, :], lkey[:, 0:CW]))
                    dve.sem_inc(tick, 1)
                    cs.seq(V.match_replace(lkey[:, 0:CW], m8[:, :], lkey[:, 0:CW], 0.0))
                    dve.sem_inc(tick, 1)
                    cs.seq(V.tensor_scalar(lval[:, bass.ds(i * 8, 8)], m8[:, :], 0.0, None, ALU.add))
                    dve.sem_inc(tick, 1)
                st.seq(V.tensor_scalar(lact, lval, -1.0, to_row, ALU.mult, ALU.add))
                st.seq(V.tensor_scalar(lact, lact, stride, None, ALU.add))
                st.seq(V.scalar_tensor_tensor(out=lact, in0=lval, scalar=0.0, in1=lact, op0=ALU.is_gt, op1=ALU.mult))
                st.seq(V.tensor_scalar(lq, lact, float(ZROW), None, ALU.add))
                return cs

            def positions(cs_v, act, n, mask, first, scale_tail):
                st.seq(V.tensor_tensor_scan(lcnt[:, 0:n], ones[:, 0:1].to_broadcast([P, n]), act[:, 0:n], 0.0,
                                            ALU.mult, ALU.add))
                st.seq(V.scalar_tensor_tensor(out=lcnt[:, 0:n], in0=lcnt[:, 0:n], scalar=pb[:, 0:1], in1=act[:, 0:n],
                                              op0=ALU.add, op1=ALU.mult))
                st.seq(V.tensor_tensor_scan(lkey[:, 0:n], mask[:, 0:n], lcnt[:, 0:n], 0.0, ALU.mult, ALU.max))
                st.seq(V.tensor_scalar(tl[:, 0:1], lkey[:, n - 1:n], scale_tail, None, ALU.mult))
                column_max(car[:, 0:1], dneg)
                st.seq(V.scalar_tensor_tensor(out=lkey[:, 0:n], in0=first[:, 0:n], scalar=car[:, 0:1],
                                              in1=lkey[:, 0:n], op0=ALU.mult, op1=ALU.max))
                st.seq(V.tensor_scalar(lcnt[:, 0:n], lkey[:, 0:n], float(-1 - ZROW), None, ALU.add))
                st.seq(V.scalar_tensor_tensor(out=lcnt[:, 0:n], in0=lkey[:, 0:n], scalar=0.0, in1=lcnt[:, 0:n],
                                              op0=ALU.is_gt, op1=ALU.mult))
                st.seq(V.tensor_scalar(lcnt[:, 0:n], lcnt[:, 0:n], float(ZROW), None, ALU.add))

            def list_gather(v, cs, m, idx, take, per):
                n = cs.trips
                fill = lambda i, h: V.tensor_scalar(
                    cidx[:, h, :], idx[:, h * CU:(h + 1) * CU] if isinstance(i, int) else
                    idx[:, bass.ds(i * (2 * CU) + h * CU, CU)], 0.0, None, ALU.add)
                for h in range(2):
                    fill(0, h).then_inc(s_lslot[v], 1)
                with cs.trip_loop(2 * per) as i:
                    for h in range(2):
                        dve.wait_ge(s_lland[v][h], i * (16 * CU) + (16 * CU) + n_times(n, m, 16 * CU))
                        dve.sem_inc(tick, 1)
                        take(i, h)
                        fill(i + 1, h).then_inc(s_lslot[v], 1)
                dve.wait_ge(s_lslot[v], n_times(n, m, 2) + n * 2 + m * 2 + 2)
                dve.sem_inc(tick, 1)

            def list_scatter(v, cs, a, b, fill):
                n = cs.trips
                with dve.Fori(0, n) as i:
                    for h in range(2):
                        fill(i, h)
                        V.tensor_scalar(cidx[:, h, :], lidx[:, bass.ds(i * (2 * CU) + h * CU, CU)], 0.0, None,
                                        ALU.add).then_inc(s_lslot[v], 1)
                    for h in range(2):
                        dve.wait_ge(s_lland[v][h], n * (16 * CU * a) + i * (16 * CU) + 16 * CU)
                    dve.sem_inc(tick, 1)

            chunk4 = lambda t, i, h, w: t[:, bass.ds(i * (2 * CU * w) + h * (CU * w), CU * w)].rearrange(
                "p (j w) -> p j w", w=w)

            def pay_take(v, cs):
                def take(i, h):
                    cs.seq(V.tensor_scalar(chunk4(PAY[v], i, h, 4), cring[:, h, 0:CU * 4].rearrange(
                        "p (j w) -> p j w", w=4), 0.0, None, ALU.add))
                    dve.sem_inc(tick, 1)
                return take

            def list_masks(v):
                key = PAY[v][:, :].rearrange("p (j w) -> p j w", w=4)[:, :, 2]
                st.do(V.tensor_tensor(lmask[:, 1:CW], key[:, 1:CW], key[:, 0:CW - 1], ALU.is_equal))
                st.do(V.memset(lmask[:, 0:1], 0.0))
                st.do(V.tensor_scalar(lkey[:, 0:CW], key, 0.0, None, ALU.is_lt))
                st.do(V.tensor_scalar(lfirst[:, 0:CW], key, dstf[:, 0:1], None, ALU.is_equal))
                st.do(V.tensor_reduce(tm[:, :], key, AX.X, ALU.max))
                st.wait()
                st.do(V.tensor_tensor(lmask[:, 0:CW], lmask[:, 0:CW], lkey[:, 0:CW], ALU.max))
                st.do(V.tensor_scalar(tm[:, :], tm[:, :], dstf[:, T - 1:T], None, ALU.is_equal))
                st.wait()

            def row_take(v, cs, w, z, zw, total, first, times=None):
                pay3 = lambda i, h: chunk4(PAY[v], i, h, 4)[:, :, 1]
                r = lambda h: cring[:, h, 0:CU * w].rearrange("p (j w) -> p j w", w=w)

                def take(i, h):
                    cs.seq(V.tensor_tensor(y4[:, :, :], r(h)[:, :, 0:D], pay3(i, h).unsqueeze(2).to_broadcast(
                        [P, CU, D]), ALU.mult))
                    dve.sem_inc(tick, 1)
                    if z is not None:
                        for j in range(CU):
                            cs.seq(V.scalar_tensor_tensor(
                                out=zr[:, j + 1, :], in0=zr[:, j, :],
                                scalar=lmask[:, bass.ds(i * (2 * CU) + h * CU + j, 1)], in1=y4[:, j, :],
                                op0=ALU.mult, op1=ALU.add))
                            dve.sem_inc(tick, 1)
                        cs.do(V.tensor_scalar(chunk4(z, i, h, zw)[:, :, 0:D], zr[:, 1:CU + 1, :], 0.0, None, ALU.add))
                        cs.do(V.tensor_scalar(zr[:, 0, :], zr[:, CU, :], 0.0, None, ALU.add))
                    if w == TW:
                        cs.do(V.tensor_scalar(lnext[:, bass.ds(i * (2 * CU) + h * CU, CU)], r(h)[:, :, D], 0.0, None,
                                              ALU.add))
                    t = chunk4(total, i, h, D)
                    if first:
                        cs.do(V.tensor_scalar(t, y4[:, :, :], 0.0, None, ALU.add))
                    elif times:
                        cs.do(V.scalar_tensor_tensor(out=t, in0=y4[:, :, :], scalar=times, in1=t, op0=ALU.mult,
                                                     op1=ALU.add))
                    else:
                        cs.do(V.tensor_tensor(t, t, y4[:, :, :], ALU.add))
                    cs.wait()
                    dve.sem_inc(tick, 1)
                return take

            def list_carry(v, cs, z, zw, count):
                st.seq(V.tensor_scalar(tl[:, 0:D], zr[:, 0, :], tm[:, 0:1], None, ALU.mult))
                dve.sem_inc(s_tail, 1)
                dve.wait_ge(s_carry, count)
                dve.sem_inc(tick, 1)
                pr8 = prod[:, 0:2 * CU * D].rearrange("p (j w) -> p j w", w=D)
                with cs.trip_loop(2) as i:
                    f = lfirst[:, bass.ds(i * (2 * CU), 2 * CU)].unsqueeze(2).to_broadcast([P, 2 * CU, D])
                    zz = z[:, bass.ds(i * (2 * CU * zw), 2 * CU * zw)].rearrange("p (j w) -> p j w", w=zw)[:, :, 0:D]
                    cs.seq(V.tensor_tensor(pr8, f, mid(bank[7][:, 0:D], 2 * CU), ALU.mult))
                    dve.sem_inc(tick, 1)
                    cs.seq(V.tensor_tensor(zz, zz, pr8, ALU.add))
                    dve.sem_inc(tick, 1)

            st.do(V.tensor_scalar(t1[:, :], ginf[:, :], float(ZROW), None, ALU.is_lt))
            st.do(V.tensor_scalar(t2[:, :], srcf[:, :], float(N), None, ALU.is_lt))
            st.wait()
            st.seq(V.tensor_tensor(t1[:, :], t1[:, :], t2[:, :], ALU.mult))
            cs = make_list(0, t1, T, pb[:, 1:2], float(-ZROW))
            pay3 = PAY[1][:, 0:T * 4].rearrange("p (j w) -> p j w", w=4)
            st.do(V.tensor_copy(pay3[:, :, 0], ginf[:, :]))
            st.do(V.tensor_copy(pay3[:, :, 1], c1[:, :]))
            st.do(V.tensor_copy(pay3[:, :, 2], dstf[:, :]))
            st.do(V.tensor_copy(pay3[:, :, 3], q_f[:, :]))
            st.wait()
            dve.sem_inc(s_pay[0], 1)
            st.seq(V.memset(PAY[0][:, :], -1.0))
            dve.sem_inc(s_actgo, 1)
            segments(dstf, dmask, dfirst, dcar, dbak, neg=dneg, n=nrow[0])
            nrow[0] += 1
            segment_ends(dmask, dcar, dend)
            st.do(V.tensor_tensor(t1w[:, 0:T], NS3[:, :, 2], posf[:, :], ALU.is_equal))
            st.do(V.tensor_scalar(t2[:, :], NS3[:, :, 1], 0.0, None, ALU.is_equal))
            st.wait()
            st.seq(V.tensor_tensor(t1w[:, 0:T], t1w[:, 0:T], t2[:, :], ALU.mult))
            for flag, key, dest in ((t1w[:, 0:T], srcf, osi), (dend, dstf, odi)):
                st.seq(V.scalar_tensor_tensor(out=t2[:, :], in0=key[:, :], scalar=float(-OOB), in1=flag[:, :],
                                              op0=ALU.add, op1=ALU.mult))
                st.seq(V.tensor_scalar(t2[:, :], t2[:, :], float(OOB), None, ALU.add))
                st.seq(V.tensor_copy(dest[:, :], t2[:, :]))
            st.seq(V.tensor_tensor(Y3, XS3, bc3(c2[:, :], D), ALU.mult))
            segment_sums(Y3, S3, D, dmask, dfirst)
            st.do(V.memset(tm[:, :], 1.0))
            st.wait()
            positions(cs, t1, T, dmask, dfirst, tm[:, 0:1])
            st.do(V.tensor_copy(FULL[:, :, 0:D], S3))
            st.do(V.tensor_copy(FULL[:, :, D], lcnt[:, 0:T]))
            st.do(V.memset(FULL[:, :, D + 1:TW], 0.0))
            st.wait()
            dve.sem_inc(s_full, 1)
            dve.wait_ge(s_pay0, cs.trips * 2)
            dve.wait_ge(s_lslot[0], cs.trips * 2 + 2)
            dve.sem_inc(tick, 1)
            list_masks(0)
            p0 = PAY[0][:, :].rearrange("p (j w) -> p j w", w=4)
            for t in (lidx, lidx2):
                st.do(V.memset(t, ZROW))
            st.do(V.memset(lnext, float(ZROW)))
            st.wait()
            st.do(V.tensor_copy(lidx2[:, 0:CW], p0[:, :, 0]))
            st.do(V.tensor_copy(lidx[:, 0:CW], p0[:, :, 3]))
            dve.wait_ge(s_fullw, 16)
            st.do(V.memset(zr[:, :, :], 0.0))
            st.do(V.memset(RB[:, 0:CW * TW], 0.0))
            st.wait()
            list_gather(0, cs, 1, lidx2, row_take(0, cs, TW, RB[:, 0:CW * TW], TW, YW, True), 9)
            dve.sem_inc(s_actgo, 1)
            ncarry[0] += 1
            list_carry(0, cs, RB[:, 0:CW * TW], TW, ncarry[0])
            st.seq(V.tensor_scalar(t1w, lnext[:, 0:CW], float(ZROW), None, ALU.is_lt))
            positions(cs, t1w, CW, lmask, lfirst, tm[:, 0:1])
            st.do(V.tensor_copy(Z0[:, :, D], lcnt[:, 0:CW]))
            st.do(V.tensor_copy(p0[:, :, 0], lnext[:, 0:CW]))
            st.wait()
            dve.sem_inc(s_ltab[0], 1)
            dve.sem_inc(s_pay[1], 1)

            def fill0(i, h):
                V.tensor_scalar(cring[:, h, 0:CU * D].rearrange("p (j w) -> p j w", w=D), chunk4(YW, i, h, D), 0.0,
                                None, ALU.add)

            trips0 = cs.trips
            dve.wait_ge(s_w, 16 * (4 * 4 + 5))
            dve.wait_ge(s_bd, 16 * 4)
            st.seq(V.tensor_reduce(bm[:, :], b_bias[:, :], AX.X, ALU.add))
            st.seq(V.tensor_scalar(bm[:, :], bm[:, :], -1.0 / D, None, ALU.mult))
            st.seq(V.tensor_scalar(bc[:, :], b_bias[:, :], bm[:, 0:1], None, ALU.add))
            for k in range(2):
                st.seq(V.tensor_tensor(prod[:, 0:NH * D].rearrange("p (h o) -> p h o", h=NH),
                                       wcat[:, :].rearrange("p (h o) -> p h o", h=NH),
                                       mid(wsd[:, k * D:(k + 1) * D], NH), ALU.mult))
                st.seq(V.tensor_reduce(ua[:, k, :], prod[:, 0:NH * D].rearrange("p (h o) -> p h o", h=NH), AX.X,
                                       ALU.add))
            for k in range(2):
                for h in range(NH):
                    m = (k * NH + h) * D
                    st.do(V.tensor_scalar(udiag[:, m:m + D], ident[0:D, 0:D], ua[0:D, k, h:h + 1], None, ALU.mult))
            for j in range(GT):
                r = slice(32 * j, 32 * j + 32)
                st.do(V.tensor_scalar(bd1[r, j * NH * D:(j + 1) * NH * D], wcat[r, :], 1.0 / NH, None, ALU.mult))
                for at_, w in ((0, wf[r, :]), (NB * D, aw[r, 0:D]), ((NB + 1) * D, aw[r, 2 * D:3 * D])):
                    part = w16[r, at_:at_ + w.shape[1]]
                    st.seq(V.tensor_copy(part, w))
                    if j >= 2:
                        st.seq(V.tensor_tensor(part, w, part, ALU.subtract))
                st.do(V.tensor_copy(bdy[r, j * D:(j + 1) * D], aw[r, D:2 * D]))
            st.wait()
            dve.sem_inc(s_wb, 1)

            ones_t = ones[:, 0:1].to_broadcast([P, T]).unsqueeze(2)
            segment_sums(ones_t, c3[:, :].unsqueeze(2), 1, dmask, dfirst)
            spread_back(c3[:, :].unsqueeze(2), 1, dend, dstf)
            dve.sem_inc(s_sri, 1)
            dve.wait_ge(s_payw[0], 16)
            st.seq(V.memset(PAY[1][:, :], -1.0))
            cs = make_list(1, t1w, CW, pb[:, 0:1], float(CW - ZROW))
            for h in range(2):
                dve.wait_ge(s_lland[0][h], trips0 * (16 * CU * 3))
            dve.sem_inc(tick, 1)
            list_gather(1, cs, 0, lq, pay_take(1, cs), 1)
            list_masks(1)
            p1 = PAY[1][:, :].rearrange("p (j w) -> p j w", w=4)
            for t in (lidx, lidx2):
                st.do(V.memset(t, ZROW))
            st.do(V.memset(lnext, float(ZROW)))
            st.wait()
            st.do(V.tensor_copy(lidx2[:, 0:CW], p1[:, :, 0]))
            st.do(V.tensor_copy(lidx[:, 0:CW], p1[:, :, 3]))
            st.do(V.memset(zr[:, :, :], 0.0))
            st.do(V.memset(S, 0.0))
            st.wait()
            list_gather(1, cs, 1, lidx2, row_take(1, cs, TW, SW, D, YW, True), 9)
            ncarry[0] += 1
            list_carry(1, cs, SW, D, ncarry[0])
            st.seq(V.tensor_copy(lidx2, lnext))
            dve.sem_inc(s_ltab[1], 1)

            def first_parts(i):
                dve.sem_inc(tick, 1)
                e = prods[:, :, :].rearrange("p a b -> p (a b)")[:, 0:RC * D]
                st.seq(V.tensor_tensor(e.rearrange("p (t d) -> p t d", d=D), chunk(XS, i), cols2(c2, i).unsqueeze(2)
                                       .to_broadcast([P, RC, D]), ALU.mult))
                rb = RB[:, bass.ds(i * (RC * D), RC * D)]
                st.seq(V.tensor_tensor(rb, rb, e, ALU.add))
                dve.sem_inc(tick, 1)

            dve.wait_ge(s_expl, 16)
            first_parts(ROUNDS - 1)
            with both_loops(st, cs, K_STEPS - 4, 4, 18) as k:
                st.seq(V.memset(zr[:, :, :], 0.0))
                list_gather(1, cs, k + 2, lidx2, row_take(1, cs, D, SW, D, YW, False), 8)
                list_carry(1, cs, SW, D, k + (ncarry[0] + 1))
                dve.sem_inc(s_ltab[1], 1)
                first_parts(k)
            ncarry[0] += K_STEPS - 4
            list_gather(1, cs, K_STEPS - 2, lidx2, row_take(1, cs, D, None, D, YW, False, float(K_STEPS)), 2)
            list_scatter(1, cs, K_STEPS - 1, K_STEPS - 1, fill0)
            dve.sem_inc(s_exp, 1)
            dve.wait_ge(s_expl, 32)
            st.seq(V.tensor_tensor(Y, Y, RB[:, 0:T * D], ALU.add))
            segment_sums(Y3, S3, D, dmask, dfirst)
            dve.sem_inc(s_tab, 1)

            def node_chunk(c):
                x3, q3, m = nx3[0:NODE_P], nsq3[0:NODE_P], [nr1[0:NODE_P, :]]
                wide = lambda t: t.unsqueeze(2).to_broadcast([NODE_P, CR, D])
                dve.wait_ge(s_nin, c * 16 + 16)
                dve.sem_inc(tick, 1)
                st.seq(V.tensor_reduce(m[0], x3, AX.X, ALU.add))
                st.seq(V.tensor_scalar(m[0], m[0], 1.0 / D, None, ALU.mult))
                st.seq(V.tensor_tensor(x3, x3, wide(m[0]), ALU.subtract))
                st.seq(V.tensor_tensor(q3, x3, x3, ALU.mult))
                st.seq(V.tensor_reduce(m[0], q3, AX.X, ALU.add))
                root()
                st.seq(V.reciprocal(m[0], m[0]))
                st.seq(V.tensor_tensor(x3, x3, wide(m[0]), ALU.mult))
                st.seq(V.tensor_tensor(x3, x3, mid(bc[0:NODE_P, :], CR), ALU.add))
                st.seq(V.tensor_tensor(q3, x3, x3, ALU.mult))
                st.seq(V.tensor_reduce(m[0], q3, AX.X, ALU.add))
                root()
                st.seq(V.reciprocal(m[0], m[0]))
                st.do(V.tensor_tensor(x3, x3, wide(m[0]), ALU.mult))
                st.wait()
                dve.sem_inc(s_nok, 1)

            def last_take(i, h):
                xs = cols(XS, i, h, D)
                y = prod[:, 0:U * D]
                st.seq(V.tensor_tensor(y.rearrange("p (t d) -> p t d", d=D), slot(h).rearrange(
                    "p (t d) -> p t d", d=D), cols(c1, i, h).unsqueeze(2).to_broadcast([P, U, D]), ALU.mult))
                st.seq(V.scalar_tensor_tensor(out=xs, in0=xs, scalar=1 + ALPHA, in1=y, op0=ALU.mult, op1=ALU.add))
                dve.sem_inc(tick, 1)

            def x1_chunk(i):
                st.seq(V.scalar_tensor_tensor(out=chunk(XD, i), in0=chunk(XD, i), scalar=1 + ALPHA, in1=chunk(S, i),
                                              op0=ALU.mult, op1=ALU.add))
                norm_chunk((XS, XD), i)
                logits_chunk(XS, 0, i)

            def spread_sums():
                dve.wait_ge(s_mm, 1)
                st.seq(V.tensor_copy(u_all[:, :], bank[6][:, 0:2 * NH * D]))
                st.seq(V.reciprocal(t2[:, :], t3[:, :]))
                st.seq(V.tensor_tensor(c1[:, :], c1[:, :], t2[:, :], ALU.mult))
                dve.wait_ge(s_sro, 2)
                st.seq(V.reciprocal(c3[:, :], c3[:, :]))
                st.seq(V.tensor_scalar(c3[:, :], c3[:, :], 1.0 - ALPHA, None, ALU.mult))
                dve.wait_ge(s_tabw, 16)
                spread_back(S3, D, dend, dstf)
                st.seq(V.tensor_tensor(S3, S3, bc3(c3[:, :], D), ALU.mult))

            def row_logits(i):
                logits_chunk(XD, 1, i)
                z, e = chunk(z4t, i, NH), chunk(e4t, i, NH)
                st.seq(V.scalar_tensor_tensor(out=z, in0=z, scalar=b_fcb[:, 0:1], in1=e, op0=ALU.add, op1=ALU.add))
                st.seq(V.scalar_tensor_tensor(out=z, in0=z, scalar=0.2, in1=z, op0=ALU.mult, op1=ALU.max))

            def row_fill(i, h):
                r = ring[:, h, 0:U * ROW1].rearrange("p (t d) -> p t d", d=ROW1)
                V.tensor_scalar(r[:, :, 0:D], cols(XD, i, h, D).rearrange("p (t d) -> p t d", d=D), 0.0, None, ALU.add)
                V.tensor_scalar(r[:, :, D:D + NH], cols(z4t, i, h, NH).rearrange("p (t d) -> p t d", d=NH), 0.0, None,
                                ALU.add)
                V.tensor_scalar(r[:, :, D + NH:D + NH + 1], cols(srcf, i, h).unsqueeze(2), 0.0, None, ALU.add)
                V.tensor_scalar(r[:, :, D + NH + 1:ROW1], cols(srcf, i, h).unsqueeze(2).to_broadcast([P, U, 3]), 0.0,
                                None, ALU.mult)
                return V.tensor_scalar(ridx[:, h, :], cols(posi, i, h), 0.0, None, ALU.add)

            def first_rows():
                row_logits(0)
                for h in range(2):
                    row_fill(0, h).then_inc(s_slot, 1)

            stepped_ring_pass(PASS_L0, fill_idx(gin), last_take, 2, x1_chunk, 1 + 13 + 2, x1_chunk, spread_sums,
                              landed=first_rows)

            stepped_ring_pass(PASS_ROW, row_fill, lambda i, h: None, 0, node_chunk, NODE_STEPS + 4, node_chunk,
                              before_fill=row_logits, filled=True, landed=lambda: dve.sem_inc(s_sct, 1))
            dve.wait_ge(s_row, 16)

            ksrc = ROWS3[:, :, D + NH]
            st.seq(V.tensor_scalar(ks[:, :], ksrc, 0.0, None, ALU.add))
            segments(ks, smask, sfirst, scar, sbak, neg=sneg, n=5)
            segment_ends(smask, scar, send)
            st.seq(V.tensor_scalar(t1[:, :], smask[:, :], 1.0, BIG, ALU.subtract, ALU.mult))
            zlog = ROWS3[:, :, D:D + NH]
            for h in range(NH):
                st.do(V.tensor_tensor_scan(e43[:, :, h], t1[:, :], zlog[:, :, h], -BIG, ALU.add, ALU.max))
            st.wait()
            st.seq(V.tensor_scalar(tl[:, 0:NH], e43[:, T - 1, :], 0.0, None, ALU.add))
            dve.sem_inc(s_trw, 1)
            dve.wait_ge(s_tr, 7)
            st.seq(V.tensor_tensor(prod[:, :].rearrange("p (h m) -> p h m", h=NH),
                                   bank[4][:, :].rearrange("p (h m) -> p h m", h=NH), mid(sneg[:, :], NH), ALU.add))
            st.seq(V.tensor_reduce(car[:, 0:NH], prod[:, :].rearrange("p (h m) -> p h m", h=NH), AX.X, ALU.max))
            st.seq(V.tensor_scalar(t1[:, :], sfirst[:, :], 1.0, BIG, ALU.subtract, ALU.mult))
            for h in range(NH):
                st.do(V.scalar_tensor_tensor(out=e43[:, :, h], in0=t1[:, :], scalar=car[:, h:h + 1], in1=e43[:, :, h],
                                             op0=ALU.add, op1=ALU.max))
            st.wait()
            spread_back(e43, NH, send, ks)
            st.seq(V.tensor_tensor(z43, zlog, e43, ALU.subtract))
            dve.sem_inc(s_ei, 1)
            dve.wait_ge(s_eo, 1)
            segment_sums(z43, e43, NH, smask, sfirst)
            spread_back(e43, NH, send, ks)
            st.seq(V.reciprocal(e4t[:, :], e4t[:, :]))
            st.seq(V.tensor_tensor(z43, z43, e43, ALU.mult))
            dve.sem_inc(s_hpu, CREDIT)
            dve.sem_inc(s_grp, 1)

            weighted = (prods[:, 0, :], prods[:, 1, :], S[:, 0:GT * NH * D])

            def head_sum(g, j):
                dve.sem_inc(tick, 1)
                st.do(V.tensor_reduce(Y[:, bass.ds(g * (GT * D), GT * D)].rearrange("p (t o) -> p t o", o=D),
                                      weighted[j % 3].rearrange("p (t h o) -> p t o h", h=NH, o=D), AX.X, ALU.add))

            with st.loop(ROUNDS, 2 * RG) as i:
                for j in range(RG):
                    g = i * RG + j
                    dve.wait_ge(s_hp, done(g))
                    dve.sem_inc(tick, 1)
                    att = z4t[:, bass.ds(g * (GT * NH), GT * NH)]
                    st.do(V.tensor_tensor(weighted[j % 3].rearrange("p (th o) -> p th o", o=D),
                                          bank[6 + j % 2][:, :].rearrange("p (th o) -> p th o", o=D),
                                          att.unsqueeze(2).to_broadcast([P, GT * NH, D]), ALU.mult))
                    if j:
                        head_sum(g - 1, j - 1)
                    st.wait(1 if j else 0)
                    dve.sem_inc(s_hpu, 1)
                head_sum(i * RG + (RG - 1), RG - 1)
                st.wait()
            segment_sums(Y3, S3, D, smask, sfirst)
            dve.sem_inc(s_tab, 1)

            def add_take(dest):
                def take(i, h):
                    st.do(V.tensor_tensor(cols(dest, i, h, D), cols(dest, i, h, D), slot(h), ALU.add))
                    st.wait()
                    dve.sem_inc(tick, 1)
                return take

            def x2_chunk(t, first, nodes=True):
                def work(i):
                    st.seq(V.tensor_tensor(chunk(t, i), chunk(t, i), mid(b_bias[:, :], RC), ALU.add))
                    norm_chunk((t,), i, rr if t is XS else None)
                    if t is XS:
                        hi, lo = (chunk16(i)[:, :, k, :] for k in range(2))
                        st.seq(V.tensor_scalar(hi, chunk(t, i), 0.0, None, ALU.add))
                        st.seq(V.tensor_tensor(lo, chunk(t, i), hi, ALU.subtract))
                    if nodes:
                        node_chunk(i + first)
                return work

            chunk16 = lambda i: S.bitcast(F16)[:, bass.ds(i * (RC * 2 * D), RC * 2 * D)].rearrange(
                "p (t k d) -> p t k d", k=2, d=D)

            def wait_att():
                dve.wait_ge(s_tabw, 32)
                dve.wait_ge(s_ptake, 2 * ROUNDS)

            stepped_ring_pass(PASS_ATT_SRC, fill_idx(gout_s), add_take(XS), 1, x2_chunk(XS, ROUNDS), 17 + NODE_STEPS,
                              x2_chunk(XS, ROUNDS), wait_att, next_fill=fill_idx(gout_d))
            stepped_ring_pass(PASS_ATT_DST, fill_idx(gout_d), add_take(XD), 1, x2_chunk(XD, 2 * ROUNDS),
                              9 + NODE_STEPS, x2_chunk(XD, 0, nodes=False), next_fill=fill_idx(etyi), filled=True)
            assert CH == 3 * ROUNDS - 1
            def relation_groups(i):
                rel = chunk(RB, i, RW)[:, :, NB:RW]
                st.seq(V.tensor_tensor(rel, rel, mid(b_b2[:, :], RC), ALU.add))
                pr3 = pr2[:, :].rearrange("p (t o) -> p t o", t=GT)
                pq3 = pq2[:, :].rearrange("p (t o) -> p t o", t=GT)
                for j in range(RG):
                    g, b = i * RG + j, j % 2
                    xh = bank[6 + b][:, 0:256].rearrange("p (t o) -> p t o", t=GT)
                    yh = bank[6 + b][:, 256:256 + P].rearrange("p (t o) -> p t o", t=GT)
                    relg = RB[:, bass.ds(g * (GT * RW), GT * RW)].rearrange("p (t o) -> p t o", t=GT)

                    def basis_mult(c):
                        dve.wait_ge(s_msg, g * GT + (c + 1 + MSG0))
                        dve.sem_inc(tick, 1)
                        st.do(V.tensor_tensor(prods[:, c % 2, :].rearrange("p (b o) -> p b o", b=NB),
                                              bank[c][:, :].rearrange("p (b o) -> p b o", b=NB),
                                              relg[:, c, 0:NB].unsqueeze(2).to_broadcast([P, NB, D]), ALU.mult))

                    def basis_sum(c):
                        dve.sem_inc(tick, 1)
                        st.do(V.tensor_reduce(Y[:, bass.ds(g * (GT * D) + c * D, D)],
                                              prods[:, c % 2, :].rearrange("p (b o) -> p o b", b=NB), AX.X, ALU.add))

                    dve.wait_ge(s_xy, g + 1)
                    dve.sem_inc(tick, 1)
                    st.do(V.tensor_tensor(pr3, xh[:, :, 0:D], mid(b_b1[:, :], GT), ALU.add))
                    st.do(V.tensor_tensor(pq3, yh, relg[:, :, NB:RW], ALU.add))
                    st.wait(2)
                    basis_mult(0)
                    st.wait(1)
                    dve.sem_inc(s_xyu, 1)
                    st.do(V.tensor_tensor(pr3, pr3, pq3, ALU.mult))
                    basis_mult(1)
                    st.wait(2)
                    dve.sem_inc(s_msgu, 1)
                    basis_sum(0)
                    st.wait(2)
                    dve.sem_inc(tick, 1)
                    st.do(V.tensor_reduce(sc4[:, :], pr3, AX.X, ALU.add))
                    st.wait(1)
                    dve.sem_inc(s_msgu, 1)
                    basis_mult(2)
                    basis_sum(1)
                    st.wait(2)
                    st.do(V.tensor_scalar(t1[:, bass.ds(g * GT, GT)], sc4[:, :], 1.0 / D ** 0.5, 0.0, ALU.mult, ALU.max))
                    st.wait(1)
                    dve.sem_inc(s_msgu, 1)
                    basis_mult(3)
                    basis_sum(2)
                    st.wait(1)
                    dve.sem_inc(s_msgu, 1)
                    basis_sum(3)

            dve.sem_inc(s_xyu, CREDIT)
            dve.sem_inc(s_msgu, GT)
            dve.sem_inc(s_grp, 1)
            stepped_ring_pass(PASS_REL, fill_idx(etyi), copy_take(RB, RW), 1, relation_groups, 1 + 13 * RG,
                              relation_groups, filled=True)
            dve.wait_ge(s_self, NG + 2)
            st.do(V.memset(tl[:, 0:1], 0.0))
            st.wait()
            dve.sem_inc(s_ei, 1)
            dve.wait_ge(s_eo, 2)
            st.seq(V.tensor_tensor(Y3, Y3, bc3(t1[:, :], D), ALU.mult))
            segment_sums(Y3, Y3, D, dmask, dfirst)
            st.seq(V.tensor_tensor(S[:, :], S[:, :], Y[:, :], ALU.add))
            st.seq(V.tensor_scalar(S[:, :], S[:, :], 0.0, None, ALU.max))
            dve.sem_inc(s_tab, 1)
            def x3_chunk(i, last=False):
                st.seq(V.tensor_tensor(chunk(XD, i), chunk(XD, i), chunk(S, i), ALU.add))
                norm_chunk((XS,) if last else (XS, XD), i)
                st.seq(V.tensor_tensor(chunk(Y, i), chunk(XS, i), cols2(ew, i).unsqueeze(2).to_broadcast([P, RC, D]),
                                       ALU.mult))

                y, sm = chunk(Y, i), chunk(S, i)
                mask = cols2(dmask, i)
                st.seq(V.scalar_tensor_tensor(out=y[:, 0, :], in0=tl[:, :], scalar=mask[:, 0:1], in1=y[:, 0, :],
                                              op0=ALU.mult, op1=ALU.add))
                for d in range(D):
                    st.do(V.tensor_tensor_scan(sm[:, :, d], mask, y[:, :, d], 0.0, ALU.mult, ALU.add))
                st.wait()
                dve.sem_inc(tick, 1)
                st.seq(V.tensor_scalar(tl[:, :], sm[:, RC - 1, :], 0.0, None, ALU.add))

            def table_read():
                dve.wait_ge(s_oslot, 2 * ROUNDS)
                dve.wait_ge(s_tabw, 48)
                st.seq(V.memset(tl[:, :], 0.0))

            stepped_ring_pass(PASS_RGCN, fill_idx(gin), add_take(XS), 1, x3_chunk, 2 + 13 + 2 + D,
                              lambda i: x3_chunk(i, last=True), table_read)
            carries()
            st.seq(V.tensor_copy(car[:, :], bank[7][:, 0:D]))

            def out_fill(rows, idx):
                def fill(i, h):
                    V.tensor_scalar(slot(h), cols(rows, i, h, D), 0.0, None, ALU.add)
                    return V.tensor_scalar(ridx[:, h, :], cols(idx, i, h), 0.0, None, ALU.add)
                return fill

            def out_dst(i):
                part = prods[:, :, :].rearrange("p a b -> p (a b)")[:, 0:RC * D].rearrange("p (t d) -> p t d", d=D)
                st.seq(V.tensor_tensor(part, cols2(dfirst, i).unsqueeze(2).to_broadcast([P, RC, D]),
                                       mid(car[:, :], RC), ALU.mult))
                st.seq(V.tensor_tensor(chunk(S, i), chunk(S, i), part, ALU.add))
                st.seq(V.scalar_tensor_tensor(out=chunk(XD, i), in0=chunk(XD, i), scalar=2.0, in1=chunk(S, i),
                                              op0=ALU.mult, op1=ALU.add))
                norm_chunk((XD,), i)

            stepped_ring_pass(PASS_OUT_DST, out_fill(XD, odi), lambda i, h: None, 0, extra=11, before_fill=out_dst,
                              between=lambda: norm_chunk((XD,), ROUNDS - 1))

        @block.scalar
        def _(act):
            A = nc.scalar
            tick = s_tick[1]

            def act_pass(n, idx, dest, w):
                ring_pass(act, tick, n,
                          lambda i, h: A.activation(ridx[:, h, :], cols(idx, i, h), ACT.Copy),
                          lambda i, h: A.activation(cols(dest, i, h, w), ring[:, h, 0:U * w], ACT.Copy))

            act.wait_ge(s_ids, 1)
            act_pass(PASS_X_SRC, xsi, XS, D)
            def copy_transposed(i, b):
                act.wait_ge(s_ohT, i + 1)
                act.sem_inc(tick, 1)
                for k in range(2):
                    last = A.activation(ohaT[b][:, 2 * k:2 * k + 2, :].rearrange("p j n -> p (j n)"),
                                        bank[2 + k][:, :].bitcast(F16), ACT.Copy)
                last.then_inc(s_ohTc, 1)

            copy_transposed(0, 0)
            with act.Fori(0, NG // 2) as k:
                for b in range(2):
                    i = k * 2 + b
                    act.wait_ge(s_ru, i + 1)
                    act.sem_inc(tick, 1)
                    for m in range(2):
                        last = A.activation(rhi[1 - b][:, 2 * m:2 * m + 2, :].rearrange("p c n -> p (c n)"),
                                            bank[m][:, :], ACT.Copy)
                    last.then_inc(s_rhi, 1)
                    copy_transposed(i + 1, 1 - b)
            act.wait_ge(s_sri, 1)
            A.activation(t1[:, :], t1[:, :], ACT.Sqrt)
            A.activation(t2[:, :], t2[:, :], ACT.Sqrt).then_inc(s_sro, 1)

            def list_cols(t, i, h, w):
                return t[:, bass.ds(i * (2 * CU * w) + h * (CU * w), CU * w)]

            act.wait_ge(s_actgo, 1)
            n0 = act.value_load(trips_i[0][0:1, 0:1], min_val=1, max_val=CW // (2 * CU))
            for h in range(2):
                A.activation(cidx[:, h, :], lq[:, h * CU:(h + 1) * CU], ACT.Copy).then_inc(s_lslot[0], 1)
            with act.Fori(0, n0) as i:
                for h in range(2):
                    act.wait_ge(s_lland[0][h], i * (16 * CU) + 16 * CU)
                    act.sem_inc(tick, 1)
                    A.activation(list_cols(PAY[0], i, h, 4), cring[:, h, 0:CU * 4], ACT.Copy).then_inc(s_pay0, 1)
                    A.activation(cidx[:, h, :], list_cols(lq, i + 1, h, 1), ACT.Copy).then_inc(s_lslot[0], 1)
            act.wait_ge(s_actgo, 2)
            with act.Fori(0, n0) as i:
                for h in range(2):
                    A.activation(cring[:, h, 0:CU * D], list_cols(YW, i, h, D), ACT.Copy)
                    A.activation(cidx[:, h, :], list_cols(lidx, i, h, 1), ACT.Copy).then_inc(s_lslot[0], 1)
                for h in range(2):
                    act.wait_ge(s_lland[0][h], n0 * (16 * CU * 2) + i * (16 * CU) + 16 * CU)
                act.sem_inc(tick, 1)

            act.wait_ge(s_sri, 2)
            A.activation(c3[:, :], c3[:, :], ACT.Sqrt).then_inc(s_sro, 1)

            n_roots = 0

            def take_roots(kinds, count):
                nonlocal n_roots
                with act.Fori(0, count) as k:
                    for m, kind in enumerate(kinds):
                        act.wait_ge(s_ri, k * len(kinds) + (n_roots + m + 1))
                        act.sem_inc(tick, 1)
                        A.activation(roots[:, :], roots[:, :], ACT.Sqrt, scale=ROOTS[kind][0] / D,
                                     bias=eps_t[kind][:, 0:1]).then_inc(s_dve, 1)
                n_roots += count * len(kinds)

            node_kinds = ("first", "all")
            take_roots(("norm",), ROUNDS)
            take_roots(node_kinds, ROUNDS)

            edges_g = lambda t3_, g: t3_[:, bass.ds(g * GT, GT), 0:D]

            def stage(k, t3_, g, j):
                act.wait_ge(s_xtp[k], free(g, j))
                act.sem_inc(tick, 1)
                if k == 1:
                    A.activation(xs16[:, j % 2, :].rearrange("p (t r m) -> p t r m", r=2, m=2 * D),
                                 S.bitcast(F16)[:, bass.ds(g * (GT * 2 * D), GT * 2 * D)].rearrange(
                                     "p (t m) -> p t m", m=2 * D).unsqueeze(2).to_broadcast([P, GT, 2, 2 * D]), ACT.Copy)
                A.activation(xg[:, j % 2, :].rearrange("p (t d) -> p t d", d=D), edges_g(t3_, g),
                             ACT.Copy).then_inc(s_stg[k], 1)

            act.wait_ge(s_ei, 1)
            A.activation(z4t[:, :], z4t[:, :], ACT.Exp).then_inc(s_eo, 1)
            act.wait_ge(s_grp, 1)

            act.sem_inc(s_xtc[0], CREDIT)
            stage(0, ROWS3, 0, 0)

            def attention_group(g, j, last):
                if not last:
                    stage(0, ROWS3, g + 1, (j + 1) % RG)
                act.wait_ge(s_xtp[0], done(g))
                act.wait_ge(s_hp, free(g, j))
                act.sem_inc(tick, 1)
                A.activation(xt[:, j % 2, :], bank[j % 2][:, 0:P], ACT.Copy).then_inc(s_xtc[0], 1)

            groups(act, attention_group)
            take_roots(("norm", "all") + node_kinds, ROUNDS)
            take_roots(("norm",) + node_kinds, ROUNDS - 1)
            take_roots(("norm",), 1)
            act.wait_ge(s_grp, 2)
            act.sem_inc(s_xtc[1], CREDIT)
            act.sem_inc(s_self, CREDIT)
            stage(1, XD3, 0, 0)

            def relation_group(g, j, last):
                b = j % 2
                if not last:
                    stage(1, XD3, g + 1, (j + 1) % RG)
                act.wait_ge(s_xtp[1], done(g))
                act.wait_ge(s_msg, free(g, j) * GT)
                act.sem_inc(tick, 1)
                A.activation(x16[:, b, :], bank[4 + b][:, 0:256].bitcast(F16), ACT.Copy)
                A.activation(xt[:, b, :], bank[4 + b][:, 256:256 + P], ACT.Copy).then_inc(s_xtc[1], 1)
                act.wait_ge(s_xyu, done(g))
                act.sem_inc(tick, 1)
                A.activation(S[:, bass.ds(g * (GT * D), GT * D)].rearrange("p (t o) -> p t o", t=GT),
                             bank[6 + b][:, 0:256].rearrange("p (t o) -> p t o", t=GT)[:, :, D:2 * D],
                             ACT.Copy).then_inc(s_self, 1)

            def out_src_fill(slot_, b):
                for t in range(U):
                    A.activation(oring[b][:, t * D:(t + 1) * D], XS[:, bass.ds(slot_ * (U * D) + t * D, D)], ACT.Copy,
                                 scale=rr[:, bass.ds(slot_ * U + t, 1)])
                A.activation(oidx[:, b, :], osi[:, bass.ds(slot_ * U, U)], ACT.Copy).then_inc(s_oslot, 1)

            def out_src_round(i):
                act.wait_ge(s_oland[0], i * (16 * U) + 16 * U)
                act.sem_inc(tick, 1)
                out_src_fill(i + 1, 0)

            out_src_fill(0, 0)
            groups(act, relation_group, out_src_round)
            out_src_fill(ROUNDS, 1)
            act.wait_ge(s_ei, 2)
            A.activation(t1[:, :], t1[:, :], ACT.Tanh).then_inc(s_eo, 1)
            with act.Fori(0, (ROUNDS - 1) // 2) as k:
                for b in range(2):
                    act.wait_ge(s_oland[b], k * (16 * U) + (1 if b else ROUNDS) * 16 * U)
                    act.sem_inc(tick, 1)
                    out_src_fill(k * 2 + (ROUNDS + 1 + b), b)
            take_roots(("norm",), 2 * ROUNDS + 1)

        @block.tensor
        def _(pe):
            M = nc.tensor
            tick = s_tick[3]
            pe.wait_ge(s_cst2, 1)
            for c in range(NA_CH):
                last = M.matmul(bank[c][:, :], ident_h[:, :], zh[:, :], start=True, stop=False)
            last.then_inc(s_ohu, 4)
            with pe.Fori(0, NG) as i:
                for j in range(4):
                    pe.wait_ge(s_oh, i * 4 + j + 1)
                    pe.sem_inc(tick, 1)
                    for c in range(NA_CH):
                        M.matmul(bank[c][:, 0:NB_COL], oha[:, j, c * P:(c + 1) * P], ohb[:, j, :], start=False, stop=False)
                        last = M.matmul(bank[c][:, NB_COL:2 * NB_COL], oha2[:, j, c * P:(c + 1) * P], ohb2[:, j, :],
                                        start=False, stop=False)
                    last.then_inc(s_ohu, 1)
            for c in range(NA_CH):
                last = M.matmul(bank[c][:, :], ident_h[:, :], zh[:, :], start=False, stop=True)
            last.then_inc(s_hist, 1)
            pe.wait_ge(s_tot, 1)
            tk = tot[:, :, :].rearrange("p k c -> p (k c)")
            M.matmul(bank[4][:, 0:2 * NA_CH], up[:, :], tk, start=True, stop=True)
            M.matmul(bank[5][:, 0:2 * NA_CH], ones[:, :], tk, start=True, stop=True).then_inc(s_base, 1)

            pe.wait_ge(s_nt, 1)
            for b in range(2):
                last = M.matmul(bank[b][:, :], ident_h[:, :], zh[:, :], start=True, stop=True, skip_group_check=True)
            chunk = lambda c: bank[c // 2][:, (c % 2) * NB_COL:(c % 2 + 1) * NB_COL]

            def rank_transposes(i, b):
                pe.wait_ge(s_oh, i + (T + 1))
                pe.wait_ge(s_eq, i + (1 if isinstance(i, int) else 0))
                pe.sem_inc(tick, 1)
                for j in range(4):
                    for c in range(NA_CH):
                        n = (j % 2) * AW + c * P
                        last = M.transpose(bank[2 + j // 2][:, :].bitcast(F16)[:, n:n + P],
                                           ohas[b][:, j, c * P:(c + 1) * P], ident_h[:, :])
                last.then_inc(s_ohT, 1)
                for j in range(4):
                    last = M.transpose(bank[4 + 3 * b][:, j * P:(j + 1) * P],
                                       kcol[:, b, j:j + 1].to_broadcast([P, P]), ident[:, :])
                last.then_inc(s_kt, 1)

            def rank_counts(i, b):
                pe.wait_ge(s_rc, i + 1)
                pe.sem_inc(tick, 1)
                for j in range(4):
                    for c in range(NA_CH):
                        last = M.matmul(chunk(c), ohas[b][:, j, c * P:(c + 1) * P], ohbs[b][:, j, :], start=False,
                                        stop=j == 3, skip_group_check=True)
                last.then_inc(s_ru, 1)
                pe.wait_ge(s_ohTc, i + 1)
                pe.wait_ge(s_gu, i + 1)
                pe.sem_inc(tick, 1)
                for j in range(4):
                    g = bank[5 + j // 2][:, (j % 2) * NB_COL:(j % 2 + 1) * NB_COL]
                    for c in range(NA_CH):
                        for m, part in enumerate((rhi, rlo)):
                            last = M.matmul(g, ohaT[b][:, j, c * P:(c + 1) * P], part[b][:, c, :],
                                            start=c == 0 and m == 0, stop=c == NA_CH - 1 and m == 1)
                last.then_inc(s_g, 1)

            rank_transposes(0, 0)
            with pe.Fori(0, NG // 2) as k:
                for b in range(2):
                    rank_counts(k * 2 + b, b)
                    rank_transposes(k * 2 + (b + 1), 1 - b)
            rank_counts(NG - 1, 0)

            def key_rows(n):
                pe.wait_ge(s_trw, n)
                M.transpose(bank[4][:, 0:P], tl[:, 0:1].to_broadcast([P, P]), ident[:, :])
                M.transpose(bank[5][:, 0:P], tl[:, 1:2].to_broadcast([P, P]), ident[:, :]).then_inc(s_tr, 1)

            n_carry = 0

            def carry(link, width):
                nonlocal n_carry
                n_carry += 1
                pe.wait_ge(s_tail, n_carry)
                M.matmul(bank[7][:, 0:width], link[:, :], tl[:, 0:width], start=True, stop=True).then_inc(s_carry, 1)

            def column_row(n):
                pe.wait_ge(s_trw, n)
                M.transpose(bank[4][:, 0:P], tl[:, 0:1].to_broadcast([P, P]), ident[:, :]).then_inc(s_tr, 1)

            column_row(1)
            key_rows(2)
            carry(dcar, D)
            column_row(3)
            carry(dcar, D)
            column_row(4)
            carry(dcar, 1)
            carry(dbak, 1)
            column_row(5)
            carry(dcar, D)
            with pe.Fori(0, K_STEPS - 4) as k:
                pe.wait_ge(s_tail, k + (n_carry + 1))
                pe.sem_inc(tick, 1)
                M.matmul(bank[7][:, 0:D], dcar[:, :], tl[:, :], start=True, stop=True).then_inc(s_carry, 1)
            n_carry += K_STEPS - 4
            carry(dcar, D)
            pe.wait_ge(s_wb, 1)
            M.matmul(bank[6][:, 0:2 * NH * D], ones[0:D, :], udiag[:, :], start=True, stop=True).then_inc(s_mm, 1)
            carry(dbak, D)


            key_rows(6)
            pe.wait_ge(s_trw, 7)
            for h in range(NH):
                last = M.transpose(bank[4][:, h * P:(h + 1) * P], tl[:, h:h + 1].to_broadcast([P, P]), ident[:, :])
            last.then_inc(s_tr, 1)
            carry(sbak, NH)
            carry(scar, NH)
            carry(sbak, NH)
            pe.wait_ge(s_grp, 1)
            pe.sem_inc(s_xtp[0], CREDIT)
            pe.sem_inc(s_hp, CREDIT)

            def attention_transpose(g, j):
                pe.wait_ge(s_stg[0], g + 1)
                pe.wait_ge(s_xtc[0], free(g, j))
                pe.sem_inc(tick, 1)
                M.transpose(bank[j % 2][:, 0:P], xg[:, j % 2, :], ident[:, :]).then_inc(s_xtp[0], 1)

            def attention_group(g, j, last):
                if not last:
                    attention_transpose(g + 1, (j + 1) % RG)
                pe.wait_ge(s_xtc[0], done(g))
                pe.wait_ge(s_hpu, free(g, j))
                pe.sem_inc(tick, 1)
                M.matmul(bank[6 + j % 2][:, :], xt[:, j % 2, :], bd1[:, :], start=True, stop=True).then_inc(s_hp, 1)

            attention_transpose(0, 0)
            groups(pe, attention_group)
            carry(scar, D)

            pe.wait_ge(s_grp, 2)
            pe.sem_inc(s_xtp[1], CREDIT)
            pe.sem_inc(s_msg, MSG0)

            def relation_transpose(g, j):
                b = j % 2
                pe.wait_ge(s_stg[1], g + 1)
                pe.wait_ge(s_xtc[1], free(g, j))
                pe.sem_inc(tick, 1)
                for c in range(GT):
                    M.transpose(bank[4 + b][:, 0:256].bitcast(F16)[:, c * P:(c + 1) * P],
                                xs16[:, b, c * P:(c + 1) * P], ident_h[:, :])
                M.transpose(bank[4 + b][:, 256:256 + P], xg[:, b, :], ident[:, :]).then_inc(s_xtp[1], 1)

            def relation_group(g, j, last):
                b = j % 2
                if not last:
                    relation_transpose(g + 1, (j + 1) % RG)
                pe.wait_ge(s_xtc[1], done(g))
                pe.wait_ge(s_self, free(g, j))
                pe.sem_inc(tick, 1)
                for c in range(GT):
                    M.matmul(bank[6 + b][:, c * 2 * D:(c + 1) * 2 * D], x16[:, b, c * P:(c + 1) * P],
                             w16[:, NB * D:(NB + 2) * D], start=True, stop=True)
                M.matmul(bank[6 + b][:, 256:256 + P], xt[:, b, :], bdy[:, :], start=True, stop=True).then_inc(s_xy, 1)
                for c in range(GT):
                    pe.wait_ge(s_msgu, g * GT + (c + 1))
                    pe.sem_inc(tick, 1)
                    M.matmul(bank[c][:, :], x16[:, b, c * P:(c + 1) * P], w16[:, 0:NB * D], start=True,
                             stop=True).then_inc(s_msg, 1)

            relation_transpose(0, 0)
            groups(pe, relation_group)
            carry(dcar, D)
            carry(dcar, D)


_INS = ['x', 'src', 'dst', 'edge_type_86', 'edge_weight', 'L1_gnn_w', 'L1_gnn_fc_w', 'L1_gnn_fc_b', 'L1_gnn_bias',
        'L2_gnn_weight', 'L2_gnn_w_comp', 'L2_gnn_self_loop_weight', 'L2_gnn_A1_w', 'L2_gnn_A1_b', 'L2_gnn_A2_w',
        'L2_gnn_A2_b', 'L2_gnn_rel_emb']
_OUTS = [((100000, 32), 'float32')]


def kernel(**inputs):
    import numpy as _np
    import concourse.bacc as _bacc
    from concourse import mybir as _mybir
    from concourse.bass_utils import run_bass_kernel_spmd as _run

    nc = _bacc.Bacc("TRN2", target_bir_lowering=False, num_devices=1)
    arrays, args = {}, []
    for name in _INS:
        a = _np.ascontiguousarray(inputs[name])
        arrays[f"in_{name}_dram"] = a
        args.append(nc.dram_tensor(f"in_{name}_dram", a.shape, _mybir.dt.from_np(a.dtype), kind="ExternalInput").ap())
    for i, (shape, dtype) in enumerate(_OUTS):
        dt = _mybir.dt.from_np(_np.dtype(dtype))
        args.append(nc.dram_tensor(f"out_{i}_dram", shape, dt, kind="ExternalOutput").ap())
    gnn_resnorm(nc, *args)
    r = _run(nc, [arrays], core_ids=[0])
    return r.results[0]["out_0_dram"]
```
